# Optimizing a Trainium2 kernel written in Bass

```python
import numpy as np
import jax
import jax.numpy as jnp

def _softmax(x, axis=-1):
    return jax.nn.softmax(x, axis=axis)

def _gelu(x):
    return jax.nn.gelu(x, approximate=True)

def _silu(x):
    return jax.nn.silu(x)

def _sigmoid(x):
    return jax.nn.sigmoid(x)

def _layernorm(x, axis=-1, eps=1e-05):
    m = jnp.mean(x, axis=axis, keepdims=True)
    v = jnp.var(x, axis=axis, keepdims=True)
    return (x - m) / jnp.sqrt(v + eps)

def _scatter_add(tgt, idx, src, axis=0):
    return tgt.at[idx].add(src)

def _segment_sum(src, seg, n):
    return jax.ops.segment_sum(src, seg, n)
kernel_name = 'mk_vit_tower_postln_d2_tok_img1024_r4_194d34'

def setup_inputs(seed: int=0):
    np.random.seed(seed)
    _w = jnp.asarray

    def _rec_inputs():
        import jax
        import jax.numpy as jnp
        _rk = jax.random.key(seed)
        x = -0.00150118 + 0.499729 * jax.random.normal(jax.random.fold_in(_rk, 1), (8, 256, 64, 2), jnp.float32)
        return x
    x = _rec_inputs()

    def _L0_tok_setup():
        import jax, jax.numpy as jnp
        import numpy as np
        import math
        H = 256
        N = 64
        CH = 1
        SEQ_L = 256
        key = jax.random.key(seed)
        k1, k2, k3, k4 = jax.random.split(key, 4)
        log_dt = jax.random.uniform(k1, (H,), dtype=jnp.float32, minval=math.log(0.001), maxval=math.log(0.1))
        inv_A_real = jnp.log(0.5 * jnp.ones((H, N), jnp.float32)) + 0.1 * jax.random.normal(k2, (H, N), dtype=jnp.float32)
        A_imag = jnp.broadcast_to(math.pi * jnp.arange(N, dtype=jnp.float32), (H, N)).copy()
        B_ri = jax.random.normal(k3, (H, N, 2), dtype=jnp.float32) * 0.5
        C_ri = jax.random.normal(k4, (CH, H, N, 2), dtype=jnp.float32) * 0.5
        return {'log_dt': log_dt, 'inv_A_real': inv_A_real, 'A_imag': A_imag, 'B_ri': B_ri, 'C_ri': C_ri, 'L': SEQ_L}
    _L0_tok_all = _L0_tok_setup()
    _L0_tok_in = {k: v for k, v in _L0_tok_all.items() if k in ('log_dt', 'inv_A_real', 'A_imag', 'B_ri')}
    del _L0_tok_all

    def _L0_attn_setup():
        import math
        import jax, jax.numpy as jnp
        import numpy as np
        B, T, D, H = (4, 256, 256, 8)
        HD = D // H

        def _trigram_dirs():
            t = np.array([[(i >> b & 1) * 2 - 1 for b in (2, 1, 0)] for i in range(8)], dtype=np.float32)
            return jnp.asarray(t / np.linalg.norm(t, axis=1, keepdims=True))
        key = jax.random.key(seed)
        k1, k2, k3, k4 = jax.random.split(key, 4)
        x = jax.random.normal(k1, (B, T, D), dtype=jnp.float32)
        Wqkv = jax.random.normal(k2, (D, 3 * D), dtype=jnp.float32) * 0.02
        Wout = jax.random.normal(k3, (D, D), dtype=jnp.float32) * 0.02
        head_scales = jax.random.normal(k4, (H,), dtype=jnp.float32) * 0.1
        head_dirs = _trigram_dirs()
        return {'x': x, 'Wqkv': Wqkv, 'Wout': Wout, 'head_scales': head_scales, 'head_dirs': head_dirs}
    _L0_attn_all = _L0_attn_setup()
    _L0_attn_in = {k: v for k, v in _L0_attn_all.items() if k in ('Wqkv', 'Wout', 'head_scales', 'head_dirs')}
    del _L0_attn_all

    def _L0_ffn_setup():
        import jax, jax.numpy as jnp
        import numpy as np
        H = 32
        MB = 2
        TOP_K = 2
        key = jax.random.key(seed)
        ks = jax.random.split(key, 8)
        B, S, D, E = (8, 256, 256, 8)
        Fd = 4 * D

        def w(k, shape, fan):
            return jax.random.normal(k, shape, jnp.float32) / np.float32(np.sqrt(fan))
        return dict(x=jax.random.normal(ks[0], (B, S, D), jnp.float32), ln_g=jnp.ones((D,), jnp.float32), ln_b=jnp.zeros((D,), jnp.float32), wq=w(ks[1], (D, D), D), wk=w(ks[2], (D, D), D), wv=w(ks[3], (D, D), D), wo=w(ks[4], (D, D), D), gate_w=w(ks[5], (E, D), D), w1=w(ks[6], (E, D, Fd), D), b1=jnp.zeros((E, Fd), jnp.float32), w2=w(ks[7], (E, Fd, D), Fd), b2=jnp.zeros((E, D), jnp.float32))
    _L0_ffn_all = _L0_ffn_setup()
    _L0_ffn_in = {k: v for k, v in _L0_ffn_all.items() if k in ('ln_g', 'ln_b', 'wq', 'wk', 'wv', 'wo', 'gate_w', 'w1', 'b1', 'w2', 'b2')}
    del _L0_ffn_all

    def _L1_attn_setup():
        import jax, jax.numpy as jnp
        import numpy as np
        B, T, H = (2, 256, 256)
        NH = 4
        DK, DV = (128, 256)
        dk, dv = (DK // NH, DV // NH)
        LR = 16
        GATE_NORM = 16.0
        EPS = 1e-05
        key = jax.random.key(seed)
        ks = jax.random.split(key, 9)
        s = 0.02
        return {'x': jax.random.normal(ks[0], (B, T, H), jnp.float32), 'Wq': jax.random.normal(ks[1], (H, DK), jnp.float32) * s, 'Wk': jax.random.normal(ks[2], (H, DK), jnp.float32) * s, 'Wv': jax.random.normal(ks[3], (H, DV), jnp.float32) * s, 'Wgk1': jax.random.normal(ks[4], (H, LR), jnp.float32) * s, 'Wgk2': jax.random.normal(ks[5], (LR, DK), jnp.float32) * s, 'bgk2': jnp.zeros((DK,), jnp.float32), 'Wg': jax.random.normal(ks[6], (H, DV), jnp.float32) * s, 'Wo': jax.random.normal(ks[7], (DV, H), jnp.float32) * s, 'gw': jnp.ones((dv,), jnp.float32)}
    _L1_attn_all = _L1_attn_setup()
    _L1_attn_in = {k: v for k, v in _L1_attn_all.items() if k in ('Wq', 'Wk', 'Wv', 'Wgk1', 'Wgk2', 'bgk2', 'Wg', 'Wo', 'gw')}
    del _L1_attn_all

    def _L1_ffn_setup():
        import jax, jax.numpy as jnp
        import numpy as np
        N_EMBD = 256
        N_EXPERTS = 8
        TOP_K = 2
        B, T = (4, 512)
        key = jax.random.key(seed)
        ks = jax.random.split(key, 8)
        C, E, H = (N_EMBD, N_EXPERTS, 4 * N_EMBD)
        s_in = 1.0 / np.sqrt(C)
        s_hid = 1.0 / np.sqrt(H)
        x = jax.random.normal(ks[0], (B, T, C), dtype=jnp.float32)
        W1 = jax.random.uniform(ks[1], (E, C, H), minval=-s_in, maxval=s_in, dtype=jnp.float32)
        b1 = jax.random.uniform(ks[2], (E, H), minval=-s_in, maxval=s_in, dtype=jnp.float32)
        W2 = jax.random.uniform(ks[3], (E, H, C), minval=-s_hid, maxval=s_hid, dtype=jnp.float32)
        b2 = jax.random.uniform(ks[4], (E, C), minval=-s_hid, maxval=s_hid, dtype=jnp.float32)
        Wg = jax.random.uniform(ks[5], (C, E), minval=-s_in, maxval=s_in, dtype=jnp.float32)
        bg = jax.random.uniform(ks[6], (E,), minval=-s_in, maxval=s_in, dtype=jnp.float32)
        return {'x': x, 'W1': W1, 'b1': b1, 'W2': W2, 'b2': b2, 'Wg': Wg, 'bg': bg}
    _L1_ffn_all = _L1_ffn_setup()
    _L1_ffn_in = {k: v for k, v in _L1_ffn_all.items() if k in ('W1', 'b1', 'W2', 'b2', 'Wg', 'bg')}
    del _L1_ffn_all
    return {'x': x, 'L0_tok_log_dt': _L0_tok_in['log_dt'], 'L0_tok_inv_A_real': _L0_tok_in['inv_A_real'], 'L0_tok_A_imag': _L0_tok_in['A_imag'], 'L0_tok_B_ri': _L0_tok_in['B_ri'], 'L0_attn_Wqkv': _L0_attn_in['Wqkv'], 'L0_attn_Wout': _L0_attn_in['Wout'], 'L0_attn_head_scales': _L0_attn_in['head_scales'], 'L0_attn_head_dirs': _L0_attn_in['head_dirs'], 'L0_ffn_ln_g': _L0_ffn_in['ln_g'], 'L0_ffn_ln_b': _L0_ffn_in['ln_b'], 'L0_ffn_wq': _L0_ffn_in['wq'], 'L0_ffn_wk': _L0_ffn_in['wk'], 'L0_ffn_wv': _L0_ffn_in['wv'], 'L0_ffn_wo': _L0_ffn_in['wo'], 'L0_ffn_gate_w': _L0_ffn_in['gate_w'], 'L0_ffn_w1': _L0_ffn_in['w1'], 'L0_ffn_b1': _L0_ffn_in['b1'], 'L0_ffn_w2': _L0_ffn_in['w2'], 'L0_ffn_b2': _L0_ffn_in['b2'], 'L1_attn_Wq': _L1_attn_in['Wq'], 'L1_attn_Wk': _L1_attn_in['Wk'], 'L1_attn_Wv': _L1_attn_in['Wv'], 'L1_attn_Wgk1': _L1_attn_in['Wgk1'], 'L1_attn_Wgk2': _L1_attn_in['Wgk2'], 'L1_attn_bgk2': _L1_attn_in['bgk2'], 'L1_attn_Wg': _L1_attn_in['Wg'], 'L1_attn_Wo': _L1_attn_in['Wo'], 'L1_attn_gw': _L1_attn_in['gw'], 'L1_ffn_W1': _L1_ffn_in['W1'], 'L1_ffn_b1': _L1_ffn_in['b1'], 'L1_ffn_W2': _L1_ffn_in['W2'], 'L1_ffn_b2': _L1_ffn_in['b2'], 'L1_ffn_Wg': _L1_ffn_in['Wg'], 'L1_ffn_bg': _L1_ffn_in['bg']}

def reference(x, L0_tok_log_dt, L0_tok_inv_A_real, L0_tok_A_imag, L0_tok_B_ri, L0_attn_Wqkv, L0_attn_Wout, L0_attn_head_scales, L0_attn_head_dirs, L0_ffn_ln_g, L0_ffn_ln_b, L0_ffn_wq, L0_ffn_wk, L0_ffn_wv, L0_ffn_wo, L0_ffn_gate_w, L0_ffn_w1, L0_ffn_b1, L0_ffn_w2, L0_ffn_b2, L1_attn_Wq, L1_attn_Wk, L1_attn_Wv, L1_attn_Wgk1, L1_attn_Wgk2, L1_attn_bgk2, L1_attn_Wg, L1_attn_Wo, L1_attn_gw, L1_ffn_W1, L1_ffn_b1, L1_ffn_W2, L1_ffn_b2, L1_ffn_Wg, L1_ffn_bg):
    import jax
    import jax.numpy as jnp

    def _L0_tok_ref(log_dt, inv_A_real, A_imag, B_ri, C_ri, L):
        import jax, jax.numpy as jnp
        import numpy as np
        import math
        H = 256
        N = 64
        CH = 1
        SEQ_L = 256
        dt = jnp.exp(log_dt)
        A = -jnp.exp(inv_A_real) + 1j * A_imag
        B = B_ri[..., 0] + 1j * B_ri[..., 1]
        C = C_ri[..., 0] + 1j * C_ri[..., 1]
        dtA = A * dt[:, None]
        dA = (1.0 + dtA / 2) / (1.0 - dtA / 2)
        C_term = C * B[None]
        log_dA = jnp.log(dA)
        V = jnp.exp(log_dA[:, :, None] * jnp.arange(L))
        K = 2.0 * jnp.einsum('chn,hnl->chl', C_term, V).real
        return K.astype(jnp.float32)

    def _L0_attn_ref(x, Wqkv, Wout, head_scales, head_dirs):
        import math
        import jax, jax.numpy as jnp
        import numpy as np
        B, T, D, H = (4, 256, 256, 8)
        HD = D // H

        def _trigram_dirs():
            t = np.array([[(i >> b & 1) * 2 - 1 for b in (2, 1, 0)] for i in range(8)], dtype=np.float32)
            return jnp.asarray(t / np.linalg.norm(t, axis=1, keepdims=True))
        b, t, d = x.shape
        scale = 1.0 / math.sqrt(HD)
        qkv = (x @ Wqkv).reshape(b, t, 3, H, HD)
        qkv = jnp.transpose(qkv, (2, 0, 3, 1, 4))
        q, k, v = (qkv[0], qkv[1], qkv[2])
        scores = jnp.einsum('bhqd,bhkd->bhqk', q, k) * scale
        q_proj = jnp.einsum('bhtd,hd->bht', q[..., :3], head_dirs)
        k_proj = jnp.einsum('bhtd,hd->bht', k[..., :3], head_dirs)
        geo_bias = q_proj[..., :, None] * k_proj[..., None, :]
        scores = scores + head_scales[None, :, None, None] * geo_bias
        causal = jnp.tril(jnp.ones((t, t), dtype=bool))
        scores = jnp.where(causal, scores, -jnp.inf)
        attn = jax.nn.softmax(scores, axis=-1)
        out = jnp.einsum('bhqk,bhkd->bhqd', attn, v)
        out = jnp.transpose(out, (0, 2, 1, 3)).reshape(b, t, d)
        return out @ Wout

    def _L0_ffn_ref(x, ln_g, ln_b, wq, wk, wv, wo, gate_w, w1, b1, w2, b2):
        import jax, jax.numpy as jnp
        import numpy as np
        H = 32
        MB = 2
        TOP_K = 2
        B, S, D = x.shape
        E = w1.shape[0]
        hd = D // H
        mu = jnp.mean(x, axis=-1, keepdims=True)
        var = jnp.var(x, axis=-1, keepdims=True)
        xn = (x - mu) / jnp.sqrt(var + 1e-05) * ln_g + ln_b
        q = (xn @ wq).reshape(B, S, H, hd)
        k = (xn @ wk).reshape(B, S, H, hd)
        v = (xn @ wv).reshape(B, S, H, hd)
        att = jnp.einsum('bqhd,bkhd->bhqk', q, k) / np.float32(np.sqrt(hd))
        p = jax.nn.softmax(att, axis=-1)
        o = jnp.einsum('bhqk,bkhd->bqhd', p, v).reshape(B, S, D) @ wo + x
        xf = o.reshape(-1, D)
        logits = xf @ gate_w.T
        _ = jax.lax.top_k(logits, TOP_K)
        tpe = xf.shape[0] // (MB * E)
        xe = xf.reshape(MB, E, tpe, D)
        h = jax.nn.gelu(jnp.einsum('metd,edf->metf', xe, w1) + b1[None, :, None, :], approximate=False)
        y = jnp.einsum('metf,efd->metd', h, w2) + b2[None, :, None, :]
        return y.reshape(B, S, D)

    def _L1_attn_ref(x, Wq, Wk, Wv, Wgk1, Wgk2, bgk2, Wg, Wo, gw):
        import jax, jax.numpy as jnp
        import numpy as np
        B, T, H = (2, 256, 256)
        NH = 4
        DK, DV = (128, 256)
        dk, dv = (DK // NH, DV // NH)
        LR = 16
        GATE_NORM = 16.0
        EPS = 1e-05
        b, t, _ = x.shape
        q = (x @ Wq).reshape(b, t, NH, dk)
        k = (x @ Wk).reshape(b, t, NH, dk)
        v = (x @ Wv).reshape(b, t, NH, dv)
        gk = (jax.nn.log_sigmoid(x @ Wgk1 @ Wgk2 + bgk2) / GATE_NORM).reshape(b, t, NH, dk)
        scale = dk ** (-0.5)

        def step(S, inp):
            q_t, k_t, v_t, gk_t = inp
            S = jnp.exp(gk_t)[..., None] * S + k_t[..., None] * v_t[..., None, :]
            o_t = jnp.einsum('bhk,bhkv->bhv', q_t, S) * scale
            return (S, o_t)
        xs = tuple((jnp.moveaxis(a, 1, 0) for a in (q, k, v, gk)))
        S0 = jnp.zeros((b, NH, dk, dv), x.dtype)
        _, o = jax.lax.scan(step, S0, xs)
        o = jnp.moveaxis(o, 0, 1)
        g = (x @ Wg).reshape(b, t, NH, dv)
        o = o * jax.lax.rsqrt(jnp.mean(o * o, axis=-1, keepdims=True) + EPS) * gw
        o = o * (g * jax.nn.sigmoid(g))
        return o.reshape(b, t, DV) @ Wo

    def _L1_ffn_ref(x, W1, b1, W2, b2, Wg, bg):
        import jax, jax.numpy as jnp
        import numpy as np
        N_EMBD = 256
        N_EXPERTS = 8
        TOP_K = 2
        B, T = (4, 512)
        gate_scores = jax.nn.softmax(jnp.einsum('btc,ce->bte', x, Wg) + bg, axis=-1)
        h = jax.nn.relu(jnp.einsum('btc,ech->bteh', x, W1) + b1)
        expert_out = jnp.einsum('bteh,ehc->btec', h, W2) + b2
        topk_scores, topk_idx = jax.lax.top_k(gate_scores, TOP_K)
        top_probs = jax.nn.softmax(topk_scores, axis=-1)
        sel = jnp.take_along_axis(expert_out, topk_idx[..., None], axis=2)
        out = jnp.sum(sel * top_probs[..., None], axis=2)
        return out
    h = _L0_tok_ref(L0_tok_log_dt, L0_tok_inv_A_real, L0_tok_A_imag, L0_tok_B_ri, x, 256)
    h = _layernorm(h + _L0_attn_ref(h, L0_attn_Wqkv, L0_attn_Wout, L0_attn_head_scales, L0_attn_head_dirs), axis=-1)
    h = _layernorm(h + _L0_ffn_ref(h, L0_ffn_ln_g, L0_ffn_ln_b, L0_ffn_wq, L0_ffn_wk, L0_ffn_wv, L0_ffn_wo, L0_ffn_gate_w, L0_ffn_w1, L0_ffn_b1, L0_ffn_w2, L0_ffn_b2), axis=-1)
    h = _layernorm(h + _L1_attn_ref(h, L1_attn_Wq, L1_attn_Wk, L1_attn_Wv, L1_attn_Wgk1, L1_attn_Wgk2, L1_attn_bgk2, L1_attn_Wg, L1_attn_Wo, L1_attn_gw), axis=-1)
    h = _layernorm(h + _L1_ffn_ref(h, L1_ffn_W1, L1_ffn_b1, L1_ffn_W2, L1_ffn_b2, L1_ffn_Wg, L1_ffn_bg), axis=-1)
    return h

_drawn_inputs = setup_inputs


def setup_inputs(seed=0):
    import zlib

    import numpy as np

    out = dict(_drawn_inputs(seed))
    spreads = {'L0_ffn_ln_g': (1.0, 0.2),
     'L0_ffn_ln_b': (0.0, 0.1),
     'L0_ffn_b1': (0.0, 0.1),
     'L0_ffn_b2': (0.0, 0.1),
     'L1_attn_bgk2': (0.0, 0.8),
     'L1_attn_gw': (1.0, 0.6)}
    factors = {'L0_attn_head_scales': 3.526,
     'L0_attn_head_dirs': 3.596,
     'L1_attn_Wgk1': 8.0,
     'L1_attn_Wgk2': 8.0,
     'L1_ffn_b1': 5.56,
     'L1_ffn_b2': 4.539}
    for name, (base, spread) in spreads.items():
        noise = np.random.default_rng([zlib.crc32(name.encode()), seed]).standard_normal(out[name].shape)
        drawn = base * np.exp(spread * noise) if base else spread * noise
        out[name] = jnp.asarray(drawn.astype(out[name].dtype))
    for name, factor in factors.items():
        out[name] = (out[name] * factor).astype(out[name].dtype)
    return out
```

```python
import numpy as np
from contextlib import ExitStack
import concourse.bass as bass
from concourse import mybir

fp32 = mybir.dt.float32
f32r = mybir.dt.float32r
bf16 = mybir.dt.bfloat16
i32 = mybir.dt.int32
u32 = mybir.dt.uint32
ALU = mybir.AluOpType
ACT = mybir.ActivationFunctionType
AX = mybir.AxisListType

P = 128
B, T, D = 8, 256, 256
N_STATE = 64
DC = D // P
LN_EPS = 1e-5
NEG = -1e30


class Counted:

    def __init__(self, eng, sem):
        self.eng, self.sem, self.n = eng, sem, 0

    def mark(self, ins):
        self.n += 1
        ins.then_inc(self.sem, 1)
        return ins

    def step(self, ins):
        self.mark(ins)
        self.eng.wait_ge(self.sem, self.n)

    def sync(self):
        if self.n:
            self.eng.wait_ge(self.sem, self.n)


def s4_tokens(nc, ctx, x, log_dt, inv_a_real, a_imag, b_ri, h0, ident):
    CH, HF, NB, NA = B, T // P, 64, 4
    HP, NG = P, 4
    GT = HP // NG
    M = CH * NA

    def sb(name, shape, dt=fp32):
        return ctx.enter_context(nc.sbuf_tensor(name, shape, dt))

    xin = sb("s4_x", [P, HF, CH, N_STATE, 2])
    bin_ = sb("s4_b", [P, HF, N_STATE, 2])
    ea = sb("s4_ea", [P, 2 + HF * N_STATE])
    ex = [sb(f"s4_ex{i}", [P, 2 + HF * N_STATE]) for i in range(3)]
    exi = sb("s4_exi", [P, 2 + HF * N_STATE], i32)
    aim = sb("s4_aim", [P, HF, N_STATE])
    q = [sb(f"s4_q{i}", [P, HF, N_STATE]) for i in range(5)]
    da = sb("s4_da", [P, 2, HF, N_STATE])
    cb = sb("s4_cb", [P, 2, CH, HF, N_STATE])
    ct = sb("s4_ct", [P, HF, CH, N_STATE])
    dat = sb("s4_dat", [P, 2, HP])
    cbt = sb("s4_cbt", [P, 2, CH, HP])
    pw = [sb(f"s4_pw{i}", [P, 2, GT, NB]) for i in range(2)]
    cs = [sb(f"s4_cs{i}", [P, 2, GT, NA, CH]) for i in range(2)]
    csn = [sb(f"s4_csn{i}", [P, GT, NA, CH]) for i in range(2)]
    dk = [sb(f"s4_dk{i}", [P, 2, GT]) for i in range(2)]
    dk2 = sb("s4_dk2", [P, GT])
    t1 = sb("s4_t1", [P, 2, GT, NB // 2])
    t2 = sb("s4_t2", [P, 2, GT, NB // 2])
    out = [sb(f"s4_out{i}", [M, GT, NB]) for i in range(4)]
    ps = [ctx.enter_context(nc.psum_tensor(f"s4_ps{i}", [P, 512], fp32)) for i in range(8)]

    def sem(n):
        return ctx.enter_context(nc.semaphore(n))

    loaded = sem("s4_loaded")
    prepared, transposed, columns = sem("s4_prepared"), sem("s4_transposed"), sem("s4_columns")
    powers, negated = sem("s4_powers"), sem("s4_negated")
    bank_full, bank_free = sem("s4_bank_full"), sem("s4_bank_free")
    stored = [sem(f"s4_stored{i}") for i in range(4)]
    steps, asteps, constants = sem("s4_steps"), sem("s4_asteps"), sem("s4_constants")
    NLOAD = 6
    NT = 2 + 2 * CH
    TOK_BANK = 8
    BG = GT // TOK_BANK

    with nc.Block() as block:
        @block.sync
        def _(sp):
            sp.dma_start(ea[:, 0:HF], log_dt).then_inc(loaded, 16)
            sp.dma_start(ea[:, HF:].rearrange("p (f n) -> p f n", f=HF),
                         inv_a_real.rearrange("(f p) n -> p f n", p=P)).then_inc(loaded, 16)
            sp.dma_start(aim[:, :, :], a_imag.rearrange("(f p) n -> p f n", p=P)).then_inc(loaded, 16)
            sp.dma_start(bin_[:, :, :, :], b_ri.rearrange("(f p) n r -> p f n r", p=P)).then_inc(loaded, 16)
            for f in range(HF):
                sp.dma_start(xin[:, f].rearrange("p c n r -> p c (n r)"),
                             x[:, f * P:(f + 1) * P].rearrange("c p n r -> p c (n r)")).then_inc(loaded, 16)
            for g in range(NG):
                for f in range(HF):
                    n = HF * g + f
                    sp.wait_ge(bank_free, BG * (n + 1))
                    t0 = f * P + g * GT
                    for a in range(NA):
                        sp.dma_start(h0[:, t0:t0 + GT, a * NB:(a + 1) * NB],
                                     out[n % 4][a * CH:(a + 1) * CH, :, :]).then_inc(stored[n % 4], 16)
            for k in range(4):
                sp.wait_ge(stored[k], 16 * NA * NG * HF // 4)

        @block.gpsimd
        def _(pool):
            nc.gpsimd.memset(ident[:, :], 0.0).then_inc(constants, 1)
            pool.wait_ge(constants, 1)
            nc.gpsimd.affine_select(out=ident[:, :], in_=ident[:, :], compare_op=ALU.not_equal, fill=1.0,
                                    base=0, pattern=[[-1, P]], channel_multiplier=1).then_inc(constants, 1)

        @block.vector
        def _(dve):
            s = Counted(dve, steps)
            v = nc.vector
            dve.wait_ge(loaded, 16 * NLOAD)
            y, r, kf = ex
            s.step(v.tensor_scalar(y[:, :], ea[:, :], -87.0, 88.0, ALU.max, ALU.min))
            s.step(v.tensor_scalar(exi[:, :], y[:, :], 1.4426950408889634, None, ALU.mult))
            s.step(v.tensor_copy(kf[:, :], exi[:, :]))
            s.step(v.scalar_tensor_tensor(r[:, :], kf[:, :], -0.693359375, y[:, :], ALU.mult, ALU.add))
            s.step(v.scalar_tensor_tensor(r[:, :], kf[:, :], 2.12194440e-4, r[:, :], ALU.mult, ALU.add))
            s.step(v.tensor_scalar(y[:, :], r[:, :], 1 / 5040, None, ALU.mult))
            for c in (1 / 720, 1 / 120, 1 / 24, 1 / 6, 1 / 2, 1.0):
                s.step(v.scalar_tensor_tensor(y[:, :], y[:, :], c, r[:, :], ALU.add, ALU.mult))
            s.step(v.tensor_scalar(exi[:, :], kf[:, :], 127.0, float(1 << 23), ALU.add, ALU.mult))
            s.step(v.scalar_tensor_tensor(ea[:, :], y[:, :], 1.0, exi[:, :].bitcast(fp32), ALU.add, ALU.mult))
            a, b, m, dn, w = q
            for f in range(HF):
                s.mark(v.tensor_scalar(a[:, f, :], ea[:, HF + f * N_STATE:HF + (f + 1) * N_STATE],
                                       ea[:, f:f + 1], -0.5, ALU.mult, ALU.mult))
                s.mark(v.tensor_scalar(b[:, f, :], aim[:, f, :], ea[:, f:f + 1], 0.5, ALU.mult, ALU.mult))
            s.sync()
            s.mark(v.tensor_tensor(m[:, :, :], b[:, :, :], b[:, :, :], ALU.mult))
            s.step(v.tensor_scalar(dn[:, :, :], a[:, :, :], -1.0, 1.0, ALU.mult, ALU.add))
            s.mark(v.tensor_tensor(dn[:, :, :], dn[:, :, :], dn[:, :, :], ALU.mult))
            s.step(v.tensor_tensor(w[:, :, :], a[:, :, :], a[:, :, :], ALU.mult))
            s.mark(v.tensor_tensor(dn[:, :, :], dn[:, :, :], m[:, :, :], ALU.add))
            s.step(v.tensor_tensor(w[:, :, :], w[:, :, :], m[:, :, :], ALU.add))
            s.mark(v.reciprocal(dn[:, :, :], dn[:, :, :]))
            s.step(v.tensor_scalar(w[:, :, :], w[:, :, :], -1.0, 1.0, ALU.mult, ALU.add))
            s.mark(v.tensor_tensor(da[:, 0, :, :], w[:, :, :], dn[:, :, :], ALU.mult))
            s.mark(v.scalar_tensor_tensor(da[:, 1, :, :], b[:, :, :], 2.0, dn[:, :, :], ALU.mult, ALU.mult))
            xr, xi = xin[:, :, :, :, 0], xin[:, :, :, :, 1]
            shape = [P, HF, CH, N_STATE]
            br = bin_[:, :, :, 0].unsqueeze(2).to_broadcast(shape)
            bi = bin_[:, :, :, 1].unsqueeze(2).to_broadcast(shape)
            cbr = cb[:, 0].rearrange("p c f n -> p f c n")
            cbi = cb[:, 1].rearrange("p c f n -> p f c n")
            s.step(v.tensor_scalar(bin_[:, :, :, :], bin_[:, :, :, :], 2.0, None, ALU.mult))
            s.mark(v.tensor_tensor(cbr, xr, br, ALU.mult))
            s.step(v.tensor_tensor(ct[:, :, :, :], xi, bi, ALU.mult))
            s.step(v.tensor_tensor(cbr, cbr, ct[:, :, :, :], ALU.subtract))
            s.mark(v.tensor_tensor(cbi, xr, bi, ALU.mult))
            s.step(v.tensor_tensor(ct[:, :, :, :], xi, br, ALU.mult))
            v.tensor_tensor(cbi, cbi, ct[:, :, :, :], ALU.add).then_inc(prepared, 1)

            def cmul(dst, src, d, n):
                shp = [P, GT] + n
                dr, di = d[:, 0, :], d[:, 1, :]
                for _ in n:
                    dr, di = dr.unsqueeze(len(dr.shape)), di.unsqueeze(len(di.shape))
                dr, di = dr.to_broadcast(shp), di.to_broadcast(shp)
                size = 1
                for k in n:
                    size *= k
                u = [t1[:, i, :, 0:size] for i in range(2)]
                w = [t2[:, i, :, 0:size] for i in range(2)]
                if len(n) > 1:
                    u = [z.rearrange("p t (a c) -> p t a c", a=n[0]) for z in u]
                    w = [z.rearrange("p t (a c) -> p t a c", a=n[0]) for z in w]
                s.mark(v.tensor_tensor(u[0], src[0], dr, ALU.mult))
                s.mark(v.tensor_tensor(w[0], src[1], di, ALU.mult))
                s.mark(v.tensor_tensor(u[1], src[0], di, ALU.mult))
                s.step(v.tensor_tensor(w[1], src[1], dr, ALU.mult))
                s.mark(v.tensor_tensor(dst[0], u[0], w[0], ALU.subtract))
                s.step(v.tensor_tensor(dst[1], u[1], w[1], ALU.add))

            dve.wait_ge(columns, 5)
            for g in range(NG):
                pg, cg = pw[g % 2], cs[g % 2]
                tok = slice(g * GT, (g + 1) * GT)
                if g >= 2:
                    dve.wait_ge(bank_full, HF * BG * (g - 1))
                    dve.wait_ge(negated, g - 1)
                s.mark(v.memset(pg[:, 0, :, 0:1], 1.0))
                s.mark(v.memset(pg[:, 1, :, 0:1], 0.0))
                s.step(v.tensor_copy(dk[0][:, :, :], dat[:, :, tok]))
                for k in range(8):
                    cur, nxt = dk[k % 2], dk[(k + 1) % 2]
                    if k < 6:
                        n = 1 << k
                        cmul([pg[:, i, :, n:2 * n] for i in range(2)], [pg[:, i, :, 0:n] for i in range(2)],
                             cur, [n])
                    elif k == 6:
                        for i in range(2):
                            s.step(v.tensor_copy(cg[:, i, :, 0, :], cbt[:, i, :, tok].rearrange("p c t -> p t c")))
                        cmul([cg[:, i, :, 1, :] for i in range(2)], [cg[:, i, :, 0, :] for i in range(2)],
                             cur, [CH])
                    else:
                        cmul([cg[:, i, :, 2:4, :] for i in range(2)], [cg[:, i, :, 0:2, :] for i in range(2)],
                             cur, [2, CH])
                    if k < 7:
                        s.mark(v.tensor_tensor(dk2[:, :], cur[:, 1, :], cur[:, 1, :], ALU.mult))
                        s.step(v.tensor_tensor(nxt[:, 0, :], cur[:, 0, :], cur[:, 0, :], ALU.mult))
                        s.mark(v.tensor_tensor(nxt[:, 0, :], nxt[:, 0, :], dk2[:, :], ALU.subtract))
                        s.step(v.scalar_tensor_tensor(nxt[:, 1, :], cur[:, 0, :], 2.0, cur[:, 1, :],
                                                      ALU.mult, ALU.mult))
                s.sync()
                v.memset(dk2[:, 0:1], 0.0).then_inc(powers, 1)

        @block.scalar
        def _(act):
            for k in range(5):
                act.wait_ge(transposed, k + 1)
                for i in range(4 if k < 4 else 2):
                    n = 4 * k + i
                    dst = cbt[:, n // CH, n % CH, :] if n < 2 * CH else dat[:, n - 2 * CH, :]
                    last = nc.scalar.copy(dst, ps[k][:, i * P:(i + 1) * P])
                last.then_inc(columns, 1)

            def negate(g):
                act.wait_ge(powers, g + 1)
                if g >= 2:
                    act.wait_ge(bank_full, HF * BG * (g - 1))
                nc.scalar.mul(csn[g % 2][:, :, :, :], cs[g % 2][:, 1], -1.0).then_inc(negated, 1)

            negate(0)
            n = 0
            for g in range(NG):
                if g + 1 < NG:
                    negate(g + 1)
                for f in range(HF):
                    m = HF * g + f
                    if m >= 4:
                        act.wait_ge(stored[m % 4], 16 * NA * (m // 4))
                    for k in range(BG):
                        act.wait_ge(bank_full, n + 1)
                        nc.scalar.copy(out[m % 4][:, k * TOK_BANK:(k + 1) * TOK_BANK, :],
                                       ps[n % 8][0:M, :].rearrange("p (t b) -> p t b", b=NB)).then_inc(bank_free, 1)
                        n += 1

        @block.tensor
        def _(pe):
            pe.wait_ge(prepared, 1)
            pe.wait_ge(constants, 2)
            for n in range(NT):
                src = cb[:, n // CH, n % CH] if n < 2 * CH else da[:, n - 2 * CH]
                last = nc.tensor.transpose(ps[n // 4][:, (n % 4) * P:(n % 4 + 1) * P],
                                           src.rearrange("p f n -> p (f n)"), ident[:, :])
                if n % 4 == 3 or n == NT - 1:
                    last.then_inc(transposed, 1)
            n = 0
            pe.wait_ge(columns, 5)
            for g in range(NG):
                pe.wait_ge(negated, g + 1)
                for f in range(HF):
                    rows = slice(64 * f, 64 * f + 64)
                    for k in range(BG):
                        if n >= 8:
                            pe.wait_ge(bank_free, n - 7)
                        for i in range(TOK_BANK):
                            t = k * TOK_BANK + i
                            o = ps[n % 8][0:M, i * NB:(i + 1) * NB]
                            nc.tensor.matmul(o, cs[g % 2][rows, 0, t].rearrange("p a c -> p (a c)"),
                                             pw[g % 2][rows, 0, t, :], start=True, stop=False)
                            last = nc.tensor.matmul(o, csn[g % 2][rows, t].rearrange("p a c -> p (a c)"),
                                                    pw[g % 2][rows, 1, t, :], start=False, stop=True)
                        last.then_inc(bank_full, 1)
                        n += 1


class Signals:

    def __init__(self, nc, ctx, prefix):
        self.nc, self.ctx, self.prefix, self.all = nc, ctx, prefix, {}

    def __call__(self, name):
        if name not in self.all:
            self.all[name] = self.ctx.enter_context(self.nc.semaphore(f"{self.prefix}_{name}"))
        return self.all[name]


def rsqrt_steps(s, v, x, y, a):
    s.step(v.tensor_scalar(y.bitcast(i32), x.bitcast(i32), 1, None, ALU.logical_shift_right))
    s.step(v.tensor_scalar(y.bitcast(i32), y.bitcast(i32), -1.0, float(0x5F3759DF), ALU.mult, ALU.add))
    for _ in range(3):
        s.step(v.scalar_tensor_tensor(a, y, -0.5, y, ALU.mult, ALU.mult))
        s.step(v.tensor_tensor(a, a, x, ALU.mult))
        s.step(v.scalar_tensor_tensor(y, a, 1.5, y, ALU.add, ALU.mult))


class Attention:

    RING = 4

    def __init__(self, name, heads, dim, causal):
        self.name, self.heads, self.dim, self.causal = name, heads, dim, causal
        self.rows = 4 * dim
        self.lanes = P // (2 * self.rows) or 1
        self.slots = 4
        self.group = self.lanes * self.slots
        self.per_batch = heads // self.group
        self.groups = 2 * self.per_batch
        self.vw = 32 if dim < 32 else 64
        self.quad = P // self.vw
        self.units = self.groups * self.group

    def lane_slot(self, n):
        return n // self.slots, n % self.slots

    def quad_end(self, u):
        return u % self.quad == self.quad - 1


def main_loop(nc, ctx, io, h0, x3, ident):
    NTB = 4
    TOK = NTB * P
    PAIRS = B // 2
    F = 1024
    FT = F // P
    E_IT = 2
    NHG, DK, DV = 4, 32, 64
    att0 = Attention("a0", 8, 32, True)
    att1 = Attention("a1", 32, 8, False)

    def sb(name, shape, dt=fp32, c=ctx):
        return c.enter_context(nc.sbuf_tensor(name, shape, dt))

    def dram(name, shape):
        return nc.dram_tensor(name, shape, fp32).ap()

    wqkv0 = sb("wqkv0", [P, DC, 3 * D])
    wout0 = sb("wout0", [P, DC, D])
    wq1, wk1, wv1, wo1 = (sb(n, [P, DC, D]) for n in ("wq1", "wk1", "wv1", "wo1"))
    gwq, gwk = sb("gwq", [P, DC, P]), sb("gwk", [P, DC, P])
    gwvg = sb("gwvg", [P, DC, 2 * D])
    gwgk1, gwgk2 = sb("gwgk1", [P, DC, 16]), sb("gwgk2", [16, P])
    gwo = sb("gwo", [P, DC, D])
    bgk = sb("bgk", [P, 1])
    gwb = sb("gwb", [P, DV])
    lng, lnb = sb("lng", [P, D]), sb("lnb", [P, D])
    dirs, hsc = sb("dirs", [P, 8, 3]), sb("hsc", [P, 8])
    gp, gq = sb("gp", [P, DC, 8, 3]), sb("gq", [P, DC, 8])
    identb = sb("identb", [P, P], bf16)
    mask_s, mask_t = sb("mask_s", [P, 3 * P], bf16), sb("mask_t", [P, 3 * P], bf16)
    mask_g = sb("mask_g", [P, P])
    ones2 = sb("ones2", [2, P], f32r)
    onesr = sb("onesr", [P, T])
    ha, hb, yb, ob, vb = (sb(n, [P, NTB, D]) for n in ("ha", "hb", "yb", "ob", "vb"))
    tt = sb("tt", [P, DC, TOK])
    stats, mv = sb("stats", [P, NTB, 6]), sb("mv", [P, NTB, 2])
    rs = [sb(f"rs{i}", [P, 16]) for i in range(3)]
    w1, w2 = sb("w1", [P, E_IT, DC, F]), sb("w2", [P, E_IT, FT, D])
    b1r, b1c = sb("b1r", [E_IT * FT, P]), sb("b1c", [P, E_IT * FT])
    b2b = sb("b2b", [P, E_IT, D])
    kst = sb("kst", [P, 4, 4, T], f32r)
    vpad = {"a0": sb("vpad0", [P, 2, 2, 2 * 384]), "a1": sb("vpad1", [P, 2, 2, 2 * 640])}
    mx = sb("mx", [P, 2, 2, 8])
    rc = sb("rc", [P, 8])
    rows_hl = sb("rows_hl", [8, 2, 2, T], f32r)
    acc = [sb(f"acc{i}", [P, T]) for i in range(2)]
    sd = sb("sd", [P, 2, D])
    shared = ExitStack()
    hl = {k: sb(k, [P, 2, TOK], f32r, shared) for k in ("q_hi", "q_lo", "k_hi", "k_lo")}
    qst = sb("qst", [P, 4, 4, T], f32r, shared)
    mrow = sb("mrow", [2, 3, 4, T], f32r, shared)
    pt = [sb(f"pt{i}", [P, 2 * T], fp32, shared) for i in range(4)]
    shared.close()
    hid = sb("hid", [P, E_IT, FT, T])
    qs, ks = sb("qs", [P, TOK]), sb("ks", [P, TOK])
    gz, gm, ge, gG = (sb(n, [P, TOK]) for n in ("gz", "gm", "ge", "gG"))
    u1 = sb("u1", [16, TOK])
    atm = sb("atm", [P, NHG, NTB, P])
    kT = sb("kT", [P, 2, P])
    dr = sb("dr", [P, 2])
    gb = sb("gb", [P, NTB, D])
    ps = [ctx.enter_context(nc.psum_tensor(f"ps{i}", [P, 512], fp32)) for i in range(8)]
    xs = {a.name: {k: dram(f"{a.name}_{k}_parts", (a.heads, 4, a.dim, TOK)) for k in "qk"} for a in (att0, att1)}

    sg = Signals(nc, ctx, "m")
    once = Signals(nc, ctx, "w")
    done, go = once("done"), {k: once(f"go_{k}") for k in ("sp", "pe", "act", "pool")}
    loads = []

    def w_in(dst, src):
        loads.append((dst, src))

    def rows_view(ap):
        return ap.rearrange("(c p) n -> p c n", p=P)

    w_in(wqkv0[:, :, :], rows_view(io["L0_attn_Wqkv"]))
    w_in(dirs[:, :, :].rearrange("p h d -> p (h d)"),
         io["L0_attn_head_dirs"].rearrange("h d -> (h d)").partition_broadcast(P))
    w_in(hsc[:, :], io["L0_attn_head_scales"].partition_broadcast(P))
    w_in(wout0[:, :, :], rows_view(io["L0_attn_Wout"]))
    for dst, n in ((wq1, "wq"), (wk1, "wk"), (wv1, "wv"), (wo1, "wo")):
        w_in(dst[:, :, :], rows_view(io[f"L0_ffn_{n}"]))
    w_in(lng[:, :], io["L0_ffn_ln_g"].partition_broadcast(P))
    w_in(lnb[:, :], io["L0_ffn_ln_b"].partition_broadcast(P))
    w_in(gwq[:, :, :], rows_view(io["L1_attn_Wq"]))
    w_in(gwk[:, :, :], rows_view(io["L1_attn_Wk"]))
    w_in(gwvg[:, :, 0:D], rows_view(io["L1_attn_Wv"]))
    w_in(gwvg[:, :, D:], rows_view(io["L1_attn_Wg"]))
    w_in(gwgk1[:, :, :], rows_view(io["L1_attn_Wgk1"]))
    w_in(gwgk2[:, :], io["L1_attn_Wgk2"])
    w_in(gwo[:, :, :], rows_view(io["L1_attn_Wo"]))
    w_in(bgk[:, :], io["L1_attn_bgk2"].rearrange("(p o) -> p o", o=1))
    w_in(gwb[:, :], io["L1_attn_gw"].partition_broadcast(P))
    w_loaded, constants, ready = once("loaded"), once("constants"), once("ready")

    def vslot(a, buf, kt, what):
        n, w = a.group // a.quad, a.vw * (a.quad + 1)
        flat = vpad[a.name][:, buf, kt, 0:n * a.quad * w]
        return flat.rearrange("p (h w) -> p h w", w=w)

    def window(a, buf, kt, n):
        w = a.vw * (a.quad + 1)
        at = (n // a.quad) * a.quad * w + (n % a.quad) * P
        return vpad[a.name][:, buf, kt, at:at + P]

    block_ctx = ExitStack()
    block = block_ctx.enter_context(nc.Block())

    @block.sync
    def _(sp):
        for dst, src in loads:
            sp.dma_start(dst, src).then_inc(w_loaded, 16)

        def attention_operands(a):
            hw = P // a.dim
            k = 0
            for t in range(2):
                for which in "qk":
                    order = ("hi", "lo", "hi", "lo") if which == "q" else ("hi", "lo", "lo", "hi")
                    if t == 0 and which == "q":
                        sp.wait_ge(sg(a.name + "_hi"), 4)
                        sp.wait_ge(sg(a.name + "_lo"), 4)
                    for part in range(4):
                        sp.dma_start(xs[a.name][which][t * hw:(t + 1) * hw, part, :, :],
                                     hl[f"{which}_{order[part]}"][:, t, :].bitcast(fp32))\
                            .then_inc(sg(a.name + "_parts_out"), 16)
                        k += 1
            sp.wait_ge(sg(a.name + "_parts_out"), 16 * k)
            def stack(g):
                bb, g1 = g // a.per_batch, g % a.per_batch
                if g >= a.RING:
                    sp.wait_ge(sg(a.name + "_st_full"), (g - a.RING + 1) * a.group)
                for which, st in (("q", qst), ("k", kst)):
                    for lane in range(a.lanes):
                        h = g1 * a.group + lane * a.slots
                        src = xs[a.name][which][h:h + a.slots, :, :, bb * T:(bb + 1) * T]
                        sp.dma_start(st[64 * lane:64 * lane + a.rows, g % a.RING, :, :].bitcast(fp32),
                                     src.rearrange("h p d t -> (p d) h t"))\
                            .then_inc(sg(f"{a.name}_stack{g % a.RING}"), 16)

            def send_rows(gr):
                sp.wait_ge(sg(a.name + "_rows"), gr + 1)
                if a.lanes == 1 and gr >= 3:
                    sp.wait_ge(sg(a.name + "_st_full"), (gr - 2) * a.group)
                for lane in range(a.lanes):
                    for part in range(2):
                        row = 64 * lane + a.rows + part
                        dst = mrow[part:part + 1, gr % 3] if a.lanes == 1 else qst[row:row + 1, gr % a.RING]
                        sp.dma_start(dst.bitcast(fp32), rows_hl[lane * a.slots:(lane + 1) * a.slots, gr % 2, part, :]
                                     .bitcast(fp32)).then_inc(sg(f"{a.name}_rows_in{gr % 2}"), 16)

            for g in range(a.RING):
                stack(g)
            for g in range(a.groups):
                send_rows(g)
                if g >= 2 and g + 2 < a.groups:
                    stack(g + 2)

        with sp.Fori(0, PAIRS) as j:
            for bb in range(2):
                sp.dma_start(ha[:, 2 * bb:2 * bb + 2, :],
                             h0[j + PAIRS * bb].rearrange("(k p) d -> p k d", p=P))\
                    .then_inc(sg("h_in"), 16)
            for e in range(E_IT):
                sp.dma_start(w1[:, e, :, :], rows_view(io["L0_ffn_w1"][E_IT * j + e])).then_inc(sg("w_in"), 16)
                sp.dma_start(w2[:, e, :, :], rows_view(io["L0_ffn_w2"][E_IT * j + e])).then_inc(sg("w_in"), 16)
                sp.dma_start(b1r[e * FT:(e + 1) * FT, :],
                             io["L0_ffn_b1"][E_IT * j + e].rearrange("(c p) -> c p", p=P)).then_inc(sg("w_in"), 16)
                sp.dma_start(b2b[:, e, :], io["L0_ffn_b2"][E_IT * j + e].partition_broadcast(P))\
                    .then_inc(sg("w_in"), 16)
            attention_operands(att0)
            attention_operands(att1)
            sp.wait_ge(sg("h3"), 1)
            for bb in range(2):
                sp.dma_start(x3[j + PAIRS * bb].rearrange("(k p) d -> p k d", p=P), hb[:, 2 * bb:2 * bb + 2, :])\
                    .then_inc(sg("x3_out"), 16)
            sp.wait_ge(sg("x3_out"), 32)
            sp.sem_inc(done, 1)
            sp.wait_ge(go["sp"], 1)
            sp.sem_clear(go["sp"])

    @block.gpsimd
    def _(pool):
        g = nc.gpsimd
        g.tensor_copy(identb[:, :], ident[:, :]).then_inc(constants, 1)
        g.memset(mask_s[:, :], 0.0).then_inc(constants, 1)
        g.memset(mask_t[:, :], 0.0).then_inc(constants, 1)
        g.memset(mask_g[:, :], 1.0).then_inc(constants, 1)
        g.memset(onesr[:, :], 1.0).then_inc(constants, 1)
        pool.wait_ge(constants, 5)
        g.memset(mask_s[:, 2 * P:], NEG).then_inc(constants, 1)
        g.memset(mask_t[:, 0:P], NEG).then_inc(constants, 1)
        g.affine_select(out=mask_s[:, P:2 * P], in_=mask_s[:, P:2 * P], compare_op=ALU.is_ge, fill=NEG,
                        base=0, pattern=[[-1, P]], channel_multiplier=1).then_inc(constants, 1)
        g.affine_select(out=mask_t[:, P:2 * P], in_=mask_t[:, P:2 * P], compare_op=ALU.is_ge, fill=NEG,
                        base=0, pattern=[[1, P]], channel_multiplier=-1).then_inc(constants, 1)
        g.affine_select(out=mask_g[:, :], in_=mask_g[:, :], compare_op=ALU.is_ge, fill=0.0,
                        base=0, pattern=[[1, P]], channel_multiplier=-1).then_inc(constants, 1)
        for a in (att0, att1):
            g.memset(vpad[a.name][:, :, :, :], 0.0).then_inc(constants, 1)
        g.memset(sd[:, :, :], 0.0).then_inc(constants, 1)
        pool.wait_ge(constants, 13)
        for a in (att0, att1):
            for buf in range(2):
                for kt in range(2):
                    g.memset(vslot(a, buf, kt, 1)[:, :, a.dim:a.dim + 1], 1.0).then_inc(constants, 1)
        pool.wait_ge(constants, 21)

        def attention_feed(a):
            def pad_v(gr):
                bb, g1 = gr // a.per_batch, gr % a.per_batch
                if gr >= 2:
                    pool.wait_ge(sg(a.name + "_av_done"), (gr - 1) * a.group)
                for kt in range(2):
                    last = g.tensor_copy(
                        vslot(a, gr % 2, kt, 0)[:, :, 0:a.dim],
                        vb[:, 2 * bb + kt, g1 * a.group * a.dim:(g1 + 1) * a.group * a.dim]
                        .rearrange("p (h d) -> p h d", d=a.dim))
                    if kt == 0:
                        last.then_inc(sg(a.name + "_pad0"), 1)
                last.then_inc(sg(a.name + "_padded"), 1)

            pool.wait_ge(sg(a.name + "_v"), 2)
            for gr in range(a.groups):
                pad_v(gr)

        with pool.Fori(0, PAIRS) as j:
            attention_feed(att0)
            pool.wait_ge(sg("a0_st_full"), att0.units)
            for lane in range(att1.lanes):
                r = 64 * lane + att1.rows
                last = g.memset(kst[r:r + 2, :, :, :].bitcast(fp32), 1.0)
                last.then_inc(sg("ones_row"), 1)
            pool.wait_ge(sg("ones_row"), att1.lanes)
            attention_feed(att1)
            pool.wait_ge(sg("h3"), 1)
            pool.sem_inc(done, 1)
            pool.wait_ge(go["pool"], 1)
            pool.sem_clear(go["pool"])

    @block.tensor
    def _(pe):
        mm = nc.tensor.matmul
        pe.wait_ge(ready, 1)

        def transposes(src, name, after=None):
            if after:
                pe.wait_ge(*after)
            for c in range(DC):
                for tb in range(NTB):
                    last = nc.tensor.transpose(ps[c][:, tb * P:(tb + 1) * P], src[:, tb, c * P:(c + 1) * P],
                                               ident[:, :])
                last.then_inc(sg(name + "_full"), 1)

        def qkv(a, wq, wk, wv, name):
            pe.wait_ge(sg(name + "_ev"), 2)
            for n, w in enumerate((wq, wq, wk, wk)):
                t = n % 2
                for c in range(DC):
                    last = mm(ps[2 + n][:, :], w[:, c, t * P:(t + 1) * P], tt[:, c, :],
                              start=c == 0, stop=c == DC - 1)
                last.then_inc(sg(a.name + "_qk_full"), 1)
            for tb in range(NTB):
                for c in range(DC):
                    last = mm(ps[6 + tb // 2][:, (tb % 2) * D:(tb % 2 + 1) * D],
                              tt[:, c, tb * P:(tb + 1) * P], wv[:, c, :], start=c == 0, stop=c == DC - 1)
                if tb % 2:
                    last.then_inc(sg(a.name + "_v_full"), 1)

        def project(w, name, ob_ready):
            transposes(ob, name + "_t", ob_ready)
            pe.wait_ge(sg(name + "_t_ev"), 2)
            for tb in range(NTB):
                for c in range(DC):
                    last = mm(ps[2 + tb // 2][:, (tb % 2) * D:(tb % 2 + 1) * D],
                              tt[:, c, tb * P:(tb + 1) * P], w[:, c, :], start=c == 0, stop=c == DC - 1)
                if tb % 2:
                    last.then_inc(sg(name + "_full"), 1)

        def attention(a):
            n_ = a.name
            stack_dmas = 2 * a.lanes

            def scores(u):
                g, n = u // a.group, u % a.group
                lane, slot = a.lane_slot(n)
                if u >= 2:
                    pe.wait_ge(sg(n_ + "_max"), u - 1)
                r0 = 64 * lane
                for qb in range(2):
                    o = ps[u % 2][:, qb * T:(qb + 1) * T]
                    last = mm(o, qst[r0:r0 + a.rows, g % a.RING, slot, qb * P:(qb + 1) * P],
                              kst[r0:r0 + a.rows, g % a.RING, slot, :], start=True, stop=not a.causal)
                    if a.causal:
                        at = P if qb == 0 else 0
                        last = mm(o, identb[:, :], mask_s[:, at:at + T], start=False, stop=True)
                last.then_inc(sg(n_ + "_s_full"), 1)

            def scores_t(u):
                g, n = u // a.group, u % a.group
                lane, slot = a.lane_slot(n)
                if u >= 2:
                    pe.wait_ge(sg(n_ + "_exp"), u - 1)
                r0 = 64 * lane
                rows = a.rows + (2 if a.lanes > 1 else 0)
                for kt in range(2):
                    o = ps[2 + u % 2][:, kt * T:(kt + 1) * T]
                    last = mm(o, kst[r0:r0 + rows, g % a.RING, slot, kt * P:(kt + 1) * P],
                              qst[r0:r0 + rows, g % a.RING, slot, :], start=True, stop=a.lanes > 1)
                    if a.lanes == 1:
                        mm(o, ones2[:, :], mrow[:, g % 3, slot, :], start=False, stop=False)
                        at = P if kt == 0 else 0
                        last = mm(o, identb[:, :], mask_t[:, at:at + T], start=False, stop=True)
                last.then_inc(sg(n_ + "_st_full"), 1)

            def values(u):
                g, n = u // a.group, u % a.group
                k = u // a.quad
                if u % a.quad == 0 and k >= 2:
                    pe.wait_ge(sg(n_ + "_acc"), k - 1)
                pe.wait_ge(sg(n_ + "_exp"), u + 1)
                for kt in range(2):
                    last = mm(ps[4 + k % 2][:, 0:T], window(a, g % 2, kt, n), pt[u % 4][:, kt * T:(kt + 1) * T],
                              start=u % a.quad == 0 and kt == 0, stop=a.quad_end(u) and kt == 1)
                last.then_inc(sg(n_ + "_av_done"), 1)

            def outputs_t(k):
                pe.wait_ge(sg(n_ + "_acc"), k + 1)
                if k:
                    pe.wait_ge(sg(n_ + "_norm"), k)
                for qb in range(2):
                    last = nc.tensor.transpose(ps[7][:, qb * P:(qb + 1) * P],
                                               acc[k % 2][:, qb * P:(qb + 1) * P], ident[:, :])
                last.then_inc(sg(n_ + "_o_full"), 1)

            def maxima_t(g):
                pe.wait_ge(sg(n_ + "_max"), (g + 1) * a.group)
                if g:
                    pe.wait_ge(sg(n_ + "_rows"), g)
                for qb in range(2):
                    last = nc.tensor.transpose(ps[6][0:a.group, qb * P:(qb + 1) * P],
                                               mx[:, g % 2, qb, 0:a.group], ident[:, :])
                last.then_inc(sg(n_ + "_mt_full"), 1)

            def after_values(u):
                values(u)
                if u and a.quad_end(u - 1):
                    outputs_t((u - 1) // a.quad)

            pe.wait_ge(sg(n_ + "_v"), 2)
            if a.lanes > 1:
                pe.wait_ge(sg("ones_row"), a.lanes)
            for p in range(a.groups + 2):
                gs, gt = p, p - 2
                if gs < a.groups:
                    pe.wait_ge(sg(f"{n_}_stack{gs % a.RING}"), 16 * stack_dmas * (gs // a.RING + 1))
                if gt >= 0:
                    pe.wait_ge(sg(f"{n_}_rows_in{gt % 2}"), 16 * 2 * a.lanes * (gt // 2 + 1))
                    pe.wait_ge(sg(n_ + "_padded"), gt + 1)
                for n in range(a.group):
                    if gt >= 0:
                        u = gt * a.group + n
                        scores_t(u)
                    if gs < a.groups:
                        scores(gs * a.group + n)
                    if gt >= 0 and u:
                        after_values(u - 1)
                if gs < a.groups:
                    maxima_t(gs)
            after_values(a.units - 1)
            outputs_t(a.units // a.quad - 1)

        def experts():
            pe.wait_ge(sg("w_in"), 16 * 4 * E_IT)
            nc.tensor.transpose(ps[6][:, 0:E_IT * FT], b1r[:, :], ident[0:E_IT * FT, 0:E_IT * FT])\
                .then_inc(sg("b1_full"), 1)
            pe.wait_ge(sg("xf_t_ev"), 2)
            n = 0
            for e in range(E_IT):
                mv_ = [tt[:, c, :].rearrange("p (b k t) -> p k b t", b=2, k=2)[:, e] for c in range(DC)]
                for f2 in range(FT // 2):
                    if n >= 4:
                        pe.wait_ge(sg("up_ev"), 2 * (n - 3))
                    for f in (2 * f2, 2 * f2 + 1):
                        for c in range(DC):
                            last = mm(ps[2 + n % 4][:, (f % 2) * T:(f % 2 + 1) * T],
                                      w1[:, e, c, f * P:(f + 1) * P], mv_[c], start=c == 0, stop=c == DC - 1)
                    last.then_inc(sg("up_full"), 1)
                    n += 1
            pe.wait_ge(sg("b1_ev"), 1)
            for e in range(E_IT):
                pe.wait_ge(sg("up_ev"), FT * (e + 1))
                for bb in range(2):
                    o = ps[(0, 1, 6, 7)[2 * e + bb]][:, 0:D]
                    for f in range(FT):
                        last = mm(o, hid[:, e, f, bb * P:(bb + 1) * P], w2[:, e, f, :], start=f == 0,
                                  stop=f == FT - 1)
                    last.then_inc(sg("down_full"), 1)

        def linear_attention():
            pe.wait_ge(sg("h2_t_ev"), 2)
            for n, w in ((2, gwq), (3, gwk)):
                for c in range(DC):
                    last = mm(ps[n][:, :], w[:, c, :], tt[:, c, :], start=c == 0, stop=c == DC - 1)
                last.then_inc(sg("g_qk_full"), 1)
            for c in range(DC):
                last = mm(ps[4][0:16, :], gwgk1[:, c, :], tt[:, c, :], start=c == 0, stop=c == DC - 1)
            last.then_inc(sg("g_u_full"), 1)
            for tb in range(NTB):
                for c in range(DC):
                    last = mm(ps[(6, 7, 0, 1)[tb]][:, :], tt[:, c, tb * P:(tb + 1) * P], gwvg[:, c, :],
                              start=c == 0, stop=c == DC - 1)
                last.then_inc(sg("g_vg_full"), 1)
                if tb == 0:
                    pe.wait_ge(sg("g_u"), 1)
                    mm(ps[5][:, :], gwgk2[:, :], u1[:, :], start=True, stop=True).then_inc(sg("g_z_full"), 1)
            pe.wait_ge(sg("g_qk"), 2)
            pe.wait_ge(sg("g_vg"), 8)
            for bb in range(2):
                last = nc.tensor.transpose(ps[6][:, bb * P:(bb + 1) * P], ks[:, 2 * bb * P:(2 * bb + 1) * P],
                                           ident[:, :])
            last.then_inc(sg("g_kt_full"), 1)
            for h in range(NHG):
                for tb in range(NTB):
                    last = mm(ps[2 + h][:, tb * P:(tb + 1) * P], ks[h * DK:(h + 1) * DK, tb * P:(tb + 1) * P],
                              qs[h * DK:(h + 1) * DK, tb * P:(tb + 1) * P], start=True, stop=True)
                last.then_inc(sg("g_at_full"), 1)
            pe.wait_ge(sg("g_kt"), 1)
            for bb in range(2):
                last = mm(ps[7][:, bb * D:(bb + 1) * D], kT[:, bb, :], vb[:, 2 * bb, :], start=True, stop=True)
            last.then_inc(sg("g_state_full"), 1)
            pe.wait_ge(sg("g_at"), NHG)
            pe.wait_ge(sg("g_state"), 1)
            for tb in range(NTB):
                o = ps[(0, 1, 6, 7)[tb]]
                if tb % 2:
                    mm(o[:, 0:D], qs[:, tb * P:(tb + 1) * P], sd[:, tb // 2, :], start=True, stop=False,
                       skip_group_check=True)
                for h in range(NHG):
                    last = mm(o[:, h * DV:(h + 1) * DV], atm[:, h, tb, :], vb[:, tb, h * DV:(h + 1) * DV],
                              start=tb % 2 == 0, stop=True, skip_group_check=True)
                last.then_inc(sg("g_o_full"), 1)

        with pe.Fori(0, PAIRS) as j:
            transposes(ha, "h_t", (sg("h_in"), 32))
            qkv(att0, wqkv0[:, :, 0:D], wqkv0[:, :, D:2 * D], wqkv0[:, :, 2 * D:], "h_t")
            attention(att0)
            project(wout0, "p0", (sg("a0_norm"), att0.units // att0.quad))
            transposes(yb, "xn_t", (sg("xn"), 1))
            qkv(att1, wq1, wk1, wv1, "xn_t")
            attention(att1)
            project(wo1, "p1", (sg("a1_norm"), att1.units // att1.quad))
            transposes(yb, "xf_t", (sg("xf"), 1))
            experts()
            transposes(ha, "h2_t", (sg("h2"), 1))
            linear_attention()
            project(gwo, "p2", (sg("g_o"), 1))
            pe.wait_ge(go["pe"], 1)
            pe.sem_clear(go["pe"])

    @block.scalar
    def _(act):
        sc = nc.scalar
        act.wait_ge(ready, 1)

        def transposed(name):
            act.wait_ge(sg(name + "_full"), 1)
            sc.copy(tt[:, 0, :], ps[0][:, :]).then_inc(sg(name + "_ev"), 1)

        def qkv(a):
            for n in range(4):
                act.wait_ge(sg(a.name + "_qk_full"), n + 1)
                sc.copy(hl[("q_hi", "k_hi")[n // 2]][:, n % 2, :], ps[2 + n][:, :]).then_inc(sg(a.name + "_hi"), 1)
            for n in range(2):
                act.wait_ge(sg(a.name + "_v_full"), n + 1)
                sc.copy(vb[:, 2 * n:2 * n + 2, :], ps[6 + n][:, :].rearrange("p (b d) -> p b d", b=2))\
                    .then_inc(sg(a.name + "_v"), 1)

        def attention(a):
            n_ = a.name

            def heads_out(k):
                act.wait_ge(sg(n_ + "_av_done"), (k + 1) * a.quad)
                if k >= 2:
                    act.wait_ge(sg(n_ + "_o_full"), k - 1)
                sc.copy(acc[k % 2][:, :], ps[4 + k % 2][:, 0:T]).then_inc(sg(n_ + "_acc"), 1)

            for u in range(a.units):
                act.wait_ge(sg(n_ + "_st_full"), u + 1)
                if u >= 4:
                    act.wait_ge(sg(n_ + "_av_done"), u - 3)
                sc.activation(pt[u % 4][:, :], ps[2 + u % 2][:, :], ACT.Exp).then_inc(sg(n_ + "_exp"), 1)
                if u and a.quad_end(u - 1):
                    heads_out((u - 1) // a.quad)
            heads_out(a.units // a.quad - 1)

        def experts():
            act.wait_ge(sg("b1_full"), 1)
            sc.copy(b1c[:, :], ps[6][:, 0:E_IT * FT]).then_inc(sg("b1_ev"), 1)
            act.wait_ge(sg("b1_ev"), 1)
            for n in range(E_IT * FT // 2):
                act.wait_ge(sg("up_full"), n + 1)
                for i in range(2):
                    f = 2 * n + i
                    sc.activation(hid[:, f // FT, f % FT, :], ps[2 + n % 4][:, i * T:(i + 1) * T], ACT.Gelu,
                                  bias=b1c[:, f:f + 1]).then_inc(sg("up_ev"), 1)

        def linear_attention():
            act.wait_ge(sg("g_u_full"), 1)
            sc.copy(u1[:, :], ps[4][0:16, :]).then_inc(sg("g_u"), 1)
            for tb in range(NTB):
                act.wait_ge(sg("g_vg_full"), tb + 1)
                o = ps[(6, 7, 0, 1)[tb]]
                sc.copy(vb[:, tb, :], o[:, 0:D]).then_inc(sg("g_vg"), 1)
                sc.copy(gb[:, tb, :], o[:, D:]).then_inc(sg("g_vg"), 1)
            act.wait_ge(sg("g_z"), 1)
            sc.activation(ge[:, :], ge[:, :], ACT.Exp).then_inc(sg("g_a"), 1)
            act.wait_ge(sg("g_a"), 1)
            sc.activation(ge[:, :], ge[:, :], ACT.Ln, bias=1.0).then_inc(sg("g_a"), 1)
            act.wait_ge(sg("g_d"), 1)
            sc.activation(ge[:, :], gz[:, :], ACT.Exp).then_inc(sg("g_a"), 1)
            sc.activation(gm[:, :], gz[:, :], ACT.Exp, scale=-1.0).then_inc(sg("g_a"), 1)
            act.wait_ge(sg("g_vg"), 8)
            sc.activation(yb[:, :, :], gb[:, :, :], ACT.Exp, scale=-1.0).then_inc(sg("g_a"), 1)
            sc.activation(dr[:, :], dr[:, :], ACT.Exp).then_inc(sg("g_dr"), 1)
            act.wait_ge(sg("g_kt_full"), 1)
            sc.copy(kT[:, :, :], ps[6][:, 0:2 * P].rearrange("p (b k) -> p b k", b=2)).then_inc(sg("g_kt"), 1)
            for tb in range(NTB):
                act.wait_ge(sg("g_o_full"), tb + 1)
                sc.activation(hb[:, tb, :], ps[(0, 1, 6, 7)[tb]][:, 0:D], ACT.Square).then_inc(sg("g_sq"), 1)

        with act.Fori(0, PAIRS) as j:
            transposed("h_t")
            qkv(att0)
            attention(att0)
            transposed("p0_t")
            transposed("xn_t")
            qkv(att1)
            attention(att1)
            transposed("p1_t")
            transposed("xf_t")
            experts()
            transposed("h2_t")
            linear_attention()
            transposed("p2_t")
            act.wait_ge(go["act"], 1)
            act.sem_clear(go["act"])

    @block.vector
    def _(dve):
        v = nc.vector
        s = Counted(dve, once("prepare"))
        dve.wait_ge(w_loaded, 16 * len(loads))
        dve.wait_ge(constants, 21)
        wq = wqkv0[:, :, 0:D].rearrange("p c (h k) -> p c h k", h=8)
        for c in range(DC):
            s.step(v.tensor_tensor(gp[:, c], wq[:, c, :, 0:3], dirs[:, :, :], ALU.mult))
            s.step(v.tensor_reduce(gq[:, c, :], gp[:, c], AX.X, ALU.add))
            s.step(v.tensor_tensor(gq[:, c, :], gq[:, c, :], hsc[:, :], ALU.mult))
            s.step(v.tensor_tensor(gp[:, c], dirs[:, :, :],
                                   gq[:, c, :].unsqueeze(2).to_broadcast([P, 8, 3]), ALU.mult))
            s.step(v.tensor_scalar(wqkv0[:, c, 0:D], wqkv0[:, c, 0:D], att0.dim ** -0.5, None, ALU.mult))
            s.step(v.tensor_tensor(wq[:, c, :, 0:3], wq[:, c, :, 0:3], gp[:, c], ALU.add))
        s.step(v.tensor_scalar(wq1[:, :, :], wq1[:, :, :], att1.dim ** -0.5, None, ALU.mult))
        s.step(v.tensor_copy(ones2[:, :], onesr[0:2, 0:P]))
        v.tensor_copy(rc[:, 0:1], onesr[:, 0:1]).then_inc(ready, 1)

        s = None

        def transposed(name):
            dve.wait_ge(sg(name + "_full"), 2)
            v.tensor_copy(tt[:, 1, :], ps[1][:, :]).then_inc(sg(name + "_ev"), 1)

        def qkv(a):
            for n in range(4):
                dve.wait_ge(sg(a.name + "_hi"), n + 1)
                w = ("q", "k")[n // 2]
                v.tensor_tensor(hl[w + "_lo"][:, n % 2, :], ps[2 + n][:, :], hl[w + "_hi"][:, n % 2, :]
                                .bitcast(fp32), ALU.subtract).then_inc(sg(a.name + "_lo"), 1)

        def attention(a, s):
            n_ = a.name

            def maximum(u):
                g, n = u // a.group, u % a.group
                dve.wait_ge(sg(n_ + "_s_full"), u + 1)
                if n == 0 and g >= 2:
                    dve.wait_ge(sg(n_ + "_mt_full"), g - 1)
                v.tensor_reduce(mx[:, g % 2, :, n], ps[u % 2][:, :].rearrange("p (b k) -> p b k", b=2),
                                AX.X, ALU.max, negate=True).then_inc(sg(n_ + "_max"), 1)

            def rows(g):
                dve.wait_ge(sg(n_ + "_mt_full"), g + 1)
                if g >= 2:
                    dve.wait_ge(sg(f"{n_}_rows_in{g % 2}"), 16 * 2 * a.lanes * (g // 2))
                hi, lo = (rows_hl[0:a.group, g % 2, i, :] for i in range(2))
                s.step(v.tensor_copy(hi, ps[6][0:a.group, 0:T]))
                v.tensor_tensor(lo, ps[6][0:a.group, 0:T], hi.bitcast(fp32), ALU.subtract)\
                    .then_inc(sg(n_ + "_rows"), 1)

            def normalise(k):
                dve.wait_ge(sg(n_ + "_o_full"), k + 1)
                h = k * a.quad % a.heads
                bb = k * a.quad // a.heads
                o = ps[7][:, 0:2 * P].rearrange("p (b h w) -> p b h w", b=2, h=a.quad)
                s.step(v.reciprocal(rc[:, 0:2 * a.quad].rearrange("p (b h) -> p b h", b=2), o[:, :, :, a.dim]))
                v.tensor_tensor(ob[:, 2 * bb:2 * bb + 2, h * a.dim:(h + a.quad) * a.dim]
                                .rearrange("p b (h d) -> p b h d", h=a.quad), o[:, :, :, 0:a.dim],
                                rc[:, 0:2 * a.quad].rearrange("p (b h) -> p b h", b=2).unsqueeze(3)
                                .to_broadcast([P, 2, a.quad, a.dim]), ALU.mult).then_inc(sg(n_ + "_norm"), 1)

            for p in range(a.groups + 2):
                gs, gt = p, p - 2
                for n in range(a.group):
                    if gs < a.groups:
                        maximum(gs * a.group + n)
                    u = gt * a.group + n
                    if u >= 2 and a.quad_end(u - 2):
                        normalise((u - 2) // a.quad)
                if gs < a.groups:
                    rows(gs)
            normalise(a.units // a.quad - 1)

        def layernorm(s, src, dst):
            for tb in range(NTB):
                s.mark(v.bn_stats(stats[:, tb, :], src[:, tb, :]))
            s.sync()
            for tb in range(NTB):
                s.mark(v.bn_aggr(mv[:, tb, :], stats[:, tb, :]))
            s.sync()
            x_, y_, a_ = (r[:, 0:NTB] for r in rs)
            s.step(v.tensor_scalar(x_, mv[:, :, 1], LN_EPS, None, ALU.add))
            rsqrt_steps(s, v, x_, y_, a_)
            for tb in range(NTB):
                last = s.mark(v.tensor_scalar(dst[:, tb, :], src[:, tb, :], mv[:, tb, 0:1], rs[1][:, tb:tb + 1],
                                              ALU.subtract, ALU.mult))
            s.sync()

        def add_projection(s, name, resid, dst):
            for n in range(2):
                dve.wait_ge(sg(name + "_full"), n + 1)
                s.mark(v.tensor_tensor(dst[:, 2 * n:2 * n + 2, :],
                                       ps[2 + n][:, :].rearrange("p (b d) -> p b d", b=2),
                                       resid[:, 2 * n:2 * n + 2, :], ALU.add))
            s.sync()

        def signal(s, name):
            s.sync()
            dve.sem_inc(sg(name), 1)

        def experts(s):
            for e in range(E_IT):
                for bb in range(2):
                    dve.wait_ge(sg("down_full"), 2 * e + bb + 1)
                    s.mark(v.tensor_tensor(yb[:, 2 * bb + e, :], ps[(0, 1, 6, 7)[2 * e + bb]][:, 0:D], b2b[:, e, :],
                                           ALU.add))
            s.sync()
            s.step(v.tensor_tensor(yb[:, :, :], yb[:, :, :], hb[:, :, :], ALU.add))

        def linear_attention(s):
            dve.wait_ge(sg("g_z_full"), 1)
            s.step(v.tensor_scalar(gz[:, :], ps[5][:, :], bgk[:, 0:1], None, ALU.add))
            s.mark(v.tensor_scalar(gm[:, :], gz[:, :], 0.0, None, ALU.min))
            v.scalar_tensor_tensor(ge[:, :], gz[:, :], -1.0, gz[:, :], ALU.mult, ALU.min).then_inc(sg("g_z"), 1)
            dve.wait_ge(sg("g_a"), 2)
            s.step(v.tensor_tensor(gm[:, :], gm[:, :], ge[:, :], ALU.subtract))
            s.step(v.tensor_scalar(gm[:, :], gm[:, :], 1 / 16.0, None, ALU.mult))
            for bb in range(2):
                s.mark(v.tensor_tensor_scan(gG[:, bb * T:(bb + 1) * T], onesr[:, :], gm[:, bb * T:(bb + 1) * T],
                                            0.0, ALU.mult, ALU.add))
            s.sync()
            mid = [gG[:, tb * P + P // 2 - 1:tb * P + P // 2] for tb in range(NTB)]
            for tb in range(NTB):
                s.mark(v.tensor_scalar(gz[:, tb * P:(tb + 1) * P], gG[:, tb * P:(tb + 1) * P], mid[tb], None,
                                       ALU.subtract))
            for bb in range(2):
                s.mark(v.tensor_tensor(dr[:, bb:bb + 1], mid[2 * bb + 1], mid[2 * bb], ALU.subtract))
            s.sync()
            signal(s, "g_d")
            dve.wait_ge(sg("g_qk_full"), 2)
            dve.wait_ge(sg("g_a"), 4)
            v.scalar_tensor_tensor(qs[:, :], ps[2][:, :], DK ** -0.5, ge[:, :], ALU.mult, ALU.mult)\
                .then_inc(sg("g_qk"), 1)
            v.tensor_tensor(ks[:, :], ps[3][:, :], gm[:, :], ALU.mult).then_inc(sg("g_qk"), 1)
            dve.wait_ge(sg("g_a"), 5)
            s.step(v.tensor_scalar(yb[:, :, :], yb[:, :, :], 1.0, None, ALU.add))
            s.step(v.reciprocal(yb[:, :, :], yb[:, :, :]))
            s.step(v.tensor_tensor(gb[:, :, :], gb[:, :, :], yb[:, :, :], ALU.mult))
            s.step(v.tensor_tensor(gb[:, :, :].rearrange("p t (h d) -> p (t h) d", d=DV),
                                   gb[:, :, :].rearrange("p t (h d) -> p (t h) d", d=DV),
                                   gwb[:, :].unsqueeze(1).to_broadcast([P, NTB * NHG, DV]), ALU.mult))
            for h in range(NHG):
                dve.wait_ge(sg("g_at_full"), h + 1)
                v.tensor_tensor(atm[:, h, :, :], ps[2 + h][:, :].rearrange("p (b t) -> p b t", b=NTB),
                                mask_g[:, :].unsqueeze(1).to_broadcast([P, NTB, P]), ALU.mult)\
                    .then_inc(sg("g_at"), 1)
            dve.wait_ge(sg("g_state_full"), 1)
            dve.wait_ge(sg("g_dr"), 1)
            for bb in range(2):
                for h in range(NHG):
                    r = slice(h * DK, (h + 1) * DK)
                    s.mark(v.tensor_scalar(sd[r, bb, h * DV:(h + 1) * DV],
                                           ps[7][r, bb * D + h * DV:bb * D + (h + 1) * DV],
                                           dr[r, bb:bb + 1], None, ALU.mult))
            s.sync()
            signal(s, "g_state")
            dve.wait_ge(sg("g_sq"), NTB)
            x_, y_, a_ = (r[:, :] for r in rs)
            s.step(v.tensor_reduce(x_, hb[:, :, :].rearrange("p t (h d) -> p (t h) d", d=DV), AX.X, ALU.add))
            s.step(v.tensor_scalar(x_, x_, 1.0 / DV, LN_EPS, ALU.mult, ALU.add))
            rsqrt_steps(s, v, x_, y_, a_)
            for tb in range(NTB):
                shape = [P, NHG, DV]
                s.mark(v.tensor_tensor(ob[:, tb, :].rearrange("p (h d) -> p h d", d=DV),
                                       ps[(0, 1, 6, 7)[tb]][:, 0:D].rearrange("p (h d) -> p h d", d=DV),
                                       rs[1][:, tb * NHG:(tb + 1) * NHG].unsqueeze(2).to_broadcast(shape),
                                       ALU.mult))
            s.sync()
            s.step(v.tensor_tensor(ob[:, :, :], ob[:, :, :], gb[:, :, :], ALU.mult))
            signal(s, "g_o")

        with dve.Fori(0, PAIRS) as j:
            s = Counted(dve, sg("dve_steps"))
            transposed("h_t")
            qkv(att0)
            attention(att0, s)
            transposed("p0_t")
            add_projection(s, "p0", ha, yb)
            layernorm(s, yb, hb)
            layernorm(s, hb, yb)
            s.step(v.tensor_tensor(yb[:, :, :], yb[:, :, :], lng[:, :].unsqueeze(1).to_broadcast([P, NTB, D]),
                                   ALU.mult))
            s.step(v.tensor_tensor(yb[:, :, :], yb[:, :, :], lnb[:, :].unsqueeze(1).to_broadcast([P, NTB, D]),
                                   ALU.add))
            signal(s, "xn")
            transposed("xn_t")
            qkv(att1)
            attention(att1, s)
            transposed("p1_t")
            add_projection(s, "p1", hb, yb)
            signal(s, "xf")
            transposed("xf_t")
            experts(s)
            layernorm(s, yb, ha)
            signal(s, "h2")
            transposed("h2_t")
            linear_attention(s)
            transposed("p2_t")
            add_projection(s, "p2", ha, yb)
            layernorm(s, yb, hb)
            signal(s, "h3")
            dve.wait_ge(done, 2)
            dve.sem_clear(done)
            for name in sg.all:
                dve.sem_clear(sg.all[name])
            for k in go:
                dve.sem_inc(go[k], 1)
    block_ctx.close()


def expert_mixture(nc, ctx, io, x3, out, ident):
    NTB = B * T // P
    E, F = 8, 1024
    FT = F // P
    TG, NG = 512, B * T // 512
    TBG = TG // P

    def sb(name, shape, dt=fp32):
        return ctx.enter_context(nc.sbuf_tensor(name, shape, dt))

    sg = Signals(nc, ctx, "x")
    acc = sb("x_acc", [P, NTB, D])
    xT = sb("x_T", [P, DC, NTB * P])
    w1 = sb("x_w1", [P, 2, DC, F])
    w2 = sb("x_w2", [P, 2, FT, D])
    hid = sb("x_hid", [P, 2, FT, TG])
    wg, bg = sb("x_wg", [P, DC, E]), sb("x_bg", [P, E])
    b1r, b1c, b2 = sb("x_b1r", [E * FT, P]), sb("x_b1c", [P, E * FT]), sb("x_b2", [E, D])
    rank = sb("x_rank", [P, E])
    lo, pr, eq, oh1, oh2, gate = (sb(f"x_{n}", [P, NTB, E]) for n in ("lo", "pr", "eq", "oh1", "oh2", "gate"))
    m1, m2, ix, dd = (sb(f"x_{n}", [P, NTB]) for n in ("m1", "m2", "ix", "dd"))
    gT = sb("x_gT", [E, NTB * P])
    stats, mv = sb("x_stats", [P, NTB, 6]), sb("x_mv", [P, NTB, 2])
    rs = [sb(f"x_rs{i}", [P, NTB]) for i in range(3)]
    ps = [ctx.enter_context(nc.psum_tensor(f"x_ps{i}", [P, 512], fp32)) for i in range(8)]

    with nc.Block() as block:
        @block.sync
        def _(sp):
            sp.dma_start(acc[:, :, :], x3.rearrange("b (k p) d -> p (b k) d", p=P)).then_inc(sg("x_in"), 16)
            sp.dma_start(wg[:, :, :], io["L1_ffn_Wg"].rearrange("(c p) e -> p c e", p=P)).then_inc(sg("small"), 16)
            sp.dma_start(bg[:, :], io["L1_ffn_bg"].partition_broadcast(P)).then_inc(sg("small"), 16)
            sp.dma_start(b1r[:, :], io["L1_ffn_b1"].rearrange("e (c p) -> (e c) p", p=P)).then_inc(sg("small"), 16)
            sp.dma_start(b2[:, :], io["L1_ffn_b2"]).then_inc(sg("small"), 16)
            for e in range(E):
                if e >= 2:
                    sp.wait_ge(sg("down_full"), (e - 1) * NTB)
                sp.dma_start(w1[:, e % 2, :, :], io["L1_ffn_W1"][e].rearrange("(c p) n -> p c n", p=P))\
                    .then_inc(sg(f"w_in{e % 2}"), 16)
                sp.dma_start(w2[:, e % 2, :, :], io["L1_ffn_W2"][e].rearrange("(c p) n -> p c n", p=P))\
                    .then_inc(sg(f"w_in{e % 2}"), 16)
            for n in range(4):
                sp.wait_ge(sg("normed"), 4 * (n + 1))
                sp.dma_start(out[2 * n:2 * n + 2].rearrange("b (k p) d -> p (b k) d", p=P),
                             acc[:, 4 * n:4 * n + 4, :]).then_inc(sg("stored"), 16)
            sp.wait_ge(sg("stored"), 64)

        @block.gpsimd
        def _(pool):
            nc.gpsimd.iota(rank[:, :], pattern=[[1, E]], base=-E, channel_multiplier=0,
                           allow_small_or_imprecise_dtypes=True).then_inc(sg("rank"), 1)

        @block.tensor
        def _(pe):
            mm = nc.tensor.matmul
            pe.wait_ge(sg("x_in"), 16)
            for n in range(DC * NG):
                for k in range(TBG):
                    tb = n // DC * TBG + k
                    last = nc.tensor.transpose(ps[n][:, k * P:(k + 1) * P],
                                               acc[:, tb, (n % DC) * P:(n % DC + 1) * P], ident[:, :])
                last.then_inc(sg("xT_full"), 1)
            pe.wait_ge(sg("small"), 64)
            pe.wait_ge(sg("xT"), DC * NG)
            for tb in range(NTB):
                for c in range(DC):
                    last = mm(ps[0][:, tb * E:(tb + 1) * E], xT[:, c, tb * P:(tb + 1) * P], wg[:, c, :],
                              start=c == 0, stop=c == DC - 1)
            last.then_inc(sg("logits_full"), 1)
            nc.tensor.transpose(ps[1][:, 0:E * FT], b1r[:, :], ident[0:E * FT, 0:E * FT]).then_inc(sg("b1_full"), 1)
            n = d = 0
            for e in range(E):
                pe.wait_ge(sg(f"w_in{e % 2}"), 32 * (e // 2 + 1))
                for g in range(NG):
                    for f in range(FT):
                        if n >= 2:
                            pe.wait_ge(sg("up"), n - 1)
                        elif n == 0:
                            pe.wait_ge(sg("b1"), 1)
                        for c in range(DC):
                            last = mm(ps[2 + n % 2][:, :], w1[:, e % 2, c, f * P:(f + 1) * P],
                                      xT[:, c, g * TG:(g + 1) * TG], start=c == 0, stop=c == DC - 1)
                        last.then_inc(sg("up_full"), 1)
                        n += 1
                    pe.wait_ge(sg("up"), n)
                    for k in range(TBG):
                        if d >= 2:
                            pe.wait_ge(sg("down"), d - 1)
                        for f in range(FT):
                            last = mm(ps[4 + d % 2][:, 0:D], hid[:, (n // FT - 1) % 2, f, k * P:(k + 1) * P],
                                      w2[:, e % 2, f, :], start=f == 0, stop=f == FT - 1)
                        last.then_inc(sg("down_full"), 1)
                        d += 1
                    if e == 0 and g == 0:
                        pe.wait_ge(sg("gate"), 1)
                        for q in range(NG):
                            for k in range(TBG):
                                tb = q * TBG + k
                                last = nc.tensor.transpose(ps[6 + q % 2][0:E, k * P:(k + 1) * P], gate[:, tb, :],
                                                           ident[:, :])
                            last.then_inc(sg("gT_full"), 1)
                            pe.wait_ge(sg("gT"), q + 1)
                            for k in range(TBG):
                                last = mm(ps[k % 2][:, (k // 2) * D:(k // 2 + 1) * D],
                                          gT[:, (q * TBG + k) * P:(q * TBG + k + 1) * P], b2[:, :],
                                          start=True, stop=True)
                            last.then_inc(sg("bias_full"), 1)
                            pe.wait_ge(sg("bias"), q + 1)

        @block.scalar
        def _(act):
            sc = nc.scalar
            for n in range(0, DC * NG, 2):
                act.wait_ge(sg("xT_full"), n + 1)
                sc.copy(xT[:, n % DC, n // DC * TG:(n // DC + 1) * TG], ps[n][:, :]).then_inc(sg("xT"), 1)
            act.wait_ge(sg("b1_full"), 1)
            sc.copy(b1c[:, :], ps[1][:, 0:E * FT]).then_inc(sg("b1"), 1)
            act.wait_ge(sg("shifted"), 1)
            sc.activation(pr[:, :, :], lo[:, :, :], ACT.Exp).then_inc(sg("exps"), 1)
            act.wait_ge(sg("two"), 1)
            sc.activation(dd[:, :], m2[:, :], ACT.Exp).then_inc(sg("exps"), 1)
            act.wait_ge(sg("b1"), 1)
            for n in range(E * NG * FT):
                e, g, f = n // (NG * FT), n // FT, n % FT
                act.wait_ge(sg("up_full"), n + 1)
                if f == 0 and g >= 2:
                    act.wait_ge(sg("down_full"), (g - 1) * TBG)
                sc.activation(hid[:, g % 2, f, :], ps[2 + n % 2][:, :], ACT.Relu,
                              bias=b1c[:, e * FT + f:e * FT + f + 1]).then_inc(sg("up"), 1)

        @block.vector
        def _(dve):
            v = nc.vector
            s = Counted(dve, sg("dve_steps"))
            for n in range(1, DC * NG, 2):
                dve.wait_ge(sg("xT_full"), n + 1)
                v.tensor_copy(xT[:, n % DC, n // DC * TG:(n // DC + 1) * TG], ps[n][:, :]).then_inc(sg("xT"), 1)
            shape = [P, NTB, E]

            def over(ap):
                return ap.unsqueeze(2).to_broadcast(shape)

            dve.wait_ge(sg("small"), 64)
            dve.wait_ge(sg("rank"), 1)
            dve.wait_ge(sg("logits_full"), 1)
            s.step(v.tensor_tensor(lo[:, :, :], ps[0][:, 0:NTB * E].rearrange("p (t e) -> p t e", e=E),
                                   bg[:, :].unsqueeze(1).to_broadcast(shape), ALU.add))
            s.step(v.tensor_reduce(m1[:, :], lo[:, :, :], AX.X, ALU.max))
            v.tensor_tensor(lo[:, :, :], lo[:, :, :], over(m1[:, :]), ALU.subtract).then_inc(sg("shifted"), 1)
            dve.wait_ge(sg("exps"), 1)
            s.step(v.tensor_reduce(m1[:, :], pr[:, :, :], AX.X, ALU.add))
            s.step(v.reciprocal(m1[:, :], m1[:, :]))
            s.step(v.tensor_tensor(pr[:, :, :], pr[:, :, :], over(m1[:, :]), ALU.mult))
            for m, oh in ((m1, oh1), (m2, oh2)):
                s.step(v.tensor_reduce(m[:, :], pr[:, :, :], AX.X, ALU.max))
                s.step(v.tensor_tensor(eq[:, :, :], pr[:, :, :], over(m[:, :]), ALU.is_equal))
                s.step(v.tensor_tensor(eq[:, :, :], eq[:, :, :], rank[:, :].unsqueeze(1).to_broadcast(shape),
                                       ALU.mult))
                s.step(v.tensor_reduce(ix[:, :], eq[:, :, :], AX.X, ALU.min))
                s.step(v.tensor_tensor(oh[:, :, :], rank[:, :].unsqueeze(1).to_broadcast(shape), over(ix[:, :]),
                                       ALU.is_equal))
                s.step(v.scalar_tensor_tensor(pr[:, :, :].rearrange("p t e -> p (t e)"),
                                              oh[:, :, :].rearrange("p t e -> p (t e)"), -4.0,
                                              pr[:, :, :].rearrange("p t e -> p (t e)"), ALU.mult, ALU.add))
            v.tensor_tensor(m2[:, :], m2[:, :], m1[:, :], ALU.subtract).then_inc(sg("two"), 1)
            dve.wait_ge(sg("exps"), 2)
            s.step(v.tensor_scalar(m1[:, :], dd[:, :], 1.0, None, ALU.add))
            s.step(v.reciprocal(m1[:, :], m1[:, :]))
            s.step(v.tensor_tensor(dd[:, :], dd[:, :], m1[:, :], ALU.mult))
            s.step(v.tensor_tensor(gate[:, :, :], oh1[:, :, :], over(m1[:, :]), ALU.mult))
            s.step(v.tensor_tensor(oh2[:, :, :], oh2[:, :, :], over(dd[:, :]), ALU.mult))
            v.tensor_tensor(gate[:, :, :], gate[:, :, :], oh2[:, :, :], ALU.add).then_inc(sg("gate"), 1)
            dve.wait_ge(sg("gate"), 1)
            d = 0
            for g in range(E * NG):
                for k in range(TBG):
                    e, tb = g // NG, g % NG * TBG + k
                    dve.wait_ge(sg("down_full"), d + 1)
                    if e:
                        dve.wait_ge(sg("down"), d - NTB + 1)
                    v.scalar_tensor_tensor(acc[:, tb, :], ps[4 + d % 2][:, 0:D], gate[:, tb, e:e + 1],
                                           acc[:, tb, :], ALU.mult, ALU.add).then_inc(sg("down"), 1)
                    d += 1
                if g == 0:
                    for q in range(NG):
                        dve.wait_ge(sg("gT_full"), q + 1)
                        v.tensor_copy(gT[:, q * TG:(q + 1) * TG], ps[6 + q % 2][0:E, :]).then_inc(sg("gT"), 1)
                        dve.wait_ge(sg("bias_full"), q + 1)
                        dve.wait_ge(sg("down"), TBG)
                        for k in range(TBG):
                            tb = q * TBG + k
                            last = s.mark(v.tensor_tensor(acc[:, tb, :], acc[:, tb, :],
                                                          ps[k % 2][:, (k // 2) * D:(k // 2 + 1) * D], ALU.add))
                        s.sync()
                        dve.sem_inc(sg("bias"), 1)
            dve.wait_ge(sg("down"), E * NTB)
            for q in range(NG):
                for tb in range(q * TBG, (q + 1) * TBG):
                    s.mark(v.bn_stats(stats[:, tb, :], acc[:, tb, :]))
            s.sync()
            for tb in range(NTB):
                s.mark(v.bn_aggr(mv[:, tb, :], stats[:, tb, :]))
            s.sync()
            x_, y_, a_ = (r[:, :] for r in rs)
            s.step(v.tensor_scalar(x_, mv[:, :, 1], LN_EPS, None, ALU.add))
            rsqrt_steps(s, v, x_, y_, a_)
            for tb in range(NTB):
                v.tensor_scalar(acc[:, tb, :], acc[:, tb, :], mv[:, tb, 0:1], rs[1][:, tb:tb + 1],
                                ALU.subtract, ALU.mult).then_inc(sg("normed"), 1)


def two_layers(nc, io, out):
    h0 = nc.dram_tensor("h0", (B, T, D), fp32).ap()
    x3 = nc.dram_tensor("x3", (B, T, D), fp32).ap()
    with ExitStack() as whole:
        ident = whole.enter_context(nc.sbuf_tensor("ident", [P, P], fp32))
        with ExitStack() as ctx:
            s4_tokens(nc, ctx, io["x"], io["L0_tok_log_dt"], io["L0_tok_inv_A_real"], io["L0_tok_A_imag"],
                      io["L0_tok_B_ri"], h0, ident)
        with ExitStack() as ctx:
            main_loop(nc, ctx, io, h0, x3, ident)
        with ExitStack() as ctx:
            expert_mixture(nc, ctx, io, x3, out, ident)


_UNUSED = ("L0_ffn_gate_w",)


def kernel(**inputs):
    import concourse.bacc as bacc
    from concourse.bass_utils import run_bass_kernel_spmd

    nc = bacc.Bacc("TRN2", target_bir_lowering=False, num_devices=1)
    arrays, io = {}, {}
    for name, value in inputs.items():
        if name in _UNUSED:
            continue
        a = np.ascontiguousarray(value)
        if name == "L0_tok_log_dt":
            a = np.ascontiguousarray(a.reshape(T // P, P).T)
        arrays[f"in_{name}"] = a
        io[name] = nc.dram_tensor(f"in_{name}", a.shape, mybir.dt.from_np(a.dtype), kind="ExternalInput").ap()
    out = nc.dram_tensor("out_h", (B, T, D), fp32, kind="ExternalOutput").ap()
    two_layers(nc, io, out)
    return run_bass_kernel_spmd(nc, [arrays], core_ids=[0]).results[0]["out_h"]
```

```python
import numpy as np
from contextlib import ExitStack
import concourse.bass as bass
from concourse import mybir

fp32 = mybir.dt.float32
f32r = mybir.dt.float32r
bf16 = mybir.dt.bfloat16
i32 = mybir.dt.int32
u32 = mybir.dt.uint32
ALU = mybir.AluOpType
ACT = mybir.ActivationFunctionType
AX = mybir.AxisListType

P = 128
B, T, D = 8, 256, 256
N_STATE = 64
DC = D // P
LN_EPS = 1e-5
NEG = -1e30


class Counted:

    def __init__(self, eng, sem):
        self.eng, self.sem, self.n = eng, sem, 0

    def mark(self, ins):
        self.n += 1
        ins.then_inc(self.sem, 1)
        return ins

    def step(self, ins):
        self.mark(ins)
        self.eng.wait_ge(self.sem, self.n)

    def sync(self):
        if self.n:
            self.eng.wait_ge(self.sem, self.n)


def s4_tokens(nc, ctx, whole, x, log_dt, inv_a_real, a_imag, b_ri, h0, ident, xs):
    CH, HF, NB, NA = B, T // P, 64, 4
    HP, NG = P, 4
    GT = HP // NG
    M = CH * NA

    def sb(name, shape, dt=fp32):
        return ctx.enter_context(nc.sbuf_tensor(name, shape, dt))

    xin = sb("s4_x", [P, HF, CH, N_STATE, 2])
    bin_ = sb("s4_b", [P, HF, N_STATE, 2])
    ea = sb("s4_ea", [P, 2 + HF * N_STATE])
    ex = [sb(f"s4_ex{i}", [P, 2 + HF * N_STATE]) for i in range(3)]
    exi = sb("s4_exi", [P, 2 + HF * N_STATE], i32)
    aim = sb("s4_aim", [P, HF, N_STATE])
    q = [sb(f"s4_q{i}", [P, HF, N_STATE]) for i in range(5)]
    da = sb("s4_da", [P, 2, HF, N_STATE])
    cb = sb("s4_cb", [P, 2, CH, HF, N_STATE])
    ct = sb("s4_ct", [P, HF, CH, N_STATE])
    dat = sb("s4_dat", [P, 2, HP])
    cbt = sb("s4_cbt", [P, 2, CH, HP])
    pw = [sb(f"s4_pw{i}", [P, 2, GT, NB]) for i in range(2)]
    cs = [sb(f"s4_cs{i}", [P, 2, GT, NA, CH]) for i in range(2)]
    csn = [sb(f"s4_csn{i}", [P, GT, NA, CH]) for i in range(2)]
    dk = [sb(f"s4_dk{i}", [P, 2, GT]) for i in range(2)]
    dk2 = sb("s4_dk2", [P, GT])
    t1 = sb("s4_t1", [P, 2, GT, NB // 2])
    t2 = sb("s4_t2", [P, 2, GT, NB // 2])
    out = [sb(f"s4_out{i}", [M, GT, NB]) for i in range(4)]
    ps = [ctx.enter_context(nc.psum_tensor(f"s4_ps{i}", [P, 512], fp32)) for i in range(8)]

    def sem(n):
        return whole.enter_context(nc.semaphore(n))

    zero = sb("s4_zero", [P, D])
    loaded, zeroed = sem("s4_loaded"), sem("s4_zeroed")
    prepared, transposed, columns = sem("s4_prepared"), sem("s4_transposed"), sem("s4_columns")
    powers, negated = sem("s4_powers"), sem("s4_negated")
    bank_full, bank_free = sem("s4_bank_full"), sem("s4_bank_free")
    stored = [sem(f"s4_stored{i}") for i in range(4)]
    steps, asteps, constants = sem("s4_steps"), sem("s4_asteps"), sem("s4_constants")
    NLOAD = 6
    NT = 2 + 2 * CH
    TOK_BANK = 8
    BG = GT // TOK_BANK

    with nc.Block() as block:
        @block.sync
        def _(sp):
            sp.dma_start(ea[:, 0:HF], log_dt).then_inc(loaded, 16)
            sp.dma_start(ea[:, HF:].rearrange("p (f n) -> p f n", f=HF),
                         inv_a_real.rearrange("(f p) n -> p f n", p=P)).then_inc(loaded, 16)
            sp.dma_start(aim[:, :, :], a_imag.rearrange("(f p) n -> p f n", p=P)).then_inc(loaded, 16)
            sp.dma_start(bin_[:, :, :, :], b_ri.rearrange("(f p) n r -> p f n r", p=P)).then_inc(loaded, 16)
            for f in range(HF):
                sp.dma_start(xin[:, f].rearrange("p c n r -> p c (n r)"),
                             x[:, f * P:(f + 1) * P].rearrange("c p n r -> p c (n r)")).then_inc(loaded, 16)
            for g in range(NG):
                for f in range(HF):
                    n = HF * g + f
                    sp.wait_ge(bank_free, BG * (n + 1))
                    t0 = f * P + g * GT
                    for a in range(NA):
                        sp.dma_start(h0[:, t0:t0 + GT, a * NB:(a + 1) * NB],
                                     out[n % 4][a * CH:(a + 1) * CH, :, :]).then_inc(stored[n % 4], 16)
            for k in range(4):
                sp.wait_ge(stored[k], 16 * NA * NG * HF // 4)

        @block.gpsimd
        def _(pool):
            nc.gpsimd.memset(ident[:, :], 0.0).then_inc(constants, 1)
            pool.wait_ge(constants, 1)
            nc.gpsimd.affine_select(out=ident[:, :], in_=ident[:, :], compare_op=ALU.not_equal, fill=1.0,
                                    base=0, pattern=[[-1, P]], channel_multiplier=1).then_inc(constants, 1)
            nc.gpsimd.memset(zero[:, :], 0.0).then_inc(constants, 1)
            pool.wait_ge(constants, 3)
            rows = xs.shape[0] // P
            pool.dma_start(xs.rearrange("(p r) d -> p r d", p=P),
                           zero[:, :].unsqueeze(1).to_broadcast([P, rows, D])).then_inc(zeroed, 16)
            pool.wait_ge(zeroed, 16)

        @block.vector
        def _(dve):
            s = Counted(dve, steps)
            v = nc.vector
            dve.wait_ge(loaded, 16 * NLOAD)
            y, r, kf = ex
            s.step(v.tensor_scalar(y[:, :], ea[:, :], -87.0, 88.0, ALU.max, ALU.min))
            s.step(v.tensor_scalar(exi[:, :], y[:, :], 1.4426950408889634, None, ALU.mult))
            s.step(v.tensor_copy(kf[:, :], exi[:, :]))
            s.step(v.scalar_tensor_tensor(r[:, :], kf[:, :], -0.693359375, y[:, :], ALU.mult, ALU.add))
            s.step(v.scalar_tensor_tensor(r[:, :], kf[:, :], 2.12194440e-4, r[:, :], ALU.mult, ALU.add))
            s.step(v.tensor_scalar(y[:, :], r[:, :], 1 / 5040, None, ALU.mult))
            for c in (1 / 720, 1 / 120, 1 / 24, 1 / 6, 1 / 2, 1.0):
                s.step(v.scalar_tensor_tensor(y[:, :], y[:, :], c, r[:, :], ALU.add, ALU.mult))
            s.step(v.tensor_scalar(exi[:, :], kf[:, :], 127.0, float(1 << 23), ALU.add, ALU.mult))
            s.step(v.scalar_tensor_tensor(ea[:, :], y[:, :], 1.0, exi[:, :].bitcast(fp32), ALU.add, ALU.mult))
            a, b, m, dn, w = q
            for f in range(HF):
                s.mark(v.tensor_scalar(a[:, f, :], ea[:, HF + f * N_STATE:HF + (f + 1) * N_STATE],
                                       ea[:, f:f + 1], -0.5, ALU.mult, ALU.mult))
                s.mark(v.tensor_scalar(b[:, f, :], aim[:, f, :], ea[:, f:f + 1], 0.5, ALU.mult, ALU.mult))
            s.sync()
            s.mark(v.tensor_tensor(m[:, :, :], b[:, :, :], b[:, :, :], ALU.mult))
            s.step(v.tensor_scalar(dn[:, :, :], a[:, :, :], -1.0, 1.0, ALU.mult, ALU.add))
            s.mark(v.tensor_tensor(dn[:, :, :], dn[:, :, :], dn[:, :, :], ALU.mult))
            s.step(v.tensor_tensor(w[:, :, :], a[:, :, :], a[:, :, :], ALU.mult))
            s.mark(v.tensor_tensor(dn[:, :, :], dn[:, :, :], m[:, :, :], ALU.add))
            s.step(v.tensor_tensor(w[:, :, :], w[:, :, :], m[:, :, :], ALU.add))
            s.mark(v.reciprocal(dn[:, :, :], dn[:, :, :]))
            s.step(v.tensor_scalar(w[:, :, :], w[:, :, :], -1.0, 1.0, ALU.mult, ALU.add))
            s.mark(v.tensor_tensor(da[:, 0, :, :], w[:, :, :], dn[:, :, :], ALU.mult))
            s.mark(v.scalar_tensor_tensor(da[:, 1, :, :], b[:, :, :], 2.0, dn[:, :, :], ALU.mult, ALU.mult))
            xr, xi = xin[:, :, :, :, 0], xin[:, :, :, :, 1]
            shape = [P, HF, CH, N_STATE]
            br = bin_[:, :, :, 0].unsqueeze(2).to_broadcast(shape)
            bi = bin_[:, :, :, 1].unsqueeze(2).to_broadcast(shape)
            cbr = cb[:, 0].rearrange("p c f n -> p f c n")
            cbi = cb[:, 1].rearrange("p c f n -> p f c n")
            s.step(v.tensor_scalar(bin_[:, :, :, :], bin_[:, :, :, :], 2.0, None, ALU.mult))
            s.mark(v.tensor_tensor(cbr, xr, br, ALU.mult))
            s.step(v.tensor_tensor(ct[:, :, :, :], xi, bi, ALU.mult))
            s.step(v.tensor_tensor(cbr, cbr, ct[:, :, :, :], ALU.subtract))
            s.mark(v.tensor_tensor(cbi, xr, bi, ALU.mult))
            s.step(v.tensor_tensor(ct[:, :, :, :], xi, br, ALU.mult))
            v.tensor_tensor(cbi, cbi, ct[:, :, :, :], ALU.add).then_inc(prepared, 1)

            def cmul(dst, src, d, n):
                shp = [P, GT] + n
                dr, di = d[:, 0, :], d[:, 1, :]
                for _ in n:
                    dr, di = dr.unsqueeze(len(dr.shape)), di.unsqueeze(len(di.shape))
                dr, di = dr.to_broadcast(shp), di.to_broadcast(shp)
                size = 1
                for k in n:
                    size *= k
                u = [t1[:, i, :, 0:size] for i in range(2)]
                w = [t2[:, i, :, 0:size] for i in range(2)]
                if len(n) > 1:
                    u = [z.rearrange("p t (a c) -> p t a c", a=n[0]) for z in u]
                    w = [z.rearrange("p t (a c) -> p t a c", a=n[0]) for z in w]
                s.mark(v.tensor_tensor(u[0], src[0], dr, ALU.mult))
                s.mark(v.tensor_tensor(w[0], src[1], di, ALU.mult))
                s.mark(v.tensor_tensor(u[1], src[0], di, ALU.mult))
                s.step(v.tensor_tensor(w[1], src[1], dr, ALU.mult))
                s.mark(v.tensor_tensor(dst[0], u[0], w[0], ALU.subtract))
                s.step(v.tensor_tensor(dst[1], u[1], w[1], ALU.add))

            dve.wait_ge(columns, 5)
            for g in range(NG):
                pg, cg = pw[g % 2], cs[g % 2]
                tok = slice(g * GT, (g + 1) * GT)
                if g >= 2:
                    dve.wait_ge(bank_full, HF * BG * (g - 1))
                    dve.wait_ge(negated, g - 1)
                s.mark(v.memset(pg[:, 0, :, 0:1], 1.0))
                s.mark(v.memset(pg[:, 1, :, 0:1], 0.0))
                s.step(v.tensor_copy(dk[0][:, :, :], dat[:, :, tok]))
                for k in range(8):
                    cur, nxt = dk[k % 2], dk[(k + 1) % 2]
                    if k < 6:
                        n = 1 << k
                        cmul([pg[:, i, :, n:2 * n] for i in range(2)], [pg[:, i, :, 0:n] for i in range(2)],
                             cur, [n])
                    elif k == 6:
                        for i in range(2):
                            s.step(v.tensor_copy(cg[:, i, :, 0, :], cbt[:, i, :, tok].rearrange("p c t -> p t c")))
                        cmul([cg[:, i, :, 1, :] for i in range(2)], [cg[:, i, :, 0, :] for i in range(2)],
                             cur, [CH])
                    else:
                        cmul([cg[:, i, :, 2:4, :] for i in range(2)], [cg[:, i, :, 0:2, :] for i in range(2)],
                             cur, [2, CH])
                    if k < 7:
                        s.mark(v.tensor_tensor(dk2[:, :], cur[:, 1, :], cur[:, 1, :], ALU.mult))
                        s.step(v.tensor_tensor(nxt[:, 0, :], cur[:, 0, :], cur[:, 0, :], ALU.mult))
                        s.mark(v.tensor_tensor(nxt[:, 0, :], nxt[:, 0, :], dk2[:, :], ALU.subtract))
                        s.step(v.scalar_tensor_tensor(nxt[:, 1, :], cur[:, 0, :], 2.0, cur[:, 1, :],
                                                      ALU.mult, ALU.mult))
                s.sync()
                v.memset(dk2[:, 0:1], 0.0).then_inc(powers, 1)

        @block.scalar
        def _(act):
            for k in range(5):
                act.wait_ge(transposed, k + 1)
                for i in range(4 if k < 4 else 2):
                    n = 4 * k + i
                    dst = cbt[:, n // CH, n % CH, :] if n < 2 * CH else dat[:, n - 2 * CH, :]
                    last = nc.scalar.copy(dst, ps[k][:, i * P:(i + 1) * P])
                last.then_inc(columns, 1)

            def negate(g):
                act.wait_ge(powers, g + 1)
                if g >= 2:
                    act.wait_ge(bank_full, HF * BG * (g - 1))
                nc.scalar.mul(csn[g % 2][:, :, :, :], cs[g % 2][:, 1], -1.0).then_inc(negated, 1)

            negate(0)
            n = 0
            for g in range(NG):
                if g + 1 < NG:
                    negate(g + 1)
                for f in range(HF):
                    m = HF * g + f
                    if m >= 4:
                        act.wait_ge(stored[m % 4], 16 * NA * (m // 4))
                    for k in range(BG):
                        act.wait_ge(bank_full, n + 1)
                        nc.scalar.copy(out[m % 4][:, k * TOK_BANK:(k + 1) * TOK_BANK, :],
                                       ps[n % 8][0:M, :].rearrange("p (t b) -> p t b", b=NB)).then_inc(bank_free, 1)
                        n += 1

        @block.tensor
        def _(pe):
            pe.wait_ge(prepared, 1)
            pe.wait_ge(constants, 2)
            for n in range(NT):
                src = cb[:, n // CH, n % CH] if n < 2 * CH else da[:, n - 2 * CH]
                last = nc.tensor.transpose(ps[n // 4][:, (n % 4) * P:(n % 4 + 1) * P],
                                           src.rearrange("p f n -> p (f n)"), ident[:, :])
                if n % 4 == 3 or n == NT - 1:
                    last.then_inc(transposed, 1)
            n = 0
            pe.wait_ge(columns, 5)
            for g in range(NG):
                pe.wait_ge(negated, g + 1)
                for f in range(HF):
                    rows = slice(64 * f, 64 * f + 64)
                    for k in range(BG):
                        if n >= 8:
                            pe.wait_ge(bank_free, n - 7)
                        for i in range(TOK_BANK):
                            t = k * TOK_BANK + i
                            o = ps[n % 8][0:M, i * NB:(i + 1) * NB]
                            nc.tensor.matmul(o, cs[g % 2][rows, 0, t].rearrange("p a c -> p (a c)"),
                                             pw[g % 2][rows, 0, t, :], start=True, stop=False)
                            last = nc.tensor.matmul(o, csn[g % 2][rows, t].rearrange("p a c -> p (a c)"),
                                                    pw[g % 2][rows, 1, t, :], start=False, stop=True)
                        last.then_inc(bank_full, 1)
                        n += 1


class Signals:

    def __init__(self, nc, ctx, prefix):
        self.nc, self.ctx, self.prefix, self.all = nc, ctx, prefix, {}

    def __call__(self, name):
        if name not in self.all:
            self.all[name] = self.ctx.enter_context(self.nc.semaphore(f"{self.prefix}_{name}"))
        return self.all[name]

    def runs(self):
        numbers = sorted(x.num for x in self.all.values())
        starts = [n for n in numbers if n - 1 not in numbers]
        ends = [n + 1 for n in numbers if n + 1 not in numbers]
        return [range(a, b) for a, b in zip(starts, ends)]


def rsqrt_steps(s, v, x, y, a):
    s.step(v.tensor_scalar(y.bitcast(i32), x.bitcast(i32), 1, None, ALU.logical_shift_right))
    s.step(v.tensor_scalar(y.bitcast(i32), y.bitcast(i32), -1.0, float(0x5F3759DF), ALU.mult, ALU.add))
    for _ in range(3):
        s.step(v.scalar_tensor_tensor(a, y, -0.5, y, ALU.mult, ALU.mult))
        s.step(v.tensor_tensor(a, a, x, ALU.mult))
        s.step(v.scalar_tensor_tensor(y, a, 1.5, y, ALU.add, ALU.mult))


class Attention:

    RING = 4

    def __init__(self, name, heads, dim, causal):
        self.name, self.heads, self.dim, self.causal = name, heads, dim, causal
        self.rows = 4 * dim
        self.lanes = P // (2 * self.rows) or 1
        self.slots = 4
        self.group = self.lanes * self.slots
        self.per_batch = heads // self.group
        self.groups = 2 * self.per_batch
        self.vw = 32 if dim < 32 else 64
        self.quad = P // self.vw
        self.units = self.groups * self.group

    def lane_slot(self, n):
        return n // self.slots, n % self.slots

    def due(self, u, lag):
        end = u - lag
        return [end // self.quad] if 0 <= end < self.units and end % self.quad == self.quad - 1 else []


AV_LAG = 2
OUT_LAG = AV_LAG + 2
NORM_LAG = OUT_LAG + 1
PT_RING = 8


def main_loop(nc, ctx, whole, io, h0, x3, ident):
    NTB = 4
    TOK = NTB * P
    PAIRS = B // 2
    F = 1024
    FT = F // P
    E_IT = 2
    NHG, DK, DV = 4, 32, 64
    att0 = Attention("a0", 8, 32, True)
    att1 = Attention("a1", 32, 8, False)

    def sb(name, shape, dt=fp32, c=ctx):
        return c.enter_context(nc.sbuf_tensor(name, shape, dt))

    def dram(name, shape):
        return nc.dram_tensor(name, shape, fp32).ap()

    wqkv0 = sb("wqkv0", [P, DC, 3 * D])
    wout0 = sb("wout0", [P, DC, D])
    wq1, wk1, wv1, wo1 = (sb(n, [P, DC, D]) for n in ("wq1", "wk1", "wv1", "wo1"))
    gwq, gwk = sb("gwq", [P, DC, P]), sb("gwk", [P, DC, P])
    gwvg = sb("gwvg", [P, DC, 2 * D])
    gwgk1, gwgk2 = sb("gwgk1", [P, DC, 16]), sb("gwgk2", [16, P])
    gwo = sb("gwo", [P, DC, D])
    bgk = sb("bgk", [P, 1])
    gwb = sb("gwb", [P, DV])
    lng, lnb = sb("lng", [P, D]), sb("lnb", [P, D])
    dirs, hsc = sb("dirs", [P, 8, 3]), sb("hsc", [P, 8])
    gp, gq = sb("gp", [P, DC, 8, 3]), sb("gq", [P, DC, 8])
    identb = sb("identb", [P, P], bf16)
    mask_s, mask_t = sb("mask_s", [P, 3 * P], bf16), sb("mask_t", [P, 3 * P], bf16)
    mask_g = sb("mask_g", [P, P])
    ones2 = sb("ones2", [2, P], f32r)
    onesr = sb("onesr", [P, T])
    ha, hb, yb, ob, vb = (sb(n, [P, NTB, D]) for n in ("ha", "hb", "yb", "ob", "vb"))
    tt = sb("tt", [P, DC, TOK])
    stats, mv = sb("stats", [P, NTB, 6]), sb("mv", [P, NTB, 2])
    rs = [sb(f"rs{i}", [P, 16]) for i in range(3)]
    w1, w2 = sb("w1", [P, E_IT, DC, F]), sb("w2", [P, E_IT, FT, D])
    b1r, b1c = sb("b1r", [E_IT * FT, P]), sb("b1c", [P, E_IT * FT])
    b2b = sb("b2b", [P, E_IT, D])
    kst = sb("kst", [P, 4, 4, T], f32r)
    vpad = {a.name: sb(f"vpad_{a.name}", [P, 2, 2, a.group, a.vw]) for a in (att0, att1)}
    mx = sb("mx", [P, 2, 2, 8])
    rc = sb("rc", [P, 8])
    rows_hl = sb("rows_hl", [8, 2, 2, T], f32r)
    acc = [sb(f"acc{i}", [P, T]) for i in range(2)]
    sd = sb("sd", [P, 2, D])
    shared = ExitStack()
    hl = {k: sb(k, [P, 2, TOK], f32r, shared) for k in ("q_hi", "q_lo", "k_hi", "k_lo")}
    qst = sb("qst", [P, 4, 4, T], f32r, shared)
    mrow = sb("mrow", [2, 3, 4, T], f32r, shared)
    pt = [sb(f"pt{i}", [P, 2 * T], fp32, shared) for i in range(PT_RING)]
    shared.close()
    sb("parts_kept", [P, 3, 2, TOK], f32r, shared)
    q1 = sb("q1", [P, 4, 2, 4, T], f32r, shared)
    shared.close()
    hid = sb("hid", [P, E_IT, FT, T])
    qs, ks = sb("qs", [P, TOK]), sb("ks", [P, TOK])
    gz, gm, ge, gG = (sb(n, [P, TOK]) for n in ("gz", "gm", "ge", "gG"))
    u1 = sb("u1", [16, TOK])
    atm = sb("atm", [P, NHG, NTB, P])
    kT = sb("kT", [P, 2, P])
    dr = sb("dr", [P, 2])
    gb = sb("gb", [P, NTB, D])
    ps = [ctx.enter_context(nc.psum_tensor(f"ps{i}", [P, 512], fp32)) for i in range(8)]
    xs = {a.name: {k: dram(f"{a.name}_{k}_parts", (a.heads, 4, a.dim, TOK)) for k in "qk"} for a in (att0, att1)}

    sg = Signals(nc, ctx, "m")
    once = Signals(nc, whole, "w")
    done, go = once("done"), {k: once(f"go_{k}") for k in ("sp", "pe", "act", "pool")}
    loads = []

    def w_in(dst, src):
        loads.append((dst, src))

    def rows_view(ap):
        return ap.rearrange("(c p) n -> p c n", p=P)

    w_in(wqkv0[:, :, :], rows_view(io["L0_attn_Wqkv"]))
    w_in(dirs[:, :, :].rearrange("p h d -> p (h d)"),
         io["L0_attn_head_dirs"].rearrange("h d -> (h d)").partition_broadcast(P))
    w_in(hsc[:, :], io["L0_attn_head_scales"].partition_broadcast(P))
    w_in(wout0[:, :, :], rows_view(io["L0_attn_Wout"]))
    for dst, n in ((wq1, "wq"), (wk1, "wk"), (wv1, "wv"), (wo1, "wo")):
        w_in(dst[:, :, :], rows_view(io[f"L0_ffn_{n}"]))
    w_in(lng[:, :], io["L0_ffn_ln_g"].partition_broadcast(P))
    w_in(lnb[:, :], io["L0_ffn_ln_b"].partition_broadcast(P))
    w_in(gwq[:, :, :], rows_view(io["L1_attn_Wq"]))
    w_in(gwk[:, :, :], rows_view(io["L1_attn_Wk"]))
    w_in(gwvg[:, :, 0:D], rows_view(io["L1_attn_Wv"]))
    w_in(gwvg[:, :, D:], rows_view(io["L1_attn_Wg"]))
    w_in(gwgk1[:, :, :], rows_view(io["L1_attn_Wgk1"]))
    w_in(gwgk2[:, :], io["L1_attn_Wgk2"])
    w_in(gwo[:, :, :], rows_view(io["L1_attn_Wo"]))
    w_in(bgk[:, :], io["L1_attn_bgk2"].rearrange("(p o) -> p o", o=1))
    w_in(gwb[:, :], io["L1_attn_gw"].partition_broadcast(P))
    w_loaded, constants, ready = once("loaded"), once("constants"), once("ready")

    MAX_ROW = 96

    def q1_at(g, lane):
        return q1[:, 3 - g % 4, lane]

    block_ctx = ExitStack()
    block = block_ctx.enter_context(nc.Block())

    @block.sync
    def _(sp):
        for dst, src in loads:
            sp.dma_start(dst, src).then_inc(w_loaded, 16)

        def attention_operands(a):
            hw = P // a.dim

            def parts_out(n):
                t, which = n // 2, "qk"[n % 2]
                order = ("hi", "lo", "hi", "lo") if which == "q" else ("hi", "lo", "lo", "hi")
                for part in range(4):
                    if part < 2:
                        sp.wait_ge(sg(f"{a.name}_{order[part]}"), n + 1)
                    sp.dma_start(xs[a.name][which][t * hw:(t + 1) * hw, part, :, :],
                                 hl[f"{which}_{order[part]}"][:, t, :].bitcast(fp32))\
                        .then_inc(sg(f"{a.name}_parts_out{t}"), 16)

            def stack(g):
                bb, g1 = g // a.per_batch, g % a.per_batch
                t = 2 * g1 // a.per_batch
                sp.wait_ge(sg(f"{a.name}_parts_out{t}"), 16 * 8)
                if g >= a.RING:
                    sp.wait_ge(sg(a.name + "_st_full"), (g - a.RING + 1) * a.group)
                if a.lanes > 1 and g < a.RING:
                    sp.wait_ge(sg("q1_zero"), 1 if g < a.RING - 1 else 2)
                for which, st in (("q", qst), ("k", kst)):
                    for lane in range(a.lanes):
                        h = g1 * a.group + lane * a.slots
                        src = xs[a.name][which][h:h + a.slots, :, :, bb * T:(bb + 1) * T]
                        dst = q1_at(g, lane) if which == "q" and a.lanes > 1 else st[:, g % a.RING]
                        sp.dma_start(dst[64 * lane:64 * lane + a.rows, :, :].bitcast(fp32),
                                     src.rearrange("h p d t -> (p d) h t"))\
                            .then_inc(sg(f"{a.name}_stack{g % a.RING}"), 16)

            def send_rows(gr):
                sp.wait_ge(sg(a.name + "_rows"), gr + 1)
                if a.lanes == 1 and gr >= 3:
                    sp.wait_ge(sg(a.name + "_st_full"), (gr - 2) * a.group)
                for lane in range(a.lanes):
                    for part in range(2):
                        row = MAX_ROW + part
                        dst = mrow[part:part + 1, gr % 3] if a.lanes == 1 else q1_at(gr, lane)[row:row + 1]
                        sp.dma_start(dst.bitcast(fp32), rows_hl[lane * a.slots:(lane + 1) * a.slots, gr % 2, part, :]
                                     .bitcast(fp32)).then_inc(sg(f"{a.name}_rows_in{gr % 2}"), 16)

            parts_out(0)
            parts_out(1)
            parts_out(2)
            parts_out(3)
            for g in range(a.RING):
                stack(g)
            for g in range(a.groups):
                send_rows(g)
                if g >= 2 and g + 2 < a.groups:
                    stack(g + 2)

        with sp.Fori(0, PAIRS) as j:
            for bb in range(2):
                sp.dma_start(ha[:, 2 * bb:2 * bb + 2, :],
                             h0[j + PAIRS * bb].rearrange("(k p) d -> p k d", p=P))\
                    .then_inc(sg("h_in"), 16)
            for e in range(E_IT):
                sp.dma_start(w1[:, e, :, :], rows_view(io["L0_ffn_w1"][E_IT * j + e])).then_inc(sg("w_in"), 16)
                sp.dma_start(w2[:, e, :, :], rows_view(io["L0_ffn_w2"][E_IT * j + e])).then_inc(sg("w_in"), 16)
                sp.dma_start(b1r[e * FT:(e + 1) * FT, :],
                             io["L0_ffn_b1"][E_IT * j + e].rearrange("(c p) -> c p", p=P)).then_inc(sg("w_in"), 16)
                sp.dma_start(b2b[:, e, :], io["L0_ffn_b2"][E_IT * j + e].partition_broadcast(P))\
                    .then_inc(sg("w_in"), 16)
            attention_operands(att0)
            attention_operands(att1)
            sp.wait_ge(sg("h3"), 1)
            for bb in range(2):
                sp.dma_start(x3[j + PAIRS * bb].rearrange("(k p) d -> p k d", p=P), hb[:, 2 * bb:2 * bb + 2, :])\
                    .then_inc(sg("x3_out"), 16)
            sp.wait_ge(sg("x3_out"), 32)
            sp.sem_inc(done, 1)
            sp.wait_ge(go["sp"], 1)
            sp.sem_clear(go["sp"])

    @block.gpsimd
    def _(pool):
        g = nc.gpsimd
        g.tensor_copy(identb[:, :], ident[:, :]).then_inc(constants, 1)
        g.memset(mask_s[:, :], 0.0).then_inc(constants, 1)
        g.memset(mask_t[:, :], 0.0).then_inc(constants, 1)
        g.memset(mask_g[:, :], 1.0).then_inc(constants, 1)
        g.memset(onesr[:, :], 1.0).then_inc(constants, 1)
        pool.wait_ge(constants, 5)
        g.memset(mask_s[:, 2 * P:], NEG).then_inc(constants, 1)
        g.memset(mask_t[:, 0:P], NEG).then_inc(constants, 1)
        g.affine_select(out=mask_s[:, P:2 * P], in_=mask_s[:, P:2 * P], compare_op=ALU.is_ge, fill=NEG,
                        base=0, pattern=[[-1, P]], channel_multiplier=1).then_inc(constants, 1)
        g.affine_select(out=mask_t[:, P:2 * P], in_=mask_t[:, P:2 * P], compare_op=ALU.is_ge, fill=NEG,
                        base=0, pattern=[[1, P]], channel_multiplier=-1).then_inc(constants, 1)
        g.affine_select(out=mask_g[:, :], in_=mask_g[:, :], compare_op=ALU.is_ge, fill=0.0,
                        base=0, pattern=[[1, P]], channel_multiplier=-1).then_inc(constants, 1)
        for a in (att0, att1):
            g.memset(vpad[a.name][:, :, :, :, :], 0.0).then_inc(constants, 1)
        g.memset(sd[:, :, :], 0.0).then_inc(constants, 1)
        pool.wait_ge(constants, 13)
        for a in (att0, att1):
            for buf in range(2):
                for kt in range(2):
                    g.memset(vpad[a.name][:, buf, kt, :, a.dim:a.dim + 1], 1.0).then_inc(constants, 1)
        pool.wait_ge(constants, 21)

        def attention_feed(a):
            def pad_v(gr):
                bb, g1 = gr // a.per_batch, gr % a.per_batch
                if gr >= 2:
                    pool.wait_ge(sg(a.name + "_av_done"), (gr - 1) * a.group)
                for kt in range(2):
                    last = g.tensor_copy(
                        vpad[a.name][:, gr % 2, kt, :, 0:a.dim],
                        vb[:, 2 * bb + kt, g1 * a.group * a.dim:(g1 + 1) * a.group * a.dim]
                        .rearrange("p (h d) -> p h d", d=a.dim))
                    if kt == 0:
                        last.then_inc(sg(a.name + "_pad0"), 1)
                last.then_inc(sg(a.name + "_padded"), 1)

            pool.wait_ge(sg(a.name + "_v"), 2)
            for gr in range(a.groups):
                pad_v(gr)

        with pool.Fori(0, PAIRS) as j:
            attention_feed(att0)
            pool.wait_ge(sg("a0_st_full"), att0.units)
            g.memset(kst[MAX_ROW:MAX_ROW + 2, :, :, :].bitcast(fp32), 1.0).then_inc(sg("ones_row"), 1)
            pool.wait_ge(sg("ones_row"), 1)
            g.memset(q1[:, 1:, :, :, :].bitcast(fp32), 0.0).then_inc(sg("q1_zero"), 1)
            pool.wait_ge(sg("a1_parts_out0"), 16 * 8)
            pool.wait_ge(sg("a1_parts_out1"), 16 * 8)
            g.memset(q1[:, 0, :, :, :].bitcast(fp32), 0.0).then_inc(sg("q1_zero"), 1)
            pool.wait_ge(sg("q1_zero"), 2)
            attention_feed(att1)
            pool.wait_ge(sg("h3"), 1)
            pool.sem_inc(done, 1)
            pool.wait_ge(go["pool"], 1)
            pool.sem_clear(go["pool"])

    @block.tensor
    def _(pe):
        mm = nc.tensor.matmul
        pe.wait_ge(ready, 1)

        def transposes(src, name, after=None):
            if after:
                pe.wait_ge(*after)
            for c in range(DC):
                for tb in range(NTB):
                    last = nc.tensor.transpose(ps[c][:, tb * P:(tb + 1) * P], src[:, tb, c * P:(c + 1) * P],
                                               ident[:, :])
                last.then_inc(sg(name + "_full"), 1)

        def qkv(a, wq, wk, wv, name):
            pe.wait_ge(sg(name + "_ev"), 2)
            for n, (t, w) in enumerate(((0, wq), (0, wk), (1, wq), (1, wk))):
                for c in range(DC):
                    last = mm(ps[2 + n][:, :], w[:, c, t * P:(t + 1) * P], tt[:, c, :],
                              start=c == 0, stop=c == DC - 1)
                last.then_inc(sg(a.name + "_qk_full"), 1)
            for tb in range(NTB):
                for c in range(DC):
                    last = mm(ps[6 + tb // 2][:, (tb % 2) * D:(tb % 2 + 1) * D],
                              tt[:, c, tb * P:(tb + 1) * P], wv[:, c, :], start=c == 0, stop=c == DC - 1)
                if tb % 2:
                    last.then_inc(sg(a.name + "_v_full"), 1)

        def project(w, name, ob_ready):
            transposes(ob, name + "_t", ob_ready)
            pe.wait_ge(sg(name + "_t_ev"), 2)
            for tb in range(NTB):
                for c in range(DC):
                    last = mm(ps[2 + tb // 2][:, (tb % 2) * D:(tb % 2 + 1) * D],
                              tt[:, c, tb * P:(tb + 1) * P], w[:, c, :], start=c == 0, stop=c == DC - 1)
                if tb % 2:
                    last.then_inc(sg(name + "_full"), 1)

        def attention(a):
            n_ = a.name
            stack_dmas = 2 * a.lanes

            def scores(u):
                g, n = u // a.group, u % a.group
                lane, slot = a.lane_slot(n)
                if u >= 2:
                    pe.wait_ge(sg(n_ + "_max"), u - 1)
                q = qst[:, g % a.RING] if a.lanes == 1 else q1_at(g, lane)
                rows = a.rows if a.lanes == 1 else MAX_ROW
                for qb in range(2):
                    o = ps[u % 2][:, qb * T:(qb + 1) * T]
                    last = mm(o, q[0:rows, slot, qb * P:(qb + 1) * P], kst[0:rows, g % a.RING, slot, :],
                              start=True, stop=not a.causal)
                    if a.causal:
                        at = P if qb == 0 else 0
                        last = mm(o, identb[:, :], mask_s[:, at:at + T], start=False, stop=True)
                last.then_inc(sg(n_ + "_s_full"), 1)

            def scores_t(u):
                g, n = u // a.group, u % a.group
                lane, slot = a.lane_slot(n)
                if u >= 2:
                    pe.wait_ge(sg(n_ + "_exp"), u - 1)
                q = qst[:, g % a.RING] if a.lanes == 1 else q1_at(g, lane)
                rows = a.rows if a.lanes == 1 else MAX_ROW + 2
                for kt in range(2):
                    o = ps[2 + u % 2][:, kt * T:(kt + 1) * T]
                    last = mm(o, kst[0:rows, g % a.RING, slot, kt * P:(kt + 1) * P], q[0:rows, slot, :],
                              start=True, stop=a.lanes > 1)
                    if a.lanes == 1:
                        mm(o, ones2[:, :], mrow[:, g % 3, slot, :], start=False, stop=False)
                        at = P if kt == 0 else 0
                        last = mm(o, identb[:, :], mask_t[:, at:at + T], start=False, stop=True)
                last.then_inc(sg(n_ + "_st_full"), 1)

            def values(k):
                if k >= 2:
                    pe.wait_ge(sg(n_ + "_acc"), k - 1)
                pe.wait_ge(sg(n_ + "_exp"), (k + 1) * a.quad)
                for kt in range(2):
                    q0 = P if a.causal and kt else 0
                    for i in range(a.quad):
                        u = k * a.quad + i
                        g, n = u // a.group, u % a.group
                        last = mm(ps[4 + k % 2][i * a.vw:(i + 1) * a.vw, q0:T], vpad[a.name][:, g % 2, kt, n, :],
                                  pt[u % PT_RING][:, kt * T + q0:(kt + 1) * T], start=kt == 0, stop=kt == 1)
                last.then_inc(sg(n_ + "_av_done"), a.quad)

            def outputs_t(k):
                pe.wait_ge(sg(n_ + "_acc"), k + 1)
                if k:
                    pe.wait_ge(sg(n_ + "_norm"), k)
                for qb in range(2):
                    last = nc.tensor.transpose(ps[7][:, qb * P:(qb + 1) * P],
                                               acc[k % 2][:, qb * P:(qb + 1) * P], ident[:, :])
                last.then_inc(sg(n_ + "_o_full"), 1)

            def maxima_t(g):
                pe.wait_ge(sg(n_ + "_max"), (g + 1) * a.group)
                if g:
                    pe.wait_ge(sg(n_ + "_rows"), g)
                for qb in range(2):
                    last = nc.tensor.transpose(ps[6][0:a.group, qb * P:(qb + 1) * P],
                                               mx[:, g % 2, qb, 0:a.group], ident[:, :])
                last.then_inc(sg(n_ + "_mt_full"), 1)

            def after_scores(u):
                for k in a.due(u, OUT_LAG):
                    outputs_t(k)
                for k in a.due(u, AV_LAG):
                    values(k)

            pe.wait_ge(sg(n_ + "_v"), 2)
            if a.lanes > 1:
                pe.wait_ge(sg("ones_row"), 1)
            for p in range(a.groups + 2):
                gs, gt = p, p - 2
                if gs < a.groups:
                    pe.wait_ge(sg(f"{n_}_stack{gs % a.RING}"), 16 * stack_dmas * (gs // a.RING + 1))
                if gt >= 0:
                    pe.wait_ge(sg(f"{n_}_rows_in{gt % 2}"), 16 * 2 * a.lanes * (gt // 2 + 1))
                    pe.wait_ge(sg(n_ + "_padded"), gt + 1)
                for n in range(a.group):
                    if gt >= 0:
                        u = gt * a.group + n
                        scores_t(u)
                    if gs < a.groups:
                        scores(gs * a.group + n)
                    if gt >= 0:
                        after_scores(u)
                if gs < a.groups:
                    maxima_t(gs)
            for u in range(a.units, a.units + OUT_LAG):
                after_scores(u)

        def experts():
            pe.wait_ge(sg("w_in"), 16 * 4 * E_IT)
            nc.tensor.transpose(ps[6][:, 0:E_IT * FT], b1r[:, :], ident[0:E_IT * FT, 0:E_IT * FT])\
                .then_inc(sg("b1_full"), 1)
            pe.wait_ge(sg("xf_t_ev"), 2)
            n = 0
            for e in range(E_IT):
                mv_ = [tt[:, c, :].rearrange("p (b k t) -> p k b t", b=2, k=2)[:, e] for c in range(DC)]
                for f2 in range(FT // 2):
                    if n >= 4:
                        pe.wait_ge(sg("up_ev"), 2 * (n - 3))
                    for f in (2 * f2, 2 * f2 + 1):
                        for c in range(DC):
                            last = mm(ps[2 + n % 4][:, (f % 2) * T:(f % 2 + 1) * T],
                                      w1[:, e, c, f * P:(f + 1) * P], mv_[c], start=c == 0, stop=c == DC - 1)
                    last.then_inc(sg("up_full"), 1)
                    n += 1
            pe.wait_ge(sg("b1_ev"), 1)
            for e in range(E_IT):
                pe.wait_ge(sg("up_ev"), FT * (e + 1))
                for bb in range(2):
                    o = ps[(0, 1, 6, 7)[2 * e + bb]][:, 0:D]
                    for f in range(FT):
                        last = mm(o, hid[:, e, f, bb * P:(bb + 1) * P], w2[:, e, f, :], start=f == 0,
                                  stop=f == FT - 1)
                    last.then_inc(sg("down_full"), 1)

        def linear_attention():
            pe.wait_ge(sg("h2_t_ev"), 2)
            for n, w in ((2, gwq), (3, gwk)):
                for c in range(DC):
                    last = mm(ps[n][:, :], w[:, c, :], tt[:, c, :], start=c == 0, stop=c == DC - 1)
                last.then_inc(sg("g_qk_full"), 1)
            for c in range(DC):
                last = mm(ps[4][0:16, :], gwgk1[:, c, :], tt[:, c, :], start=c == 0, stop=c == DC - 1)
            last.then_inc(sg("g_u_full"), 1)
            for tb in range(NTB):
                for c in range(DC):
                    last = mm(ps[(6, 7, 0, 1)[tb]][:, :], tt[:, c, tb * P:(tb + 1) * P], gwvg[:, c, :],
                              start=c == 0, stop=c == DC - 1)
                last.then_inc(sg("g_vg_full"), 1)
                if tb == 0:
                    pe.wait_ge(sg("g_u"), 1)
                    mm(ps[5][:, :], gwgk2[:, :], u1[:, :], start=True, stop=True).then_inc(sg("g_z_full"), 1)
            pe.wait_ge(sg("g_qk"), 2)
            pe.wait_ge(sg("g_vg"), 8)
            for bb in range(2):
                last = nc.tensor.transpose(ps[6][:, bb * P:(bb + 1) * P], ks[:, 2 * bb * P:(2 * bb + 1) * P],
                                           ident[:, :])
            last.then_inc(sg("g_kt_full"), 1)
            for h in range(NHG):
                for tb in range(NTB):
                    last = mm(ps[2 + h][:, tb * P:(tb + 1) * P], ks[h * DK:(h + 1) * DK, tb * P:(tb + 1) * P],
                              qs[h * DK:(h + 1) * DK, tb * P:(tb + 1) * P], start=True, stop=True)
                last.then_inc(sg("g_at_full"), 1)
            pe.wait_ge(sg("g_kt"), 1)
            for bb in range(2):
                last = mm(ps[7][:, bb * D:(bb + 1) * D], kT[:, bb, :], vb[:, 2 * bb, :], start=True, stop=True)
            last.then_inc(sg("g_state_full"), 1)
            pe.wait_ge(sg("g_at"), NHG)
            pe.wait_ge(sg("g_state"), 1)
            for tb in range(NTB):
                o = ps[(0, 1, 6, 7)[tb]]
                if tb % 2:
                    mm(o[:, 0:D], qs[:, tb * P:(tb + 1) * P], sd[:, tb // 2, :], start=True, stop=False,
                       skip_group_check=True)
                for h in range(NHG):
                    last = mm(o[:, h * DV:(h + 1) * DV], atm[:, h, tb, :], vb[:, tb, h * DV:(h + 1) * DV],
                              start=tb % 2 == 0, stop=True, skip_group_check=True)
                last.then_inc(sg("g_o_full"), 1)

        with pe.Fori(0, PAIRS) as j:
            transposes(ha, "h_t", (sg("h_in"), 32))
            qkv(att0, wqkv0[:, :, 0:D], wqkv0[:, :, D:2 * D], wqkv0[:, :, 2 * D:], "h_t")
            attention(att0)
            project(wout0, "p0", (sg("a0_norm"), att0.units // att0.quad))
            transposes(yb, "xn_t", (sg("xn"), 1))
            qkv(att1, wq1, wk1, wv1, "xn_t")
            attention(att1)
            project(wo1, "p1", (sg("a1_norm"), att1.units // att1.quad))
            transposes(yb, "xf_t", (sg("xf"), 1))
            experts()
            transposes(ha, "h2_t", (sg("h2"), 1))
            linear_attention()
            project(gwo, "p2", (sg("g_o"), 1))
            pe.wait_ge(go["pe"], 1)
            pe.sem_clear(go["pe"])

    @block.scalar
    def _(act):
        sc = nc.scalar
        act.wait_ge(ready, 1)

        def transposed(name):
            act.wait_ge(sg(name + "_full"), 1)
            sc.copy(tt[:, 0, :], ps[0][:, :]).then_inc(sg(name + "_ev"), 1)

        def qkv(a):
            for n in range(4):
                act.wait_ge(sg(a.name + "_qk_full"), n + 1)
                sc.copy(hl[("q_hi", "k_hi")[n % 2]][:, n // 2, :], ps[2 + n][:, :]).then_inc(sg(a.name + "_hi"), 1)
            for n in range(2):
                act.wait_ge(sg(a.name + "_v_full"), n + 1)
                sc.copy(vb[:, 2 * n:2 * n + 2, :], ps[6 + n][:, :].rearrange("p (b d) -> p b d", b=2))\
                    .then_inc(sg(a.name + "_v"), 1)

        def attention(a):
            n_ = a.name

            def heads_out(k):
                act.wait_ge(sg(n_ + "_av_done"), (k + 1) * a.quad)
                if k >= 2:
                    act.wait_ge(sg(n_ + "_o_full"), k - 1)
                sc.copy(acc[k % 2][:, :], ps[4 + k % 2][:, 0:T]).then_inc(sg(n_ + "_acc"), 1)

            for u in range(a.units):
                act.wait_ge(sg(n_ + "_st_full"), u + 1)
                if u >= PT_RING:
                    act.wait_ge(sg(n_ + "_av_done"), u - PT_RING + 1)
                sc.activation(pt[u % PT_RING][:, :], ps[2 + u % 2][:, :], ACT.Exp).then_inc(sg(n_ + "_exp"), 1)
                for k in a.due(u, AV_LAG):
                    heads_out(k)
            for u in range(a.units, a.units + AV_LAG):
                for k in a.due(u, AV_LAG):
                    heads_out(k)

        def experts():
            act.wait_ge(sg("b1_full"), 1)
            sc.copy(b1c[:, :], ps[6][:, 0:E_IT * FT]).then_inc(sg("b1_ev"), 1)
            act.wait_ge(sg("b1_ev"), 1)
            for n in range(E_IT * FT // 2):
                act.wait_ge(sg("up_full"), n + 1)
                for i in range(2):
                    f = 2 * n + i
                    sc.activation(hid[:, f // FT, f % FT, :], ps[2 + n % 4][:, i * T:(i + 1) * T], ACT.Gelu,
                                  bias=b1c[:, f:f + 1]).then_inc(sg("up_ev"), 1)

        def linear_attention():
            act.wait_ge(sg("g_u_full"), 1)
            sc.copy(u1[:, :], ps[4][0:16, :]).then_inc(sg("g_u"), 1)
            for tb in range(NTB):
                act.wait_ge(sg("g_vg_full"), tb + 1)
                o = ps[(6, 7, 0, 1)[tb]]
                sc.copy(vb[:, tb, :], o[:, 0:D]).then_inc(sg("g_vg"), 1)
                sc.copy(gb[:, tb, :], o[:, D:]).then_inc(sg("g_vg"), 1)
            act.wait_ge(sg("g_z"), 1)
            sc.activation(ge[:, :], ge[:, :], ACT.Exp).then_inc(sg("g_a"), 1)
            act.wait_ge(sg("g_a"), 1)
            sc.activation(ge[:, :], ge[:, :], ACT.Ln, bias=1.0).then_inc(sg("g_a"), 1)
            act.wait_ge(sg("g_d"), 1)
            sc.activation(ge[:, :], gz[:, :], ACT.Exp).then_inc(sg("g_a"), 1)
            sc.activation(gm[:, :], gz[:, :], ACT.Exp, scale=-1.0).then_inc(sg("g_a"), 1)
            act.wait_ge(sg("g_vg"), 8)
            sc.activation(yb[:, :, :], gb[:, :, :], ACT.Exp, scale=-1.0).then_inc(sg("g_a"), 1)
            sc.activation(dr[:, :], dr[:, :], ACT.Exp).then_inc(sg("g_dr"), 1)
            act.wait_ge(sg("g_kt_full"), 1)
            sc.copy(kT[:, :, :], ps[6][:, 0:2 * P].rearrange("p (b k) -> p b k", b=2)).then_inc(sg("g_kt"), 1)
            for tb in range(NTB):
                act.wait_ge(sg("g_o_full"), tb + 1)
                sc.activation(hb[:, tb, :], ps[(0, 1, 6, 7)[tb]][:, 0:D], ACT.Square).then_inc(sg("g_sq"), 1)

        with act.Fori(0, PAIRS) as j:
            transposed("h_t")
            qkv(att0)
            attention(att0)
            transposed("p0_t")
            transposed("xn_t")
            qkv(att1)
            attention(att1)
            transposed("p1_t")
            transposed("xf_t")
            experts()
            transposed("h2_t")
            linear_attention()
            transposed("p2_t")
            act.wait_ge(go["act"], 1)
            act.sem_clear(go["act"])

    @block.vector
    def _(dve):
        v = nc.vector
        s = Counted(dve, once("prepare"))
        dve.wait_ge(w_loaded, 16 * len(loads))
        dve.wait_ge(constants, 21)
        wq = wqkv0[:, :, 0:D].rearrange("p c (h k) -> p c h k", h=8)
        for c in range(DC):
            s.step(v.tensor_tensor(gp[:, c], wq[:, c, :, 0:3], dirs[:, :, :], ALU.mult))
            s.step(v.tensor_reduce(gq[:, c, :], gp[:, c], AX.X, ALU.add))
            s.step(v.tensor_tensor(gq[:, c, :], gq[:, c, :], hsc[:, :], ALU.mult))
            s.step(v.tensor_tensor(gp[:, c], dirs[:, :, :],
                                   gq[:, c, :].unsqueeze(2).to_broadcast([P, 8, 3]), ALU.mult))
            s.step(v.tensor_scalar(wqkv0[:, c, 0:D], wqkv0[:, c, 0:D], att0.dim ** -0.5, None, ALU.mult))
            s.step(v.tensor_tensor(wq[:, c, :, 0:3], wq[:, c, :, 0:3], gp[:, c], ALU.add))
        s.step(v.tensor_scalar(wq1[:, :, :], wq1[:, :, :], att1.dim ** -0.5, None, ALU.mult))
        s.step(v.tensor_copy(ones2[:, :], onesr[0:2, 0:P]))
        v.tensor_copy(rc[:, 0:1], onesr[:, 0:1]).then_inc(ready, 1)

        s = None

        def transposed(name):
            dve.wait_ge(sg(name + "_full"), 2)
            v.tensor_copy(tt[:, 1, :], ps[1][:, :]).then_inc(sg(name + "_ev"), 1)

        def qkv(a):
            for n in range(4):
                dve.wait_ge(sg(a.name + "_hi"), n + 1)
                w = ("q", "k")[n % 2]
                v.tensor_tensor(hl[w + "_lo"][:, n // 2, :], ps[2 + n][:, :], hl[w + "_hi"][:, n // 2, :]
                                .bitcast(fp32), ALU.subtract).then_inc(sg(a.name + "_lo"), 1)

        def attention(a, s):
            n_ = a.name

            def maximum(u):
                g, n = u // a.group, u % a.group
                dve.wait_ge(sg(n_ + "_s_full"), u + 1)
                if n == 0 and g >= 2:
                    dve.wait_ge(sg(n_ + "_mt_full"), g - 1)
                v.tensor_reduce(mx[:, g % 2, :, n], ps[u % 2][:, :].rearrange("p (b k) -> p b k", b=2),
                                AX.X, ALU.max, negate=True).then_inc(sg(n_ + "_max"), 1)

            def rows(g):
                dve.wait_ge(sg(n_ + "_mt_full"), g + 1)
                if g >= 2:
                    dve.wait_ge(sg(f"{n_}_rows_in{g % 2}"), 16 * 2 * a.lanes * (g // 2))
                hi, lo = (rows_hl[0:a.group, g % 2, i, :] for i in range(2))
                s.step(v.tensor_copy(hi, ps[6][0:a.group, 0:T]))
                v.tensor_tensor(lo, ps[6][0:a.group, 0:T], hi.bitcast(fp32), ALU.subtract)\
                    .then_inc(sg(n_ + "_rows"), 1)

            def normalise(k):
                dve.wait_ge(sg(n_ + "_o_full"), k + 1)
                h = k * a.quad % a.heads
                bb = k * a.quad // a.heads
                o = ps[7][:, 0:2 * P].rearrange("p (b h w) -> p b h w", b=2, h=a.quad)
                s.step(v.reciprocal(rc[:, 0:2 * a.quad].rearrange("p (b h) -> p b h", b=2), o[:, :, :, a.dim]))
                v.tensor_tensor(ob[:, 2 * bb:2 * bb + 2, h * a.dim:(h + a.quad) * a.dim]
                                .rearrange("p b (h d) -> p b h d", h=a.quad), o[:, :, :, 0:a.dim],
                                rc[:, 0:2 * a.quad].rearrange("p (b h) -> p b h", b=2).unsqueeze(3)
                                .to_broadcast([P, 2, a.quad, a.dim]), ALU.mult).then_inc(sg(n_ + "_norm"), 1)

            for p in range(a.groups + 2):
                gs, gt = p, p - 2
                for n in range(a.group):
                    if gs < a.groups:
                        maximum(gs * a.group + n)
                    for k in a.due(gt * a.group + n, NORM_LAG):
                        normalise(k)
                if gs < a.groups:
                    rows(gs)
            for u in range(a.units, a.units + NORM_LAG):
                for k in a.due(u, NORM_LAG):
                    normalise(k)

        def layernorm(s, src, dst):
            for tb in range(NTB):
                s.mark(v.bn_stats(stats[:, tb, :], src[:, tb, :]))
            s.sync()
            for tb in range(NTB):
                s.mark(v.bn_aggr(mv[:, tb, :], stats[:, tb, :]))
            s.sync()
            x_, y_, a_ = (r[:, 0:NTB] for r in rs)
            s.step(v.tensor_scalar(x_, mv[:, :, 1], LN_EPS, None, ALU.add))
            rsqrt_steps(s, v, x_, y_, a_)
            for tb in range(NTB):
                last = s.mark(v.tensor_scalar(dst[:, tb, :], src[:, tb, :], mv[:, tb, 0:1], rs[1][:, tb:tb + 1],
                                              ALU.subtract, ALU.mult))
            s.sync()

        def add_projection(s, name, resid, dst):
            for n in range(2):
                dve.wait_ge(sg(name + "_full"), n + 1)
                s.mark(v.tensor_tensor(dst[:, 2 * n:2 * n + 2, :],
                                       ps[2 + n][:, :].rearrange("p (b d) -> p b d", b=2),
                                       resid[:, 2 * n:2 * n + 2, :], ALU.add))
            s.sync()

        def signal(s, name):
            s.sync()
            dve.sem_inc(sg(name), 1)

        def experts(s):
            for e in range(E_IT):
                for bb in range(2):
                    dve.wait_ge(sg("down_full"), 2 * e + bb + 1)
                    s.mark(v.tensor_tensor(yb[:, 2 * bb + e, :], ps[(0, 1, 6, 7)[2 * e + bb]][:, 0:D], b2b[:, e, :],
                                           ALU.add))
            s.sync()
            s.step(v.tensor_tensor(yb[:, :, :], yb[:, :, :], hb[:, :, :], ALU.add))

        def linear_attention(s):
            dve.wait_ge(sg("g_z_full"), 1)
            s.step(v.tensor_scalar(gz[:, :], ps[5][:, :], bgk[:, 0:1], None, ALU.add))
            s.mark(v.tensor_scalar(gm[:, :], gz[:, :], 0.0, None, ALU.min))
            v.scalar_tensor_tensor(ge[:, :], gz[:, :], -1.0, gz[:, :], ALU.mult, ALU.min).then_inc(sg("g_z"), 1)
            dve.wait_ge(sg("g_a"), 2)
            s.step(v.tensor_tensor(gm[:, :], gm[:, :], ge[:, :], ALU.subtract))
            s.step(v.tensor_scalar(gm[:, :], gm[:, :], 1 / 16.0, None, ALU.mult))
            for bb in range(2):
                s.mark(v.tensor_tensor_scan(gG[:, bb * T:(bb + 1) * T], onesr[:, :], gm[:, bb * T:(bb + 1) * T],
                                            0.0, ALU.mult, ALU.add))
            s.sync()
            mid = [gG[:, tb * P + P // 2 - 1:tb * P + P // 2] for tb in range(NTB)]
            for tb in range(NTB):
                s.mark(v.tensor_scalar(gz[:, tb * P:(tb + 1) * P], gG[:, tb * P:(tb + 1) * P], mid[tb], None,
                                       ALU.subtract))
            for bb in range(2):
                s.mark(v.tensor_tensor(dr[:, bb:bb + 1], mid[2 * bb + 1], mid[2 * bb], ALU.subtract))
            s.sync()
            signal(s, "g_d")
            dve.wait_ge(sg("g_qk_full"), 2)
            dve.wait_ge(sg("g_a"), 4)
            v.scalar_tensor_tensor(qs[:, :], ps[2][:, :], DK ** -0.5, ge[:, :], ALU.mult, ALU.mult)\
                .then_inc(sg("g_qk"), 1)
            v.tensor_tensor(ks[:, :], ps[3][:, :], gm[:, :], ALU.mult).then_inc(sg("g_qk"), 1)
            dve.wait_ge(sg("g_a"), 5)
            s.step(v.tensor_scalar(yb[:, :, :], yb[:, :, :], 1.0, None, ALU.add))
            s.step(v.reciprocal(yb[:, :, :], yb[:, :, :]))
            s.step(v.tensor_tensor(gb[:, :, :], gb[:, :, :], yb[:, :, :], ALU.mult))
            s.step(v.tensor_tensor(gb[:, :, :].rearrange("p t (h d) -> p (t h) d", d=DV),
                                   gb[:, :, :].rearrange("p t (h d) -> p (t h) d", d=DV),
                                   gwb[:, :].unsqueeze(1).to_broadcast([P, NTB * NHG, DV]), ALU.mult))
            for h in range(NHG):
                dve.wait_ge(sg("g_at_full"), h + 1)
                v.tensor_tensor(atm[:, h, :, :], ps[2 + h][:, :].rearrange("p (b t) -> p b t", b=NTB),
                                mask_g[:, :].unsqueeze(1).to_broadcast([P, NTB, P]), ALU.mult)\
                    .then_inc(sg("g_at"), 1)
            dve.wait_ge(sg("g_state_full"), 1)
            dve.wait_ge(sg("g_dr"), 1)
            for bb in range(2):
                for h in range(NHG):
                    r = slice(h * DK, (h + 1) * DK)
                    s.mark(v.tensor_scalar(sd[r, bb, h * DV:(h + 1) * DV],
                                           ps[7][r, bb * D + h * DV:bb * D + (h + 1) * DV],
                                           dr[r, bb:bb + 1], None, ALU.mult))
            s.sync()
            signal(s, "g_state")
            dve.wait_ge(sg("g_sq"), NTB)
            x_, y_, a_ = (r[:, :] for r in rs)
            s.step(v.tensor_reduce(x_, hb[:, :, :].rearrange("p t (h d) -> p (t h) d", d=DV), AX.X, ALU.add))
            s.step(v.tensor_scalar(x_, x_, 1.0 / DV, LN_EPS, ALU.mult, ALU.add))
            rsqrt_steps(s, v, x_, y_, a_)
            for tb in range(NTB):
                shape = [P, NHG, DV]
                s.mark(v.tensor_tensor(ob[:, tb, :].rearrange("p (h d) -> p h d", d=DV),
                                       ps[(0, 1, 6, 7)[tb]][:, 0:D].rearrange("p (h d) -> p h d", d=DV),
                                       rs[1][:, tb * NHG:(tb + 1) * NHG].unsqueeze(2).to_broadcast(shape),
                                       ALU.mult))
            s.sync()
            s.step(v.tensor_tensor(ob[:, :, :], ob[:, :, :], gb[:, :, :], ALU.mult))
            signal(s, "g_o")

        with dve.Fori(0, PAIRS) as j:
            s = Counted(dve, sg("dve_steps"))
            transposed("h_t")
            qkv(att0)
            attention(att0, s)
            transposed("p0_t")
            add_projection(s, "p0", ha, yb)
            layernorm(s, yb, hb)
            layernorm(s, hb, yb)
            s.step(v.tensor_tensor(yb[:, :, :], yb[:, :, :], lng[:, :].unsqueeze(1).to_broadcast([P, NTB, D]),
                                   ALU.mult))
            s.step(v.tensor_tensor(yb[:, :, :], yb[:, :, :], lnb[:, :].unsqueeze(1).to_broadcast([P, NTB, D]),
                                   ALU.add))
            signal(s, "xn")
            transposed("xn_t")
            qkv(att1)
            attention(att1, s)
            transposed("p1_t")
            add_projection(s, "p1", hb, yb)
            signal(s, "xf")
            transposed("xf_t")
            experts(s)
            layernorm(s, yb, ha)
            signal(s, "h2")
            transposed("h2_t")
            linear_attention(s)
            transposed("p2_t")
            add_projection(s, "p2", ha, yb)
            layernorm(s, yb, hb)
            signal(s, "h3")
            dve.wait_ge(done, 2)
            dve.sem_clear(done)
            for numbers in sg.runs():
                dve.sem_clear(numbers)
            for k in go:
                dve.sem_inc(go[k], 1)
    block_ctx.close()


def expert_mixture(nc, ctx, io, x3, xs, ys, out, ident):
    NTB = B * T // P
    E, F = 8, 1024
    FT = F // P
    GRP, NG = 4, NTB // 4
    TILES = xs.shape[0] // P
    HALF = F // 2
    KH = FT // 2
    XR = 4
    GR = 4

    def sb(name, shape, dt=fp32):
        return ctx.enter_context(nc.sbuf_tensor(name, shape, dt))

    sg = Signals(nc, ctx, "x")
    acc = sb("x_acc", [P, NTB, D])
    xTr = sb("x_Tr", [P, 2, DC, GRP * P])
    w1, w2 = sb("x_w1", [P, E, DC, F]), sb("x_w2", [P, E, FT, D])
    xt, xtT = sb("x_xt", [P, XR, D]), sb("x_xtT", [P, 2, DC, P])
    raw = sb("x_raw", [P, 2, HALF])
    hT = sb("x_hT", [P, 2, FT, P])
    y = sb("x_y", [P, 2, D])
    pair = sb("x_pair", [P, GR, 2, D])
    wg, bg = sb("x_wg", [P, DC, E]), sb("x_bg", [P, E])
    b1r, b1c = sb("x_b1r", [E * FT, P]), sb("x_b1c", [P, E * FT])
    b2b = sb("x_b2b", [P, E, D])
    rank = sb("x_rank", [P, E])
    before, ones = sb("x_before", [P, P]), sb("x_ones", [P, P])
    lo, pr, eq, oh1, oh2, both, sa, sc_ = (sb(f"x_{n}", [P, NTB, E])
                                          for n in ("lo", "pr", "eq", "oh1", "oh2", "both", "sa", "sc"))
    m1, m2, ix, dd = (sb(f"x_{n}", [P, NTB]) for n in ("m1", "m2", "ix", "dd"))
    cnt, cum, cum2 = (sb(f"x_{n}", [P, E]) for n in ("cnt", "cum", "cum2"))
    cnti = sb("x_cnti", [P, E], i32)
    tile_no, past = sb("x_tile_no", [1, TILES, E]), sb("x_past", [1, TILES, E])
    tef, te = sb("x_tef", [1, TILES]), sb("x_te", [1, TILES], i32)
    slotf, slot = sb("x_slotf", [P, 2, NTB]), sb("x_slot", [P, 2, NTB], u32)
    stats, mv = sb("x_stats", [P, NTB, 6]), sb("x_mv", [P, NTB, 2])
    rs = [sb(f"x_rs{i}", [P, GRP]) for i in range(3)]
    ps = [ctx.enter_context(nc.psum_tensor(f"x_ps{i}", [P, 512], fp32)) for i in range(8)]

    with nc.Block() as block:
        @block.sync
        def _(sp):
            sp.dma_start(wg[:, :, :], io["L1_ffn_Wg"].rearrange("(c p) e -> p c e", p=P)).then_inc(sg("small"), 16)
            sp.dma_start(bg[:, :], io["L1_ffn_bg"].partition_broadcast(P)).then_inc(sg("small"), 16)
            sp.dma_start(b1r[:, :], io["L1_ffn_b1"].rearrange("e (c p) -> (e c) p", p=P)).then_inc(sg("small"), 16)
            for g in range(NG):
                sp.dma_start(acc[:, g * GRP:(g + 1) * GRP, :],
                             x3[2 * g:2 * g + 2].rearrange("b (k p) d -> p (b k) d", p=P)).then_inc(sg(f"x_in{g}"), 16)
            for e in range(E):
                sp.dma_start(w1[:, e], io["L1_ffn_W1"][e].rearrange("(c p) n -> p c n", p=P)).then_inc(sg("w_in"), 16)
                sp.dma_start(w2[:, e], io["L1_ffn_W2"][e].rearrange("(c p) n -> p c n", p=P)).then_inc(sg("w_in"), 16)
            sp.dma_start(b2b[:, :, :], io["L1_ffn_b2"].partition_broadcast(P)).then_inc(sg("w_in"), 16)
            sp.wait_ge(sg("scattered"), 16 * 2 * NTB)

            def load_tile(i):
                if i >= XR:
                    sp.wait_ge(sg("xt_full"), i - XR + 1)
                sp.dma_start(xt[:, i % XR, :], xs[i * P:(i + 1) * P, :]).then_inc(sg(f"xt_in{i % XR}"), 16)

            for i in range(XR - 1):
                load_tile(i)
            for i in range(TILES):
                if i + XR - 1 < TILES:
                    load_tile(i + XR - 1)
                sp.wait_ge(sg("y"), i + 1)
                sp.dma_start(ys[i * P:(i + 1) * P, :], y[:, i % 2, :]).then_inc(sg(f"y_out{i % 2}"), 16)
            for g in range(NG):
                sp.wait_ge(sg("normed"), GRP * (g + 1))
                sp.dma_start(out[2 * g:2 * g + 2].rearrange("b (k p) d -> p (b k) d", p=P),
                             acc[:, g * GRP:(g + 1) * GRP, :]).then_inc(sg("stored"), 16)
            sp.wait_ge(sg("stored"), 16 * NG)

        @block.gpsimd
        def _(pool):
            g = nc.gpsimd
            g.iota(rank[:, :], pattern=[[1, E]], base=-E, channel_multiplier=0,
                   allow_small_or_imprecise_dtypes=True).then_inc(sg("constants"), 1)
            g.iota(tile_no[:, :, :], pattern=[[1, TILES], [0, E]], base=0, channel_multiplier=0,
                   allow_small_or_imprecise_dtypes=True).then_inc(sg("constants"), 1)
            g.memset(ones[:, :], 1.0).then_inc(sg("constants"), 1)
            pool.wait_ge(sg("constants"), 3)
            g.affine_select(out=before[:, :], in_=ones[:, :], compare_op=ALU.is_ge, fill=0.0, base=-1,
                            pattern=[[1, P]], channel_multiplier=-1).then_inc(sg("constants"), 1)
            pool.wait_ge(sg("slots"), 1)
            for g_ in range(NG):
                pool.wait_ge(sg(f"x_in{g_}"), 16)
            for tb in range(NTB):
                for k in range(2):
                    g.indirect_dma_start(out=xs[:, :], out_offset=bass.IndirectOffsetOnAxis(slot[:, k, tb:tb + 1], 0),
                                         in_=acc[:, tb, :], in_offset=None).then_inc(sg("scattered"), 16)
            pool.wait_ge(sg("y_out0"), 16 * ((TILES + 1) // 2))
            pool.wait_ge(sg("y_out1"), 16 * (TILES // 2))
            for tb in range(NTB):
                if tb >= GR:
                    pool.wait_ge(sg("combined"), tb - GR + 1)
                for k in range(2):
                    g.indirect_dma_start(out=pair[:, tb % GR, k, :], out_offset=None, in_=ys[:, :],
                                         in_offset=bass.IndirectOffsetOnAxis(slot[:, k, tb:tb + 1], 0))\
                        .then_inc(sg(f"pair_in{tb % GR}"), 16)

        @block.tensor
        def _(pe):
            mm, tr = nc.tensor.matmul, nc.tensor.transpose

            def group_t(g):
                pe.wait_ge(sg(f"x_in{g}"), 16)
                if g >= 2:
                    pe.wait_ge(sg("xT"), DC * (g - 1))
                for c in range(DC):
                    for k in range(GRP):
                        last = tr(ps[g % 2 * 2 + c][:, k * P:(k + 1) * P], acc[:, g * GRP + k, c * P:(c + 1) * P],
                                  ident[:, :])
                    last.then_inc(sg("xT_full"), 1)

            def scores(g):
                pe.wait_ge(sg("xT"), DC * (g + 1))
                for k in range(GRP):
                    tb = g * GRP + k
                    for c in range(DC):
                        last = mm(ps[4][:, tb * E:(tb + 1) * E], xTr[:, g % 2, c, k * P:(k + 1) * P], wg[:, c, :],
                                  start=c == 0, stop=c == DC - 1)
                last.then_inc(sg("scores_full"), 1)

            pe.wait_ge(sg("small"), 48)
            tr(ps[6][:, 0:E * FT], b1r[:, :], ident[0:E * FT, 0:E * FT]).then_inc(sg("b1_full"), 1)
            group_t(0)
            for g in range(NG):
                if g + 1 < NG:
                    group_t(g + 1)
                scores(g)
            pe.wait_ge(sg("constants"), 4)
            pe.wait_ge(sg("both"), 1)
            flat = both[:, :, :].rearrange("p t e -> p (t e)")
            mm(ps[5][:, 0:NTB * E], before[:, :], flat, start=True, stop=True)
            mm(ps[5][:, NTB * E:2 * NTB * E], ones[:, :], flat, start=True, stop=True).then_inc(sg("counts_full"), 1)

            def rows_t(i):
                pe.wait_ge(sg(f"xt_in{i % XR}"), 16 * (i // XR + 1))
                if i >= 2:
                    pe.wait_ge(sg("xtT"), i - 1)
                for c in range(DC):
                    last = tr(ps[6 + i % 2][:, c * P:(c + 1) * P], xt[:, i % XR, c * P:(c + 1) * P], ident[:, :])
                last.then_inc(sg("xt_full"), 1)

            pe.wait_ge(sg("b1"), 1)
            rows_t(0)
            pe.wait_ge(sg("te"), 1)
            pe.wait_ge(sg("w_in"), 16 * (2 * E + 1))
            expert = None
            for i in range(TILES + 1):
                last_expert = expert
                if i < TILES:
                    expert = pe.value_load(te[0:1, i:i + 1], min_val=0, max_val=E - 1)
                    pe.wait_ge(sg("xtT"), i + 1)
                    if i:
                        pe.wait_ge(sg("raw"), 2 * i)
                    for h in range(2):
                        for c in range(DC):
                            last = mm(ps[h][:, :], xtT[:, i % 2, c, :],
                                      w1[:, bass.ds(expert, 1), c, h * HALF:(h + 1) * HALF],
                                      start=c == 0, stop=c == DC - 1)
                        last.then_inc(sg("up_full"), 1)
                if i + 1 < TILES:
                    rows_t(i + 1)
                if i:
                    pe.wait_ge(sg("hT"), FT * i)
                    if i >= 3:
                        pe.wait_ge(sg("y"), i - 2)
                    for f in range(FT):
                        last = mm(ps[4 + (i - 1) % 2][:, 0:D], hT[:, (i - 1) % 2, f, :],
                                  w2[:, bass.ds(last_expert, 1), f, :], start=f == 0, stop=f == FT - 1)
                    last.then_inc(sg("down_full"), 1)
                if i < TILES:
                    for h in range(2):
                        pe.wait_ge(sg("raw"), 2 * i + h + 1)
                        for k in range(KH):
                            last = tr(ps[2 + h][:, k * P:(k + 1) * P], raw[:, h, k * P:(k + 1) * P], ident[:, :])
                        last.then_inc(sg("hT_full"), 1)

        @block.scalar
        def _(act):
            sc = nc.scalar
            act.wait_ge(sg("b1_full"), 1)
            sc.copy(b1c[:, :], ps[6][:, 0:E * FT]).then_inc(sg("b1"), 1)
            for g in range(NG):
                if g >= 2:
                    act.wait_ge(sg("scores_full"), g - 1)
                for c in range(DC):
                    act.wait_ge(sg("xT_full"), DC * g + c + 1)
                    sc.copy(xTr[:, g % 2, c, :], ps[g % 2 * 2 + c][:, :]).then_inc(sg("xT"), 1)
            act.wait_ge(sg("shifted"), 1)
            sc.activation(pr[:, :, :], lo[:, :, :], ACT.Exp).then_inc(sg("exps"), 1)
            act.wait_ge(sg("two"), 1)
            sc.activation(dd[:, :], m2[:, :], ACT.Exp).then_inc(sg("exps"), 1)

            def rows_in(i):
                act.wait_ge(sg("xt_full"), i + 1)
                if i >= 2:
                    act.wait_ge(sg("up_full"), 2 * (i - 1))
                sc.copy(xtT[:, i % 2, :, :], ps[6 + i % 2][:, 0:D].rearrange("p (c t) -> p c t", c=DC))\
                    .then_inc(sg("xtT"), 1)

            rows_in(0)
            act.wait_ge(sg("te"), 1)
            act.wait_ge(sg("b1"), 1)
            for i in range(TILES):
                if i + 1 < TILES:
                    rows_in(i + 1)
                expert = act.value_load(te[0:1, i:i + 1], min_val=0, max_val=E - 1)
                if i >= 2:
                    act.wait_ge(sg("down_full"), i - 1)
                for f in range(FT):
                    if f % KH == 0:
                        act.wait_ge(sg("hT_full"), 2 * i + f // KH + 1)
                    sc.activation(hT[:, i % 2, f, :], ps[2 + f // KH][:, f % KH * P:(f % KH + 1) * P], ACT.Relu,
                                  bias=b1c[:, bass.ds(expert * FT + f, 1)]).then_inc(sg("hT"), 1)

        @block.vector
        def _(dve):
            v = nc.vector
            s = Counted(dve, sg("dve_steps"))
            shape = [P, NTB, E]

            def over(ap):
                return ap.unsqueeze(2).to_broadcast(shape)

            dve.wait_ge(sg("small"), 48)
            dve.wait_ge(sg("constants"), 4)
            dve.wait_ge(sg("scores_full"), NG)
            s.step(v.tensor_tensor(lo[:, :, :], ps[4][:, 0:NTB * E].rearrange("p (t e) -> p t e", e=E),
                                   bg[:, :].unsqueeze(1).to_broadcast(shape), ALU.add))
            s.step(v.tensor_reduce(m1[:, :], lo[:, :, :], AX.X, ALU.max))
            v.tensor_tensor(lo[:, :, :], lo[:, :, :], over(m1[:, :]), ALU.subtract).then_inc(sg("shifted"), 1)
            dve.wait_ge(sg("exps"), 1)
            s.step(v.tensor_reduce(m1[:, :], pr[:, :, :], AX.X, ALU.add))
            s.step(v.reciprocal(m1[:, :], m1[:, :]))
            s.step(v.tensor_tensor(pr[:, :, :], pr[:, :, :], over(m1[:, :]), ALU.mult))
            for m, oh in ((m1, oh1), (m2, oh2)):
                s.step(v.tensor_reduce(m[:, :], pr[:, :, :], AX.X, ALU.max))
                s.step(v.tensor_tensor(eq[:, :, :], pr[:, :, :], over(m[:, :]), ALU.is_equal))
                s.step(v.tensor_tensor(eq[:, :, :], eq[:, :, :], rank[:, :].unsqueeze(1).to_broadcast(shape),
                                       ALU.mult))
                s.step(v.tensor_reduce(ix[:, :], eq[:, :, :], AX.X, ALU.min))
                s.step(v.tensor_tensor(oh[:, :, :], rank[:, :].unsqueeze(1).to_broadcast(shape), over(ix[:, :]),
                                       ALU.is_equal))
                s.step(v.scalar_tensor_tensor(pr[:, :, :].rearrange("p t e -> p (t e)"),
                                              oh[:, :, :].rearrange("p t e -> p (t e)"), -4.0,
                                              pr[:, :, :].rearrange("p t e -> p (t e)"), ALU.mult, ALU.add))
            v.tensor_tensor(both[:, :, :], oh1[:, :, :], oh2[:, :, :], ALU.add).then_inc(sg("both"), 1)
            v.tensor_tensor(m2[:, :], m2[:, :], m1[:, :], ALU.subtract).then_inc(sg("two"), 1)
            dve.wait_ge(sg("exps"), 2)
            s.step(v.tensor_scalar(m1[:, :], dd[:, :], 1.0, None, ALU.add))
            s.step(v.reciprocal(m1[:, :], m1[:, :]))
            s.mark(v.tensor_tensor(dd[:, :], dd[:, :], m1[:, :], ALU.mult))
            dve.wait_ge(sg("counts_full"), 1)
            inside = ps[5][:, 0:NTB * E].rearrange("p (t e) -> p t e", e=E)
            total = ps[5][:, NTB * E:2 * NTB * E].rearrange("p (t e) -> p t e", e=E)
            s.step(v.tensor_copy(sa[:, :, :], total))
            src, dst = sa, sc_
            for d in (1, 2, 4, 8):
                s.mark(v.tensor_copy(dst[:, 0:d, :], src[:, 0:d, :]))
                s.step(v.tensor_tensor(dst[:, d:, :], src[:, d:, :], src[:, 0:NTB - d, :], ALU.add))
                src, dst = dst, src
            s.step(v.tensor_scalar(cnti[:, :], src[:, NTB - 1, :], float(P - 1), None, ALU.add))
            s.step(v.tensor_scalar(cnti[:, :], cnti[:, :], P.bit_length() - 1, None, ALU.logical_shift_right))
            s.step(v.tensor_copy(cnt[:, :], cnti[:, :]))
            s.step(v.tensor_copy(cum[:, :], cnt[:, :]))
            a, b = cum, cum2
            for d in (1, 2, 4):
                s.mark(v.tensor_copy(b[:, 0:d], a[:, 0:d]))
                s.step(v.tensor_tensor(b[:, d:], a[:, d:], a[:, 0:E - d], ALU.add))
                a, b = b, a
            s.step(v.tensor_tensor(cnt[:, :], a[:, :], cnt[:, :], ALU.subtract))
            s.step(v.tensor_scalar(cnt[:, :], cnt[:, :], float(P), None, ALU.mult))
            s.step(v.tensor_tensor(src[:, :, :], src[:, :, :], total, ALU.subtract))
            s.step(v.tensor_tensor(src[:, :, :], src[:, :, :], inside, ALU.add))
            s.step(v.tensor_tensor(src[:, :, :], src[:, :, :], cnt[:, :].unsqueeze(1).to_broadcast(shape), ALU.add))
            for k, oh in enumerate((oh1, oh2)):
                s.step(v.tensor_tensor(oh[:, :, :], oh[:, :, :], src[:, :, :], ALU.mult))
                s.step(v.tensor_reduce(slotf[:, k, :], oh[:, :, :], AX.X, ALU.add))
            v.tensor_copy(slot[:, :, :], slotf[:, :, :]).then_inc(sg("slots"), 1)
            s.step(v.tensor_tensor(past[:, :, :], a[0:1, :].unsqueeze(1).to_broadcast([1, TILES, E]),
                                   tile_no[:, :, :], ALU.is_le))
            s.step(v.tensor_reduce(tef[:, :], past[:, :, :], AX.X, ALU.add))
            s.step(v.tensor_scalar(tef[:, :], tef[:, :], float(E - 1), None, ALU.min))
            v.tensor_copy(te[:, :], tef[:, :]).then_inc(sg("te"), 1)
            dve.wait_ge(sg("te"), 1)
            dve.wait_ge(sg("w_in"), 16 * (2 * E + 1))
            for i in range(TILES + 1):
                if i < TILES:
                    for h in range(2):
                        dve.wait_ge(sg("up_full"), 2 * i + h + 1)
                        if i:
                            dve.wait_ge(sg("hT_full"), 2 * (i - 1) + h + 1)
                        v.tensor_copy(raw[:, h, :], ps[h][:, :]).then_inc(sg("raw"), 1)
                if i:
                    j = i - 1
                    expert = dve.value_load(te[0:1, j:j + 1], min_val=0, max_val=E - 1)
                    dve.wait_ge(sg("down_full"), i)
                    if j >= 2:
                        dve.wait_ge(sg(f"y_out{j % 2}"), 16 * (j // 2))
                    v.tensor_tensor(y[:, j % 2, :], ps[4 + j % 2][:, 0:D], b2b[:, bass.ds(expert, 1), :]
                                    .rearrange("p o d -> p (o d)"), ALU.add).then_inc(sg("y"), 1)
            for tb in range(NTB):
                dve.wait_ge(sg(f"pair_in{tb % GR}"), 32 * (tb // GR + 1))
                s.step(v.scalar_tensor_tensor(acc[:, tb, :], pair[:, tb % GR, 0, :], m1[:, tb:tb + 1],
                                              acc[:, tb, :], ALU.mult, ALU.add))
                s.step(v.scalar_tensor_tensor(acc[:, tb, :], pair[:, tb % GR, 1, :], dd[:, tb:tb + 1],
                                              acc[:, tb, :], ALU.mult, ALU.add))
                dve.sem_inc(sg("combined"), 1)
                s.mark(v.bn_stats(stats[:, tb, :], acc[:, tb, :]))
                if tb % GRP == GRP - 1:
                    g = slice(tb - GRP + 1, tb + 1)
                    s.sync()
                    for k in range(g.start, g.stop):
                        s.mark(v.bn_aggr(mv[:, k, :], stats[:, k, :]))
                    s.sync()
                    x_, y_, a_ = (r[:, :] for r in rs)
                    s.step(v.tensor_scalar(x_, mv[:, g, 1], LN_EPS, None, ALU.add))
                    rsqrt_steps(s, v, x_, y_, a_)
                    for k in range(g.start, g.stop):
                        v.tensor_scalar(acc[:, k, :], acc[:, k, :], mv[:, k, 0:1], rs[1][:, k % GRP:k % GRP + 1],
                                        ALU.subtract, ALU.mult).then_inc(sg("normed"), 1)
                    dve.wait_ge(sg("normed"), g.stop)


def two_layers(nc, io, out):
    h0 = nc.dram_tensor("h0", (B, T, D), fp32).ap()
    x3 = nc.dram_tensor("x3", (B, T, D), fp32).ap()
    TOP, E = 2, 8
    slots = ((TOP * B * T + E * (P - 1)) // P) * P
    xs = nc.dram_tensor("x_slots", (slots, D), fp32).ap()
    ys = nc.dram_tensor("y_slots", (slots, D), fp32).ap()
    with ExitStack() as whole:
        ident = whole.enter_context(nc.sbuf_tensor("ident", [P, P], fp32))
        with ExitStack() as ctx:
            s4_tokens(nc, ctx, whole, io["x"], io["L0_tok_log_dt"], io["L0_tok_inv_A_real"], io["L0_tok_A_imag"],
                      io["L0_tok_B_ri"], h0, ident, xs)
        with ExitStack() as ctx:
            main_loop(nc, ctx, whole, io, h0, x3, ident)
        with ExitStack() as ctx:
            expert_mixture(nc, ctx, io, x3, xs, ys, out, ident)


_UNUSED = ("L0_ffn_gate_w",)


def kernel(**inputs):
    import concourse.bacc as bacc
    from concourse.bass_utils import run_bass_kernel_spmd

    nc = bacc.Bacc("TRN2", target_bir_lowering=False, num_devices=1)
    arrays, io = {}, {}
    for name, value in inputs.items():
        if name in _UNUSED:
            continue
        a = np.ascontiguousarray(value)
        if name == "L0_tok_log_dt":
            a = np.ascontiguousarray(a.reshape(T // P, P).T)
        arrays[f"in_{name}"] = a
        io[name] = nc.dram_tensor(f"in_{name}", a.shape, mybir.dt.from_np(a.dtype), kind="ExternalInput").ap()
    out = nc.dram_tensor("out_h", (B, T, D), fp32, kind="ExternalOutput").ap()
    two_layers(nc, io, out)
    return run_bass_kernel_spmd(nc, [arrays], core_ids=[0]).results[0]["out_h"]
```

```python
import numpy as np
from contextlib import ExitStack
import concourse.bass as bass
from concourse import mybir

fp32 = mybir.dt.float32
f32r = mybir.dt.float32r
bf16 = mybir.dt.bfloat16
i32 = mybir.dt.int32
u32 = mybir.dt.uint32
ALU = mybir.AluOpType
ACT = mybir.ActivationFunctionType
AX = mybir.AxisListType

P = 128
B, T, D = 8, 256, 256
N_STATE = 64
DC = D // P
LN_EPS = 1e-5
NEG = -1e30


class Counted:

    def __init__(self, eng, sem):
        self.eng, self.sem, self.n = eng, sem, 0

    def mark(self, ins):
        self.n += 1
        ins.then_inc(self.sem, 1)
        return ins

    def step(self, ins):
        self.mark(ins)
        self.eng.wait_ge(self.sem, self.n)

    def sync(self):
        if self.n:
            self.eng.wait_ge(self.sem, self.n)


class Weights:

    def __init__(self, nc, ctx, whole, io):
        def sb(name, shape):
            return ctx.enter_context(nc.sbuf_tensor(name, shape, fp32))

        def rows_view(ap):
            return ap.rearrange("(c p) n -> p c n", p=P)

        self.loaded = whole.enter_context(nc.semaphore("weights_loaded"))
        self.wqkv0 = sb("wqkv0", [P, DC, 3 * D])
        self.wout0 = sb("wout0", [P, DC, D])
        self.wq1, self.wk1, self.wv1, self.wo1 = (sb(n, [P, DC, D]) for n in ("wq1", "wk1", "wv1", "wo1"))
        self.gwq, self.gwk = sb("gwq", [P, DC, P]), sb("gwk", [P, DC, P])
        self.gwvg = sb("gwvg", [P, DC, 2 * D])
        self.gwgk1, self.gwgk2 = sb("gwgk1", [P, DC, 16]), sb("gwgk2", [16, P])
        self.gwo = sb("gwo", [P, DC, D])
        self.bgk = sb("bgk", [P, 1])
        self.gwb = sb("gwb", [P, 64])
        self.lng, self.lnb = sb("lng", [P, D]), sb("lnb", [P, D])
        self.dirs, self.hsc = sb("dirs", [P, 8, 3]), sb("hsc", [P, 8])
        self.loads = []

        def w_in(dst, src):
            self.loads.append((dst, src))

        w_in(self.wqkv0[:, :, :], rows_view(io["L0_attn_Wqkv"]))
        w_in(self.dirs[:, :, :].rearrange("p h d -> p (h d)"),
             io["L0_attn_head_dirs"].rearrange("h d -> (h d)").partition_broadcast(P))
        w_in(self.hsc[:, :], io["L0_attn_head_scales"].partition_broadcast(P))
        w_in(self.wout0[:, :, :], rows_view(io["L0_attn_Wout"]))
        for dst, n in ((self.wq1, "wq"), (self.wk1, "wk"), (self.wv1, "wv"), (self.wo1, "wo")):
            w_in(dst[:, :, :], rows_view(io[f"L0_ffn_{n}"]))
        w_in(self.lng[:, :], io["L0_ffn_ln_g"].partition_broadcast(P))
        w_in(self.lnb[:, :], io["L0_ffn_ln_b"].partition_broadcast(P))
        w_in(self.gwq[:, :, :], rows_view(io["L1_attn_Wq"]))
        w_in(self.gwk[:, :, :], rows_view(io["L1_attn_Wk"]))
        w_in(self.gwvg[:, :, 0:D], rows_view(io["L1_attn_Wv"]))
        w_in(self.gwvg[:, :, D:], rows_view(io["L1_attn_Wg"]))
        w_in(self.gwgk1[:, :, :], rows_view(io["L1_attn_Wgk1"]))
        w_in(self.gwgk2[:, :], io["L1_attn_Wgk2"])
        w_in(self.gwo[:, :, :], rows_view(io["L1_attn_Wo"]))
        w_in(self.bgk[:, :], io["L1_attn_bgk2"].rearrange("(p o) -> p o", o=1))
        w_in(self.gwb[:, :], io["L1_attn_gw"].partition_broadcast(P))


def s4_tokens(nc, ctx, whole, x, log_dt, inv_a_real, a_imag, b_ri, h0, ident, xs, weights):
    CH, HF, NB, NA = B, T // P, 64, 4
    HP, NG = P, 4
    GT = HP // NG
    M = CH * NA
    J = P // M
    TI = GT // J

    def sb(name, shape, dt=fp32):
        return ctx.enter_context(nc.sbuf_tensor(name, shape, dt))

    xin = sb("s4_x", [P, HF, CH, N_STATE, 2])
    bin_ = sb("s4_b", [P, HF, N_STATE, 2])
    ea = sb("s4_ea", [P, 2 + HF * N_STATE])
    ex = [sb(f"s4_ex{i}", [P, 2 + HF * N_STATE]) for i in range(3)]
    exi = sb("s4_exi", [P, 2 + HF * N_STATE], i32)
    aim = sb("s4_aim", [P, HF, N_STATE])
    q = [sb(f"s4_q{i}", [P, HF, N_STATE]) for i in range(5)]
    da = sb("s4_da", [P, 2, HF, N_STATE])
    cb = sb("s4_cb", [P, 2, CH, HF, N_STATE])
    ct = [sb(f"s4_ct{i}", [P, HF, CH, N_STATE]) for i in range(2)]
    dat = sb("s4_dat", [P, 2, HP])
    cbt = sb("s4_cbt", [P, 2, CH, HP])
    pw = [sb(f"s4_pw{i}", [P, 2, GT, NB]) for i in range(2)]
    cs = [sb(f"s4_cs{i}", [P, 2, GT, CH, NA]) for i in range(2)]
    csn = [sb(f"s4_csn{i}", [P, GT, CH, NA]) for i in range(2)]
    dk = [sb(f"s4_dk{i}", [P, 2, HP]) for i in range(8)]
    dk2 = sb("s4_sq", [P, HP])
    t1, t2 = sb("s4_t1", [P, 2, GT, NB // 2]), sb("s4_t2", [P, 2, GT, NB // 2])
    pt1, pt2 = sb("s4_pt1", [P, 2, GT, 2 * CH]), sb("s4_pt2", [P, 2, GT, 2 * CH])
    out = [sb(f"s4_out{i}", [P, TI, NB]) for i in range(4)]
    ps = [ctx.enter_context(nc.psum_tensor(f"s4_ps{i}", [P, 512], fp32)) for i in range(8)]

    def sem(n):
        return whole.enter_context(nc.semaphore(n))

    zero = sb("s4_zero", [P, D])
    loaded, x_loaded, zeroed, doubled = (sem(f"s4_{n}") for n in ("loaded", "x_loaded", "zeroed", "doubled"))
    prepared, transposed, columns = sem("s4_prepared"), sem("s4_transposed"), sem("s4_columns")
    squares, powers, strides, negated = (sem(f"s4_{n}") for n in ("squares", "powers", "strides", "negated"))
    banks_full, copied = sem("s4_banks_full"), sem("s4_copied")
    stored = [sem(f"s4_stored{i}") for i in range(4)]
    steps, psteps, constants = sem("s4_steps"), sem("s4_psteps"), sem("s4_constants")
    NLOAD = 4
    NT = 2 + 2 * CH

    xr, xi = xin[:, :, :, :, 0], xin[:, :, :, :, 1]
    shape = [P, HF, CH, N_STATE]
    br, bi = (bin_[:, :, :, i].unsqueeze(2).to_broadcast(shape) for i in range(2))

    def cb_part(i):
        return cb[:, i].rearrange("p c f n -> p f c n")

    def cmul(v, s, temps, dst, src, d, n):
        shp = [P, GT] + n
        dr, di = d[:, 0, :], d[:, 1, :]
        for _ in n:
            dr, di = dr.unsqueeze(len(dr.shape)), di.unsqueeze(len(di.shape))
        dr, di = dr.to_broadcast(shp), di.to_broadcast(shp)
        size = 1
        for k in n:
            size *= k
        u, w = ([t[:, i, :, 0:size] for i in range(2)] for t in temps)
        if len(n) > 1:
            u = [z.rearrange("p t (a c) -> p t a c", a=n[0]) for z in u]
            w = [z.rearrange("p t (a c) -> p t a c", a=n[0]) for z in w]
        s.mark(v.tensor_tensor(u[0], src[0], dr, ALU.mult))
        s.mark(v.tensor_tensor(w[0], src[1], di, ALU.mult))
        s.mark(v.tensor_tensor(u[1], src[0], di, ALU.mult))
        s.step(v.tensor_tensor(w[1], src[1], dr, ALU.mult))
        s.mark(v.tensor_tensor(dst[0], u[0], w[0], ALU.subtract))
        s.step(v.tensor_tensor(dst[1], u[1], w[1], ALU.add))

    with nc.Block() as block:
        @block.sync
        def _(sp):
            sp.dma_start(ea[:, 0:HF], log_dt).then_inc(loaded, 16)
            sp.dma_start(ea[:, HF:].rearrange("p (f n) -> p f n", f=HF),
                         inv_a_real.rearrange("(f p) n -> p f n", p=P)).then_inc(loaded, 16)
            sp.dma_start(aim[:, :, :], a_imag.rearrange("(f p) n -> p f n", p=P)).then_inc(loaded, 16)
            sp.dma_start(bin_[:, :, :, :], b_ri.rearrange("(f p) n r -> p f n r", p=P)).then_inc(loaded, 16)
            for f in range(HF):
                sp.dma_start(xin[:, f].rearrange("p c n r -> p c (n r)"),
                             x[:, f * P:(f + 1) * P].rearrange("c p n r -> p c (n r)")).then_inc(x_loaded, 16)
            for dst, src in weights.loads:
                sp.dma_start(dst, src).then_inc(weights.loaded, 16)
            for n in range(HF * NG):
                g, f = n // HF, n % HF
                sp.wait_ge(copied, n + 1)
                for j in range(J):
                    t0 = f * P + g * GT + j * TI
                    sp.dma_start(h0[t0:t0 + TI].rearrange("t c (a b) -> (c a) t b", b=NB),
                                 out[n % 4][j * M:(j + 1) * M, :, :]).then_inc(stored[n % 4], 16)
            for k in range(4):
                sp.wait_ge(stored[k], 16 * J * NG * HF // 4)

        @block.gpsimd
        def _(pool):
            nc.gpsimd.memset(ident[:, :], 0.0).then_inc(constants, 1)
            pool.wait_ge(constants, 1)
            nc.gpsimd.affine_select(out=ident[:, :], in_=ident[:, :], compare_op=ALU.not_equal, fill=1.0,
                                    base=0, pattern=[[-1, P]], channel_multiplier=1).then_inc(constants, 1)
            g_ = nc.gpsimd
            s = Counted(pool, psteps)
            pool.wait_ge(loaded, 16 * NLOAD)
            g_.tensor_scalar(bin_[:, :, :, :], bin_[:, :, :, :], 2.0, None, ALU.mult).then_inc(doubled, 1)
            pool.wait_ge(doubled, 1)
            pool.wait_ge(x_loaded, 16 * HF)
            s.mark(g_.tensor_tensor(cb_part(0), xr, br, ALU.mult))
            s.step(g_.tensor_tensor(ct[0][:, :, :, :], xi, bi, ALU.mult))
            g_.tensor_tensor(cb_part(0), cb_part(0), ct[0][:, :, :, :], ALU.subtract).then_inc(prepared, 1)

            nc.gpsimd.memset(zero[:, :], 0.0).then_inc(constants, 1)
            pool.wait_ge(constants, 3)
            rows = xs.shape[0] // P
            pool.dma_start(xs.rearrange("(p r) d -> p r d", p=P),
                           zero[:, :].unsqueeze(1).to_broadcast([P, rows, D])).then_inc(zeroed, 16)
            pool.wait_ge(columns, 5)
            pool.wait_ge(squares, 1)
            for g in range(NG):
                cg, tok = cs[g % 2], slice(g * GT, (g + 1) * GT)
                if g >= 2:
                    pool.wait_ge(banks_full, g - 1)
                    pool.wait_ge(negated, g - 1)
                for i in range(2):
                    s.step(g_.tensor_copy(cg[:, i, :, :, 0], cbt[:, i, :, tok].rearrange("p c t -> p t c")))
                cmul(g_, s, (pt1, pt2), [cg[:, i, :, :, 1] for i in range(2)], [cg[:, i, :, :, 0] for i in range(2)],
                     dk[6][:, :, tok], [CH])
                cmul(g_, s, (pt1, pt2), [cg[:, i, :, :, 2:4] for i in range(2)],
                     [cg[:, i, :, :, 0:2] for i in range(2)], dk[7][:, :, tok], [CH, 2])
                pool.sem_inc(strides, 1)
            pool.wait_ge(zeroed, 16)

        @block.vector
        def _(dve):
            s = Counted(dve, steps)
            v = nc.vector
            dve.wait_ge(loaded, 16 * NLOAD)
            y, r, kf = ex
            s.step(v.tensor_scalar(y[:, :], ea[:, :], -87.0, 88.0, ALU.max, ALU.min))
            s.step(v.tensor_scalar(exi[:, :], y[:, :], 1.4426950408889634, None, ALU.mult))
            s.step(v.tensor_copy(kf[:, :], exi[:, :]))
            s.step(v.scalar_tensor_tensor(r[:, :], kf[:, :], -0.693359375, y[:, :], ALU.mult, ALU.add))
            s.step(v.scalar_tensor_tensor(r[:, :], kf[:, :], 2.12194440e-4, r[:, :], ALU.mult, ALU.add))
            s.step(v.tensor_scalar(y[:, :], r[:, :], 1 / 5040, None, ALU.mult))
            for c in (1 / 720, 1 / 120, 1 / 24, 1 / 6, 1 / 2, 1.0):
                s.step(v.scalar_tensor_tensor(y[:, :], y[:, :], c, r[:, :], ALU.add, ALU.mult))
            s.step(v.tensor_scalar(exi[:, :], kf[:, :], 127.0, float(1 << 23), ALU.add, ALU.mult))
            s.step(v.scalar_tensor_tensor(ea[:, :], y[:, :], 1.0, exi[:, :].bitcast(fp32), ALU.add, ALU.mult))
            a, b, m, dn, w = q
            for f in range(HF):
                s.mark(v.tensor_scalar(a[:, f, :], ea[:, HF + f * N_STATE:HF + (f + 1) * N_STATE],
                                       ea[:, f:f + 1], -0.5, ALU.mult, ALU.mult))
                s.mark(v.tensor_scalar(b[:, f, :], aim[:, f, :], ea[:, f:f + 1], 0.5, ALU.mult, ALU.mult))
            s.sync()
            s.mark(v.tensor_tensor(m[:, :, :], b[:, :, :], b[:, :, :], ALU.mult))
            s.step(v.tensor_scalar(dn[:, :, :], a[:, :, :], -1.0, 1.0, ALU.mult, ALU.add))
            s.mark(v.tensor_tensor(dn[:, :, :], dn[:, :, :], dn[:, :, :], ALU.mult))
            s.step(v.tensor_tensor(w[:, :, :], a[:, :, :], a[:, :, :], ALU.mult))
            s.mark(v.tensor_tensor(dn[:, :, :], dn[:, :, :], m[:, :, :], ALU.add))
            s.step(v.tensor_tensor(w[:, :, :], w[:, :, :], m[:, :, :], ALU.add))
            s.mark(v.reciprocal(dn[:, :, :], dn[:, :, :]))
            s.step(v.tensor_scalar(w[:, :, :], w[:, :, :], -1.0, 1.0, ALU.mult, ALU.add))
            s.mark(v.tensor_tensor(da[:, 0, :, :], w[:, :, :], dn[:, :, :], ALU.mult))
            s.mark(v.scalar_tensor_tensor(da[:, 1, :, :], b[:, :, :], 2.0, dn[:, :, :], ALU.mult, ALU.mult))
            dve.wait_ge(doubled, 1)
            dve.wait_ge(x_loaded, 16 * HF)
            s.mark(v.tensor_tensor(cb_part(1), xr, bi, ALU.mult))
            s.step(v.tensor_tensor(ct[1][:, :, :, :], xi, br, ALU.mult))
            s.step(v.tensor_tensor(cb_part(1), cb_part(1), ct[1][:, :, :, :], ALU.add))
            dve.sem_inc(prepared, 1)
            dve.wait_ge(columns, 5)
            s.step(v.tensor_copy(dk[0][:, :, :], dat[:, :, :]))
            for k in range(7):
                cur, nxt = dk[k], dk[k + 1]
                s.mark(v.tensor_tensor(dk2[:, :], cur[:, 1, :], cur[:, 1, :], ALU.mult))
                s.step(v.tensor_tensor(nxt[:, 0, :], cur[:, 0, :], cur[:, 0, :], ALU.mult))
                s.mark(v.tensor_tensor(nxt[:, 0, :], nxt[:, 0, :], dk2[:, :], ALU.subtract))
                s.step(v.scalar_tensor_tensor(nxt[:, 1, :], cur[:, 0, :], 2.0, cur[:, 1, :], ALU.mult, ALU.mult))
            dve.sem_inc(squares, 1)
            for g in range(NG):
                pg = pw[g % 2]
                if g >= 2:
                    dve.wait_ge(banks_full, g - 1)
                s.mark(v.memset(pg[:, 0, :, 0:1], 1.0))
                s.step(v.memset(pg[:, 1, :, 0:1], 0.0))
                for k in range(6):
                    n = 1 << k
                    cmul(v, s, (t1, t2), [pg[:, i, :, n:2 * n] for i in range(2)],
                         [pg[:, i, :, 0:n] for i in range(2)], dk[k][:, :, g * GT:(g + 1) * GT], [n])
                dve.sem_inc(powers, 1)

        @block.scalar
        def _(act):
            for k in range(5):
                act.wait_ge(transposed, k + 1)
                for i in range(4 if k < 4 else 2):
                    n = 4 * k + i
                    dst = cbt[:, n // CH, n % CH, :] if n < 2 * CH else dat[:, n - 2 * CH, :]
                    last = nc.scalar.copy(dst, ps[k][:, i * P:(i + 1) * P])
                last.then_inc(columns, 1)

            def negate(g):
                act.wait_ge(strides, g + 1)
                if g >= 2:
                    act.wait_ge(banks_full, g - 1)
                nc.scalar.mul(csn[g % 2][:, :, :, :], cs[g % 2][:, 1], -1.0).then_inc(negated, 1)

            negate(0)
            for g in range(NG):
                if g + 1 < NG:
                    negate(g + 1)
                act.wait_ge(banks_full, g + 1)
                for f in range(HF):
                    n = HF * g + f
                    if n >= 4:
                        act.wait_ge(stored[n % 4], 16 * J * (n // 4))
                    nc.scalar.copy(out[n % 4][:, :, :], ps[n][:, :].rearrange("p (t b) -> p t b", b=NB))\
                        .then_inc(copied, 1)

        @block.tensor
        def _(pe):
            pe.wait_ge(prepared, 2)
            pe.wait_ge(constants, 2)
            for n in range(NT):
                src = cb[:, n // CH, n % CH] if n < 2 * CH else da[:, n - 2 * CH]
                last = nc.tensor.transpose(ps[n // 4][:, (n % 4) * P:(n % 4 + 1) * P],
                                           src.rearrange("p f n -> p (f n)"), ident[:, :])
                if n % 4 == 3 or n == NT - 1:
                    last.then_inc(transposed, 1)
            pe.wait_ge(columns, 5)
            for g in range(NG):
                pe.wait_ge(powers, g + 1)
                pe.wait_ge(negated, g + 1)
                for i in range(TI):
                    for part in range(2):
                        for j in range(J):
                            t = j * TI + i
                            for f in range(HF):
                                rows = slice(64 * f, 64 * f + 64)
                                lhs = csn[g % 2][rows, t] if part else cs[g % 2][rows, 0, t]
                                last = nc.tensor.matmul(
                                    ps[HF * g + f][j * M:(j + 1) * M, i * NB:(i + 1) * NB],
                                    lhs.rearrange("p c a -> p (c a)"), pw[g % 2][rows, part, t, :],
                                    start=part == 0, stop=part == 1)
                last.then_inc(banks_full, 1)


class Signals:

    def __init__(self, nc, ctx, prefix):
        self.nc, self.ctx, self.prefix, self.all = nc, ctx, prefix, {}

    def __call__(self, name):
        if name not in self.all:
            self.all[name] = self.ctx.enter_context(self.nc.semaphore(f"{self.prefix}_{name}"))
        return self.all[name]

    def runs(self):
        numbers = sorted(x.num for x in self.all.values())
        starts = [n for n in numbers if n - 1 not in numbers]
        ends = [n + 1 for n in numbers if n + 1 not in numbers]
        return [range(a, b) for a, b in zip(starts, ends)]


def rsqrt_steps(s, v, x, y, a):
    s.step(v.tensor_scalar(y.bitcast(i32), x.bitcast(i32), 1, None, ALU.logical_shift_right))
    s.step(v.tensor_scalar(y.bitcast(i32), y.bitcast(i32), -1.0, float(0x5F3759DF), ALU.mult, ALU.add))
    for _ in range(3):
        s.step(v.scalar_tensor_tensor(a, y, -0.5, y, ALU.mult, ALU.mult))
        s.step(v.tensor_tensor(a, a, x, ALU.mult))
        s.step(v.scalar_tensor_tensor(y, a, 1.5, y, ALU.add, ALU.mult))


class Attention:

    RING = 4

    def __init__(self, name, heads, dim, causal):
        self.name, self.heads, self.dim, self.causal = name, heads, dim, causal
        self.rows = 4 * dim
        self.lanes = P // (2 * self.rows) or 1
        self.slots = 4
        self.group = self.lanes * self.slots
        self.per_batch = heads // self.group
        self.groups = 2 * self.per_batch
        self.vw = 32 if dim < 32 else 64
        self.quad = P // self.vw
        self.units = self.groups * self.group

    def lane_slot(self, n):
        return n // self.slots, n % self.slots

    def due(self, u, lag):
        end = u - lag
        return [end // self.quad] if 0 <= end < self.units and end % self.quad == self.quad - 1 else []


AV_LAG = 2
OUT_LAG = AV_LAG + 2
NORM_LAG = OUT_LAG + 1
PT_RING = 8
WARM = {"a0_stack": 40, "a1_stack": 40, "h2_t": 40, "g_qk": 35, "p2_t": 30}


def main_loop(nc, ctx, whole, io, h0, x3, ident, weights):
    NTB = 4
    TOK = NTB * P
    PAIRS = B // 2
    F = 1024
    FT = F // P
    E_IT = 2
    NHG, DK, DV = 4, 32, 64
    att0 = Attention("a0", 8, 32, True)
    att1 = Attention("a1", 32, 8, False)

    def sb(name, shape, dt=fp32, c=ctx):
        return c.enter_context(nc.sbuf_tensor(name, shape, dt))

    def dram(name, shape):
        return nc.dram_tensor(name, shape, fp32).ap()

    wt = weights
    gp, gq = sb("gp", [P, DC, 8, 3]), sb("gq", [P, DC, 8])
    identb = sb("identb", [P, P], bf16)
    mask_s, mask_t = sb("mask_s", [P, 3 * P], bf16), sb("mask_t", [P, 3 * P], bf16)
    mask_g = sb("mask_g", [P, P])
    ones2 = sb("ones2", [2, P], f32r)
    onesr = sb("onesr", [P, T])
    ha, hb, yb, ob, vb = (sb(n, [P, NTB, D]) for n in ("ha", "hb", "yb", "ob", "vb"))
    tt = sb("tt", [P, DC, TOK])
    stats, mv = sb("stats", [P, NTB, 6]), sb("mv", [P, NTB, 2])
    rs = [sb(f"rs{i}", [P, 16]) for i in range(3)]
    w1, w2 = sb("w1", [P, E_IT, DC, F]), sb("w2", [P, E_IT, FT, D])
    b1r, b1c = sb("b1r", [E_IT * FT, P]), sb("b1c", [P, E_IT * FT])
    b2b = sb("b2b", [P, E_IT, D])
    kst = sb("kst", [P, 4, 4, T], f32r)
    vpad = {a.name: sb(f"vpad_{a.name}", [P, 2, 2, a.group, a.vw]) for a in (att0, att1)}
    mx = sb("mx", [P, 2, 2, 8])
    rc = sb("rc", [P, 8])
    rows_hl = sb("rows_hl", [8, 2, 2, T], f32r)
    acc = [sb(f"acc{i}", [P, T]) for i in range(2)]
    sd = sb("sd", [P, 2, D])
    shared = ExitStack()
    hl = {k: sb(k, [P, 2, TOK], f32r, shared) for k in ("q_hi", "q_lo", "k_hi", "k_lo")}
    qst = sb("qst", [P, 4, 4, T], f32r, shared)
    mrow = sb("mrow", [2, 3, 4, T], f32r, shared)
    pt = [sb(f"pt{i}", [P, 2 * T], fp32, shared) for i in range(PT_RING)]
    shared.close()
    sb("parts_kept", [P, 3, 2, TOK], f32r, shared)
    q1 = sb("q1", [P, 4, 2, 4, T], f32r, shared)
    shared.close()
    hid = sb("hid", [P, E_IT, FT, T])
    qs, ks = sb("qs", [P, TOK]), sb("ks", [P, TOK])
    gz, gm, ge, gG = (sb(n, [P, TOK]) for n in ("gz", "gm", "ge", "gG"))
    u1 = sb("u1", [16, TOK])
    atm = sb("atm", [P, NHG, NTB, P])
    kT = sb("kT", [P, 2, P])
    dr = sb("dr", [P, 2])
    gb = sb("gb", [P, NTB, D])
    ps = [ctx.enter_context(nc.psum_tensor(f"ps{i}", [P, 512], fp32)) for i in range(8)]
    xs = {a.name: {k: dram(f"{a.name}_{k}_parts", (a.heads, 4, a.dim, TOK)) for k in "qk"} for a in (att0, att1)}

    sg = Signals(nc, ctx, "m")
    once = Signals(nc, whole, "w")
    done, go = once("done"), {k: once(f"go_{k}") for k in ("sp", "pe", "act", "pool")}

    constants, ready = once("constants"), once("ready")
    pair_io = once("pair_io")

    def pair_ready(j):
        return 64 * j + 32


    MAX_ROW = 96

    def q1_at(g, lane):
        return q1[:, 3 - g % 4, lane]

    block_ctx = ExitStack()
    block = block_ctx.enter_context(nc.Block())

    def rows_view(ap):
        return ap.rearrange("(c p) n -> p c n", p=P)

    @block.sync
    def _(sp):
        def attention_operands(a):
            hw = P // a.dim

            def parts_out(n):
                t, which = n // 2, "qk"[n % 2]
                order = ("hi", "lo", "hi", "lo") if which == "q" else ("hi", "lo", "lo", "hi")
                for part in range(4):
                    if part < 2:
                        sp.wait_ge(sg(f"{a.name}_{order[part]}"), n + 1)
                    sp.dma_start(xs[a.name][which][t * hw:(t + 1) * hw, part, :, :],
                                 hl[f"{which}_{order[part]}"][:, t, :].bitcast(fp32))\
                        .then_inc(sg(f"{a.name}_parts_out{t}"), 16)

            def stack(g):
                bb, g1 = g // a.per_batch, g % a.per_batch
                t = 2 * g1 // a.per_batch
                sp.wait_ge(sg(f"{a.name}_parts_out{t}"), 16 * 8)
                if g >= a.RING:
                    sp.wait_ge(sg(a.name + "_st_full"), (g - a.RING + 1) * a.group)
                if a.lanes > 1 and g < a.RING:
                    sp.wait_ge(sg("q1_zero"), 1 if g < a.RING - 1 else 2)
                for which, st in (("q", qst), ("k", kst)):
                    for lane in range(a.lanes):
                        h = g1 * a.group + lane * a.slots
                        src = xs[a.name][which][h:h + a.slots, :, :, bb * T:(bb + 1) * T]
                        dst = q1_at(g, lane) if which == "q" and a.lanes > 1 else st[:, g % a.RING]
                        sp.dma_start(dst[64 * lane:64 * lane + a.rows, :, :].bitcast(fp32),
                                     src.rearrange("h p d t -> (p d) h t"))\
                            .then_inc(sg(f"{a.name}_stack{g % a.RING}"), 16)

            def send_rows(gr):
                sp.wait_ge(sg(a.name + "_rows"), gr + 1)
                if a.lanes == 1 and gr >= 3:
                    sp.wait_ge(sg(a.name + "_st_full"), (gr - 2) * a.group)
                for lane in range(a.lanes):
                    for part in range(2):
                        row = MAX_ROW + part
                        dst = mrow[part:part + 1, gr % 3] if a.lanes == 1 else q1_at(gr, lane)[row:row + 1]
                        sp.dma_start(dst.bitcast(fp32), rows_hl[lane * a.slots:(lane + 1) * a.slots, gr % 2, part, :]
                                     .bitcast(fp32)).then_inc(sg(f"{a.name}_rows_in{gr % 2}"), 16)

            parts_out(0)
            parts_out(1)
            parts_out(2)
            parts_out(3)
            for g in range(a.RING):
                stack(g)
            for g in range(a.groups):
                send_rows(g)
                if g >= 2 and g + 2 < a.groups:
                    stack(g + 2)

        def load_pair(j):
            for bb in range(2):
                sp.dma_start(ha[:, 2 * bb:2 * bb + 2, :],
                             h0[:, j + PAIRS * bb, :].rearrange("(k p) d -> p k d", p=P))\
                    .then_inc(pair_io, 16)

        load_pair(0)
        with sp.Fori(0, PAIRS) as j:
            for e in range(E_IT):
                sp.dma_start(w1[:, e, :, :], rows_view(io["L0_ffn_w1"][E_IT * j + e])).then_inc(sg("w_in"), 16)
                sp.dma_start(w2[:, e, :, :], rows_view(io["L0_ffn_w2"][E_IT * j + e])).then_inc(sg("w_in"), 16)
                sp.dma_start(b1r[e * FT:(e + 1) * FT, :],
                             io["L0_ffn_b1"][E_IT * j + e].rearrange("(c p) -> c p", p=P)).then_inc(sg("w_in"), 16)
                sp.dma_start(b2b[:, e, :], io["L0_ffn_b2"][E_IT * j + e].partition_broadcast(P))\
                    .then_inc(sg("w_in"), 16)
            attention_operands(att0)
            attention_operands(att1)
            sp.wait_ge(sg("ha_free"), 1)
            load_pair((j + 1) % PAIRS)
            sp.wait_ge(sg("h3"), 1)
            for bb in range(2):
                sp.dma_start(x3[j + PAIRS * bb].rearrange("(k p) d -> p k d", p=P), hb[:, 2 * bb:2 * bb + 2, :])\
                    .then_inc(pair_io, 16)
            sp.sem_inc(done, 1)
            sp.wait_ge(go["sp"], 1)
            sp.sem_clear(go["sp"])
        sp.wait_ge(pair_io, pair_ready(PAIRS))

    @block.gpsimd
    def _(pool):
        g = nc.gpsimd
        g.memset(onesr[:, :], 1.0).then_inc(constants, 1)
        g.tensor_copy(identb[:, :], ident[:, :]).then_inc(constants, 1)
        g.memset(mask_s[:, :], 0.0).then_inc(constants, 1)
        g.memset(mask_t[:, :], 0.0).then_inc(constants, 1)
        g.memset(mask_g[:, :], 1.0).then_inc(constants, 1)
        pool.wait_ge(constants, 5)
        g.memset(mask_s[:, 2 * P:], NEG).then_inc(constants, 1)
        g.memset(mask_t[:, 0:P], NEG).then_inc(constants, 1)
        g.affine_select(out=mask_s[:, P:2 * P], in_=mask_s[:, P:2 * P], compare_op=ALU.is_ge, fill=NEG,
                        base=0, pattern=[[-1, P]], channel_multiplier=1).then_inc(constants, 1)
        g.affine_select(out=mask_t[:, P:2 * P], in_=mask_t[:, P:2 * P], compare_op=ALU.is_ge, fill=NEG,
                        base=0, pattern=[[1, P]], channel_multiplier=-1).then_inc(constants, 1)
        g.affine_select(out=mask_g[:, :], in_=mask_g[:, :], compare_op=ALU.is_ge, fill=0.0,
                        base=0, pattern=[[1, P]], channel_multiplier=-1).then_inc(constants, 1)
        for a in (att0, att1):
            g.memset(vpad[a.name][:, :, :, :, :], 0.0).then_inc(constants, 1)
        g.memset(sd[:, :, :], 0.0).then_inc(constants, 1)
        pool.wait_ge(constants, 13)
        for a in (att0, att1):
            for buf in range(2):
                for kt in range(2):
                    g.memset(vpad[a.name][:, buf, kt, :, a.dim:a.dim + 1], 1.0).then_inc(constants, 1)
        pool.wait_ge(constants, 21)

        def attention_feed(a):
            def pad_v(gr):
                bb, g1 = gr // a.per_batch, gr % a.per_batch
                if gr >= 2:
                    pool.wait_ge(sg(a.name + "_av_done"), (gr - 1) * a.group)
                for kt in range(2):
                    last = g.tensor_copy(
                        vpad[a.name][:, gr % 2, kt, :, 0:a.dim],
                        vb[:, 2 * bb + kt, g1 * a.group * a.dim:(g1 + 1) * a.group * a.dim]
                        .rearrange("p (h d) -> p h d", d=a.dim))
                last.then_inc(sg(a.name + "_padded"), 1)

            pool.wait_ge(sg(a.name + "_v"), 2)
            for gr in range(a.groups):
                pad_v(gr)

        with pool.Fori(0, PAIRS) as j:
            attention_feed(att0)
            pool.wait_ge(sg("a0_st_full"), att0.units)
            g.memset(kst[MAX_ROW:MAX_ROW + 2, :, :, :].bitcast(fp32), 1.0).then_inc(sg("ones_row"), 1)
            pool.wait_ge(sg("ones_row"), 1)
            g.memset(q1[:, 1:, :, :, :].bitcast(fp32), 0.0).then_inc(sg("q1_zero"), 1)
            pool.wait_ge(sg("a1_parts_out0"), 16 * 8)
            pool.wait_ge(sg("a1_parts_out1"), 16 * 8)
            g.memset(q1[:, 0, :, :, :].bitcast(fp32), 0.0).then_inc(sg("q1_zero"), 1)
            pool.wait_ge(sg("q1_zero"), 2)
            attention_feed(att1)
            pool.wait_ge(sg("h3"), 1)
            pool.sem_inc(done, 1)
            pool.wait_ge(go["pool"], 1)
            pool.sem_clear(go["pool"])

    @block.tensor
    def _(pe):
        mm = nc.tensor.matmul
        pe.wait_ge(ready, 1)
        def keep_warm(n, bank=5):
            for _ in range(n):
                mm(ps[bank][:, 0:3 * P], identb[:, :], mask_s[:, :], start=True, stop=True)

        def transposes(src, name, after=None):
            if after:
                keep_warm(WARM.get(name, 0))
                pe.wait_ge(*after)
            for c in range(DC):
                for tb in range(NTB):
                    last = nc.tensor.transpose(ps[c][:, tb * P:(tb + 1) * P], src[:, tb, c * P:(c + 1) * P],
                                               ident[:, :])
                last.then_inc(sg(name + "_full"), 1)

        def qkv(a, wq, wk, wv, name):
            pe.wait_ge(sg(name + "_ev"), 2)
            for n, (t, w) in enumerate(((0, wq), (0, wk), (1, wq), (1, wk))):
                for c in range(DC):
                    last = mm(ps[2 + n][:, :], w[:, c, t * P:(t + 1) * P], tt[:, c, :],
                              start=c == 0, stop=c == DC - 1)
                last.then_inc(sg(a.name + "_qk_full"), 1)
            for tb in range(NTB):
                for c in range(DC):
                    last = mm(ps[6 + tb // 2][:, (tb % 2) * D:(tb % 2 + 1) * D],
                              tt[:, c, tb * P:(tb + 1) * P], wv[:, c, :], start=c == 0, stop=c == DC - 1)
                if tb % 2:
                    last.then_inc(sg(a.name + "_v_full"), 1)

        def project(w, name, ob_ready):
            transposes(ob, name + "_t", ob_ready)
            pe.wait_ge(sg(name + "_t_ev"), 2)
            for tb in range(NTB):
                for c in range(DC):
                    last = mm(ps[2 + tb // 2][:, (tb % 2) * D:(tb % 2 + 1) * D],
                              tt[:, c, tb * P:(tb + 1) * P], w[:, c, :], start=c == 0, stop=c == DC - 1)
                if tb % 2:
                    last.then_inc(sg(name + "_full"), 1)

        def attention(a):
            n_ = a.name
            stack_dmas = 2 * a.lanes

            def scores(u):
                g, n = u // a.group, u % a.group
                lane, slot = a.lane_slot(n)
                if u >= 2:
                    pe.wait_ge(sg(n_ + "_max"), u - 1)
                q = qst[:, g % a.RING] if a.lanes == 1 else q1_at(g, lane)
                rows = a.rows if a.lanes == 1 else MAX_ROW
                for qb in range(2):
                    o = ps[u % 2][:, qb * T:(qb + 1) * T]
                    last = mm(o, q[0:rows, slot, qb * P:(qb + 1) * P], kst[0:rows, g % a.RING, slot, :],
                              start=True, stop=not a.causal)
                    if a.causal:
                        last = mm(o[:, qb * P:], identb[:, :], mask_s[:, P:3 * P - qb * P], start=False, stop=True)
                last.then_inc(sg(n_ + "_s_full"), 1)

            def scores_t(u):
                g, n = u // a.group, u % a.group
                lane, slot = a.lane_slot(n)
                if u >= 2:
                    pe.wait_ge(sg(n_ + "_exp"), u - 1)
                q = qst[:, g % a.RING] if a.lanes == 1 else q1_at(g, lane)
                rows = a.rows if a.lanes == 1 else MAX_ROW + 2
                for kt in range(2):
                    o = ps[2 + u % 2][:, kt * T:(kt + 1) * T]
                    last = mm(o, kst[0:rows, g % a.RING, slot, kt * P:(kt + 1) * P], q[0:rows, slot, :],
                              start=True, stop=a.lanes > 1)
                    if a.lanes == 1:
                        mm(o, ones2[:, :], mrow[:, g % 3, slot, :], start=False, stop=False)
                        last = mm(o[:, 0:(kt + 1) * P], identb[:, :], mask_t[:, P - kt * P:2 * P], start=False,
                                  stop=True)
                last.then_inc(sg(n_ + "_st_full"), 1)

            def values(k):
                if k >= 2:
                    pe.wait_ge(sg(n_ + "_acc"), k - 1)
                pe.wait_ge(sg(n_ + "_exp"), (k + 1) * a.quad)
                for kt in range(2):
                    q0 = P if a.causal and kt else 0
                    for i in range(a.quad):
                        u = k * a.quad + i
                        g, n = u // a.group, u % a.group
                        last = mm(ps[4 + k % 2][i * a.vw:(i + 1) * a.vw, q0:T], vpad[a.name][:, g % 2, kt, n, :],
                                  pt[u % PT_RING][:, kt * T + q0:(kt + 1) * T], start=kt == 0, stop=kt == 1)
                last.then_inc(sg(n_ + "_av_done"), a.quad)

            def outputs_t(k):
                pe.wait_ge(sg(n_ + "_acc"), k + 1)
                if k:
                    pe.wait_ge(sg(n_ + "_norm"), k)
                for qb in range(2):
                    last = nc.tensor.transpose(ps[7][:, qb * P:(qb + 1) * P],
                                               acc[k % 2][:, qb * P:(qb + 1) * P], ident[:, :])
                last.then_inc(sg(n_ + "_o_full"), 1)

            def maxima_t(g):
                pe.wait_ge(sg(n_ + "_max"), (g + 1) * a.group)
                if g:
                    pe.wait_ge(sg(n_ + "_rows"), g)
                for qb in range(2):
                    last = nc.tensor.transpose(ps[6][0:a.group, qb * P:(qb + 1) * P],
                                               mx[:, g % 2, qb, 0:a.group], ident[:, :])
                last.then_inc(sg(n_ + "_mt_full"), 1)

            def after_scores(u):
                for k in a.due(u, OUT_LAG):
                    outputs_t(k)
                for k in a.due(u, AV_LAG):
                    values(k)

            pe.wait_ge(constants, 21)
            pe.wait_ge(sg(n_ + "_v"), 2)
            if a.lanes > 1:
                pe.wait_ge(sg("ones_row"), 1)
            pe.wait_ge(sg(n_ + "_hi"), 4)
            pe.wait_ge(sg(n_ + "_lo"), 4)
            keep_warm(WARM[n_ + "_stack"])
            for p in range(a.groups + 2):
                gs, gt = p, p - 2
                if gs < a.groups:
                    pe.wait_ge(sg(f"{n_}_stack{gs % a.RING}"), 16 * stack_dmas * (gs // a.RING + 1))
                if gt >= 0:
                    pe.wait_ge(sg(f"{n_}_rows_in{gt % 2}"), 16 * 2 * a.lanes * (gt // 2 + 1))
                    pe.wait_ge(sg(n_ + "_padded"), gt + 1)
                for n in range(a.group):
                    if gt >= 0:
                        u = gt * a.group + n
                        scores_t(u)
                    if gs < a.groups:
                        scores(gs * a.group + n)
                    if gt >= 0:
                        after_scores(u)
                if gs < a.groups:
                    maxima_t(gs)
            for u in range(a.units, a.units + OUT_LAG):
                after_scores(u)

        def experts():
            pe.wait_ge(sg("w_in"), 16 * 4 * E_IT)
            nc.tensor.transpose(ps[6][:, 0:E_IT * FT], b1r[:, :], ident[0:E_IT * FT, 0:E_IT * FT])\
                .then_inc(sg("b1_full"), 1)
            pe.wait_ge(sg("xf_t_ev"), 2)
            n = 0
            for e in range(E_IT):
                mv_ = [tt[:, c, :].rearrange("p (b k t) -> p k b t", b=2, k=2)[:, e] for c in range(DC)]
                for f2 in range(FT // 2):
                    if n >= 4:
                        pe.wait_ge(sg("up_ev"), 2 * (n - 3))
                    for f in (2 * f2, 2 * f2 + 1):
                        for c in range(DC):
                            last = mm(ps[2 + n % 4][:, (f % 2) * T:(f % 2 + 1) * T],
                                      w1[:, e, c, f * P:(f + 1) * P], mv_[c], start=c == 0, stop=c == DC - 1)
                    last.then_inc(sg("up_full"), 1)
                    n += 1
            pe.wait_ge(sg("b1_ev"), 1)
            for e in range(E_IT):
                pe.wait_ge(sg("up_ev"), FT * (e + 1))
                for bb in range(2):
                    o = ps[(0, 1, 6, 7)[2 * e + bb]][:, 0:D]
                    for f in range(FT):
                        last = mm(o, hid[:, e, f, bb * P:(bb + 1) * P], w2[:, e, f, :], start=f == 0,
                                  stop=f == FT - 1)
                    last.then_inc(sg("down_full"), 1)

        def linear_attention():
            pe.wait_ge(sg("h2_t_ev"), 2)
            for n, w in ((2, wt.gwq), (3, wt.gwk)):
                for c in range(DC):
                    last = mm(ps[n][:, :], w[:, c, :], tt[:, c, :], start=c == 0, stop=c == DC - 1)
                last.then_inc(sg("g_qk_full"), 1)
            for c in range(DC):
                last = mm(ps[4][0:16, :], wt.gwgk1[:, c, :], tt[:, c, :], start=c == 0, stop=c == DC - 1)
            last.then_inc(sg("g_u_full"), 1)
            for tb in range(NTB):
                for c in range(DC):
                    last = mm(ps[(6, 7, 0, 1)[tb]][:, :], tt[:, c, tb * P:(tb + 1) * P], wt.gwvg[:, c, :],
                              start=c == 0, stop=c == DC - 1)
                last.then_inc(sg("g_vg_full"), 1)
                if tb == 0:
                    pe.wait_ge(sg("g_u"), 1)
                    mm(ps[5][:, :], wt.gwgk2[:, :], u1[:, :], start=True, stop=True).then_inc(sg("g_z_full"), 1)
            keep_warm(WARM["g_qk"], bank=4)
            pe.wait_ge(sg("g_qk"), 2)
            pe.wait_ge(sg("g_vg"), 8)
            for bb in range(2):
                last = nc.tensor.transpose(ps[6][:, bb * P:(bb + 1) * P], ks[:, 2 * bb * P:(2 * bb + 1) * P],
                                           ident[:, :])
            last.then_inc(sg("g_kt_full"), 1)
            for h in range(NHG):
                for tb in range(NTB):
                    last = mm(ps[2 + h][:, tb * P:(tb + 1) * P], ks[h * DK:(h + 1) * DK, tb * P:(tb + 1) * P],
                              qs[h * DK:(h + 1) * DK, tb * P:(tb + 1) * P], start=True, stop=True)
                last.then_inc(sg("g_at_full"), 1)
            pe.wait_ge(sg("g_kt"), 1)
            for bb in range(2):
                last = mm(ps[7][:, bb * D:(bb + 1) * D], kT[:, bb, :], vb[:, 2 * bb, :], start=True, stop=True)
            last.then_inc(sg("g_state_full"), 1)
            pe.wait_ge(sg("g_at"), NHG)
            pe.wait_ge(sg("g_state"), 1)
            for tb in range(NTB):
                o = ps[(0, 1, 6, 7)[tb]]
                if tb % 2:
                    mm(o[:, 0:D], qs[:, tb * P:(tb + 1) * P], sd[:, tb // 2, :], start=True, stop=False,
                       skip_group_check=True)
                for h in range(NHG):
                    last = mm(o[:, h * DV:(h + 1) * DV], atm[:, h, tb, :], vb[:, tb, h * DV:(h + 1) * DV],
                              start=tb % 2 == 0, stop=True, skip_group_check=True)
                last.then_inc(sg("g_o_full"), 1)

        with pe.Fori(0, PAIRS) as j:
            transposes(ha, "h_t", (pair_io, pair_ready(j)))
            qkv(att0, wt.wqkv0[:, :, 0:D], wt.wqkv0[:, :, D:2 * D], wt.wqkv0[:, :, 2 * D:], "h_t")
            attention(att0)
            project(wt.wout0, "p0", (sg("a0_norm"), att0.units // att0.quad))
            transposes(ob, "xn_t", (sg("xn"), 1))
            qkv(att1, wt.wq1, wt.wk1, wt.wv1, "xn_t")
            attention(att1)
            project(wt.wo1, "p1", (sg("a1_norm"), att1.units // att1.quad))
            transposes(yb, "xf_t", (sg("xf"), 1))
            experts()
            transposes(ha, "h2_t", (sg("h2"), 1))
            linear_attention()
            project(wt.gwo, "p2", (sg("g_o"), 1))
            pe.wait_ge(go["pe"], 1)
            pe.sem_clear(go["pe"])

    @block.scalar
    def _(act):
        sc = nc.scalar
        act.wait_ge(ready, 1)

        def transposed(name):
            act.wait_ge(sg(name + "_full"), 1)
            sc.copy(tt[:, 0, :], ps[0][:, :]).then_inc(sg(name + "_ev"), 1)

        def qkv(a):
            for n in range(4):
                act.wait_ge(sg(a.name + "_qk_full"), n + 1)
                sc.copy(hl[("q_hi", "k_hi")[n % 2]][:, n // 2, :], ps[2 + n][:, :]).then_inc(sg(a.name + "_hi"), 1)
            for n in range(2):
                act.wait_ge(sg(a.name + "_v_full"), n + 1)
                sc.copy(vb[:, 2 * n:2 * n + 2, :], ps[6 + n][:, :].rearrange("p (b d) -> p b d", b=2))\
                    .then_inc(sg(a.name + "_v"), 1)

        def attention(a):
            n_ = a.name

            def heads_out(k):
                act.wait_ge(sg(n_ + "_av_done"), (k + 1) * a.quad)
                if k >= 2:
                    act.wait_ge(sg(n_ + "_o_full"), k - 1)
                sc.copy(acc[k % 2][:, :], ps[4 + k % 2][:, 0:T]).then_inc(sg(n_ + "_acc"), 1)

            for u in range(a.units):
                act.wait_ge(sg(n_ + "_st_full"), u + 1)
                if u >= PT_RING:
                    act.wait_ge(sg(n_ + "_av_done"), u - PT_RING + 1)
                sc.activation(pt[u % PT_RING][:, :], ps[2 + u % 2][:, :], ACT.Exp).then_inc(sg(n_ + "_exp"), 1)
                for k in a.due(u, AV_LAG):
                    heads_out(k)
            for u in range(a.units, a.units + AV_LAG):
                for k in a.due(u, AV_LAG):
                    heads_out(k)

        def experts():
            act.wait_ge(sg("b1_full"), 1)
            sc.copy(b1c[:, :], ps[6][:, 0:E_IT * FT]).then_inc(sg("b1_ev"), 1)
            act.wait_ge(sg("b1_ev"), 1)
            for n in range(E_IT * FT // 2):
                act.wait_ge(sg("up_full"), n + 1)
                for i in range(2):
                    f = 2 * n + i
                    sc.activation(hid[:, f // FT, f % FT, :], ps[2 + n % 4][:, i * T:(i + 1) * T], ACT.Gelu,
                                  bias=b1c[:, f:f + 1]).then_inc(sg("up_ev"), 1)

        def linear_attention():
            sc.preload_act_table_set("natural_log_exp_and_others")
            act.wait_ge(sg("g_u_full"), 1)
            sc.copy(u1[:, :], ps[4][0:16, :]).then_inc(sg("g_u"), 1)
            for tb in range(NTB):
                act.wait_ge(sg("g_vg_full"), tb + 1)
                o = ps[(6, 7, 0, 1)[tb]]
                sc.copy(vb[:, tb, :], o[:, 0:D]).then_inc(sg("g_vg"), 1)
                sc.copy(gb[:, tb, :], o[:, D:]).then_inc(sg("g_vg"), 1)
            act.wait_ge(sg("g_z"), 1)
            sc.activation(ge[:, :], ge[:, :], ACT.Exp).then_inc(sg("g_a"), 1)
            act.wait_ge(sg("g_a"), 1)
            sc.activation(ge[:, :], ge[:, :], ACT.Ln, bias=1.0).then_inc(sg("g_a"), 1)
            act.wait_ge(sg("g_d"), 1)
            sc.activation(ge[:, :], gz[:, :], ACT.Exp).then_inc(sg("g_a"), 1)
            sc.activation(gm[:, :], gz[:, :], ACT.Exp, scale=-1.0).then_inc(sg("g_a"), 1)
            act.wait_ge(sg("g_vg"), 8)
            sc.activation(yb[:, :, :], gb[:, :, :], ACT.Exp, scale=-1.0).then_inc(sg("g_a"), 1)
            sc.activation(dr[:, :], dr[:, :], ACT.Exp).then_inc(sg("g_dr"), 1)
            act.wait_ge(sg("g_kt_full"), 1)
            sc.copy(kT[:, :, :], ps[6][:, 0:2 * P].rearrange("p (b k) -> p b k", b=2)).then_inc(sg("g_kt"), 1)
            for tb in range(NTB):
                act.wait_ge(sg("g_o_full"), tb + 1)
                sc.activation(hb[:, tb, :], ps[(0, 1, 6, 7)[tb]][:, 0:D], ACT.Square).then_inc(sg("g_sq"), 1)

        with act.Fori(0, PAIRS) as j:
            transposed("h_t")
            qkv(att0)
            attention(att0)
            transposed("p0_t")
            transposed("xn_t")
            qkv(att1)
            attention(att1)
            transposed("p1_t")
            transposed("xf_t")
            experts()
            transposed("h2_t")
            linear_attention()
            transposed("p2_t")
            act.wait_ge(go["act"], 1)
            act.sem_clear(go["act"])

    @block.vector
    def _(dve):
        v = nc.vector
        s = Counted(dve, once("prepare"))
        dve.wait_ge(wt.loaded, 16 * len(wt.loads))
        dve.wait_ge(constants, 1)
        wq = wt.wqkv0[:, :, 0:D].rearrange("p c (h k) -> p c h k", h=8)
        for c in range(DC):
            s.step(v.tensor_tensor(gp[:, c], wq[:, c, :, 0:3], wt.dirs[:, :, :], ALU.mult))
            s.step(v.tensor_reduce(gq[:, c, :], gp[:, c], AX.X, ALU.add))
            s.step(v.tensor_tensor(gq[:, c, :], gq[:, c, :], wt.hsc[:, :], ALU.mult))
            s.step(v.tensor_tensor(gp[:, c], wt.dirs[:, :, :],
                                   gq[:, c, :].unsqueeze(2).to_broadcast([P, 8, 3]), ALU.mult))
            s.step(v.tensor_scalar(wt.wqkv0[:, c, 0:D], wt.wqkv0[:, c, 0:D], att0.dim ** -0.5, None, ALU.mult))
            s.step(v.tensor_tensor(wq[:, c, :, 0:3], wq[:, c, :, 0:3], gp[:, c], ALU.add))
        s.step(v.tensor_scalar(wt.wq1[:, :, :], wt.wq1[:, :, :], att1.dim ** -0.5, None, ALU.mult))
        s.step(v.tensor_copy(ones2[:, :], onesr[0:2, 0:P]))
        v.tensor_copy(rc[:, 0:1], onesr[:, 0:1]).then_inc(ready, 1)

        s = None

        def transposed(name):
            dve.wait_ge(sg(name + "_full"), 2)
            v.tensor_copy(tt[:, 1, :], ps[1][:, :]).then_inc(sg(name + "_ev"), 1)

        def qkv(a):
            for n in range(4):
                dve.wait_ge(sg(a.name + "_hi"), n + 1)
                w = ("q", "k")[n % 2]
                v.tensor_tensor(hl[w + "_lo"][:, n // 2, :], ps[2 + n][:, :], hl[w + "_hi"][:, n // 2, :]
                                .bitcast(fp32), ALU.subtract).then_inc(sg(a.name + "_lo"), 1)

        def attention(a, s):
            n_ = a.name

            def maximum(u):
                g, n = u // a.group, u % a.group
                dve.wait_ge(sg(n_ + "_s_full"), u + 1)
                if n == 0 and g >= 2:
                    dve.wait_ge(sg(n_ + "_mt_full"), g - 1)
                v.tensor_reduce(mx[:, g % 2, :, n], ps[u % 2][:, :].rearrange("p (b k) -> p b k", b=2),
                                AX.X, ALU.max, negate=True).then_inc(sg(n_ + "_max"), 1)

            def rows(g):
                dve.wait_ge(sg(n_ + "_mt_full"), g + 1)
                if g >= 2:
                    dve.wait_ge(sg(f"{n_}_rows_in{g % 2}"), 16 * 2 * a.lanes * (g // 2))
                hi, lo = (rows_hl[0:a.group, g % 2, i, :] for i in range(2))
                s.step(v.tensor_copy(hi, ps[6][0:a.group, 0:T]))
                v.tensor_tensor(lo, ps[6][0:a.group, 0:T], hi.bitcast(fp32), ALU.subtract)\
                    .then_inc(sg(n_ + "_rows"), 1)

            def normalise(k):
                dve.wait_ge(sg(n_ + "_o_full"), k + 1)
                h = k * a.quad % a.heads
                bb = k * a.quad // a.heads
                o = ps[7][:, 0:2 * P].rearrange("p (b h w) -> p b h w", b=2, h=a.quad)
                s.step(v.reciprocal(rc[:, 0:2 * a.quad].rearrange("p (b h) -> p b h", b=2), o[:, :, :, a.dim]))
                v.tensor_tensor(ob[:, 2 * bb:2 * bb + 2, h * a.dim:(h + a.quad) * a.dim]
                                .rearrange("p b (h d) -> p b h d", h=a.quad), o[:, :, :, 0:a.dim],
                                rc[:, 0:2 * a.quad].rearrange("p (b h) -> p b h", b=2).unsqueeze(3)
                                .to_broadcast([P, 2, a.quad, a.dim]), ALU.mult).then_inc(sg(n_ + "_norm"), 1)

            for p in range(a.groups + 2):
                gs, gt = p, p - 2
                for n in range(a.group):
                    if gs < a.groups:
                        maximum(gs * a.group + n)
                    for k in a.due(gt * a.group + n, NORM_LAG):
                        normalise(k)
                if gs < a.groups:
                    rows(gs)
            for u in range(a.units, a.units + NORM_LAG):
                for k in a.due(u, NORM_LAG):
                    normalise(k)

        def normalised(s, src, dst, root):
            for tb in range(NTB):
                s.mark(v.tensor_scalar(dst[:, tb, :], src[:, tb, :], mv[:, tb, 0:1], root[:, tb:tb + 1],
                                       ALU.subtract, ALU.mult))

        def layernorm(s, src, dst):
            s.sync()
            for tb in range(NTB):
                s.mark(v.bn_aggr(mv[:, tb, :], stats[:, tb, :]))
            s.sync()
            x_, y_, a_ = (r[:, 0:NTB] for r in rs)
            s.step(v.tensor_scalar(x_, mv[:, :, 1], LN_EPS, None, ALU.add))
            rsqrt_steps(s, v, x_, y_, a_)
            if dst is not None:
                normalised(s, src, dst, rs[1])
                s.sync()

        def statistics(s, src, blocks):
            for tb in blocks:
                s.mark(v.bn_stats(stats[:, tb, :], src[:, tb, :]))

        def add_projection(s, name, resid, dst, normed):
            for n in range(2):
                dve.wait_ge(sg(name + "_full"), n + 1)
                s.step(v.tensor_tensor(dst[:, 2 * n:2 * n + 2, :],
                                       ps[2 + n][:, :].rearrange("p (b d) -> p b d", b=2),
                                       resid[:, 2 * n:2 * n + 2, :], ALU.add))
                if normed:
                    statistics(s, dst, (2 * n, 2 * n + 1))

        def signal(s, name):
            s.sync()
            dve.sem_inc(sg(name), 1)

        def experts(s):
            dve.wait_ge(sg("w_in"), 16 * 4 * E_IT)
            for e in range(E_IT):
                for bb in range(2):
                    s.mark(v.tensor_tensor(hb[:, 2 * bb + e, :], hb[:, 2 * bb + e, :], b2b[:, e, :], ALU.add))
            s.sync()
            for e in range(E_IT):
                for bb in range(2):
                    dve.wait_ge(sg("down_full"), 2 * e + bb + 1)
                    s.step(v.tensor_tensor(yb[:, 2 * bb + e, :], ps[(0, 1, 6, 7)[2 * e + bb]][:, 0:D],
                                           hb[:, 2 * bb + e, :], ALU.add))
                    statistics(s, yb, (2 * bb + e,))

        def linear_attention(s):
            dve.wait_ge(constants, 21)
            dve.wait_ge(sg("g_z_full"), 1)
            s.step(v.tensor_scalar(gz[:, :], ps[5][:, :], wt.bgk[:, 0:1], None, ALU.add))
            s.mark(v.tensor_scalar(gm[:, :], gz[:, :], 0.0, None, ALU.min))
            v.scalar_tensor_tensor(ge[:, :], gz[:, :], -1.0, gz[:, :], ALU.mult, ALU.min).then_inc(sg("g_z"), 1)
            dve.wait_ge(sg("g_a"), 2)
            s.step(v.tensor_tensor(gm[:, :], gm[:, :], ge[:, :], ALU.subtract))
            s.step(v.tensor_scalar(gm[:, :], gm[:, :], 1 / 16.0, None, ALU.mult))
            for bb in range(2):
                s.mark(v.tensor_tensor_scan(gG[:, bb * T:(bb + 1) * T], onesr[:, :], gm[:, bb * T:(bb + 1) * T],
                                            0.0, ALU.mult, ALU.add))
            s.sync()
            mid = [gG[:, tb * P + P // 2 - 1:tb * P + P // 2] for tb in range(NTB)]
            for tb in range(NTB):
                s.mark(v.tensor_scalar(gz[:, tb * P:(tb + 1) * P], gG[:, tb * P:(tb + 1) * P], mid[tb], None,
                                       ALU.subtract))
            for bb in range(2):
                s.mark(v.tensor_tensor(dr[:, bb:bb + 1], mid[2 * bb + 1], mid[2 * bb], ALU.subtract))
            s.sync()
            signal(s, "g_d")
            dve.wait_ge(sg("g_qk_full"), 2)
            dve.wait_ge(sg("g_a"), 4)
            v.scalar_tensor_tensor(qs[:, :], ps[2][:, :], DK ** -0.5, ge[:, :], ALU.mult, ALU.mult)\
                .then_inc(sg("g_qk"), 1)
            v.tensor_tensor(ks[:, :], ps[3][:, :], gm[:, :], ALU.mult).then_inc(sg("g_qk"), 1)
            for h in range(NHG):
                dve.wait_ge(sg("g_at_full"), h + 1)
                v.tensor_tensor(atm[:, h, :, :], ps[2 + h][:, :].rearrange("p (b t) -> p b t", b=NTB),
                                mask_g[:, :].unsqueeze(1).to_broadcast([P, NTB, P]), ALU.mult)\
                    .then_inc(sg("g_at"), 1)
            dve.wait_ge(sg("g_state_full"), 1)
            dve.wait_ge(sg("g_dr"), 1)
            for bb in range(2):
                for h in range(NHG):
                    r = slice(h * DK, (h + 1) * DK)
                    s.mark(v.tensor_scalar(sd[r, bb, h * DV:(h + 1) * DV],
                                           ps[7][r, bb * D + h * DV:bb * D + (h + 1) * DV],
                                           dr[r, bb:bb + 1], None, ALU.mult))
            s.sync()
            signal(s, "g_state")
            dve.wait_ge(sg("g_a"), 5)
            s.step(v.tensor_scalar(yb[:, :, :], yb[:, :, :], 1.0, None, ALU.add))
            s.step(v.reciprocal(yb[:, :, :], yb[:, :, :]))
            s.step(v.tensor_tensor(gb[:, :, :], gb[:, :, :], yb[:, :, :], ALU.mult))
            s.step(v.tensor_tensor(gb[:, :, :].rearrange("p t (h d) -> p (t h) d", d=DV),
                                   gb[:, :, :].rearrange("p t (h d) -> p (t h) d", d=DV),
                                   wt.gwb[:, :].unsqueeze(1).to_broadcast([P, NTB * NHG, DV]), ALU.mult))
            dve.wait_ge(sg("g_sq"), NTB)
            x_, y_, a_ = (r[:, :] for r in rs)
            s.step(v.tensor_reduce(x_, hb[:, :, :].rearrange("p t (h d) -> p (t h) d", d=DV), AX.X, ALU.add))
            s.step(v.tensor_scalar(x_, x_, 1.0 / DV, LN_EPS, ALU.mult, ALU.add))
            rsqrt_steps(s, v, x_, y_, a_)
            for tb in range(NTB):
                shape = [P, NHG, DV]
                s.mark(v.tensor_tensor(ob[:, tb, :].rearrange("p (h d) -> p h d", d=DV),
                                       ps[(0, 1, 6, 7)[tb]][:, 0:D].rearrange("p (h d) -> p h d", d=DV),
                                       rs[1][:, tb * NHG:(tb + 1) * NHG].unsqueeze(2).to_broadcast(shape),
                                       ALU.mult))
            s.sync()
            s.step(v.tensor_tensor(ob[:, :, :], ob[:, :, :], gb[:, :, :], ALU.mult))
            signal(s, "g_o")

        with dve.Fori(0, PAIRS) as j:
            s = Counted(dve, sg("dve_steps"))
            transposed("h_t")
            qkv(att0)
            attention(att0, s)
            transposed("p0_t")
            add_projection(s, "p0", ha, yb, True)
            layernorm(s, yb, None)
            r1, x2, r2, a2, r12 = rs[1][:, 0:4], rs[0][:, 4:8], rs[1][:, 4:8], rs[2][:, 4:8], rs[0][:, 8:12]
            s.step(v.tensor_tensor(x2, mv[:, :, 1], r1, ALU.mult))
            s.step(v.tensor_tensor(x2, x2, r1, ALU.mult))
            s.step(v.tensor_scalar(x2, x2, LN_EPS, None, ALU.add))
            rsqrt_steps(s, v, x2, r2, a2)
            s.step(v.tensor_tensor(r12, r1, r2, ALU.mult))
            normalised(s, yb, ob, r12)
            s.sync()
            s.step(v.tensor_tensor(ob[:, :, :], ob[:, :, :], wt.lng[:, :].unsqueeze(1).to_broadcast([P, NTB, D]),
                                   ALU.mult))
            s.step(v.tensor_tensor(ob[:, :, :], ob[:, :, :], wt.lnb[:, :].unsqueeze(1).to_broadcast([P, NTB, D]),
                                   ALU.add))
            signal(s, "xn")
            normalised(s, yb, hb, rs[1])
            s.sync()
            transposed("xn_t")
            qkv(att1)
            attention(att1, s)
            transposed("p1_t")
            add_projection(s, "p1", hb, yb, False)
            signal(s, "xf")
            transposed("xf_t")
            experts(s)
            layernorm(s, yb, ha)
            signal(s, "h2")
            transposed("h2_t")
            linear_attention(s)
            transposed("p2_t")
            add_projection(s, "p2", ha, yb, True)
            signal(s, "ha_free")
            layernorm(s, yb, hb)
            signal(s, "h3")
            dve.wait_ge(done, 2)
            dve.sem_clear(done)
            for numbers in sg.runs():
                dve.sem_clear(numbers)
            for k in go:
                dve.sem_inc(go[k], 1)
    block_ctx.close()


def expert_mixture(nc, ctx, io, x3, xs, ys, out, ident):
    NTB = B * T // P
    E, F = 8, 1024
    FT = F // P
    GRP, NG = 4, NTB // 4
    TILES = xs.shape[0] // P
    HALF = F // 2
    KH = FT // 2
    XR = 4
    GR = 8

    def sb(name, shape, dt=fp32):
        return ctx.enter_context(nc.sbuf_tensor(name, shape, dt))

    sg = Signals(nc, ctx, "x")
    acc = sb("x_acc", [P, NTB, D])
    xTr = sb("x_Tr", [P, 2, DC, GRP * P])
    w1, w2 = sb("x_w1", [P, E, DC, F]), sb("x_w2", [P, E, FT, D])
    xt, xtT = sb("x_xt", [P, XR, D]), sb("x_xtT", [P, 2, DC, P])
    raw = sb("x_raw", [P, 2, HALF])
    hT = sb("x_hT", [P, 2, FT, P])
    y = sb("x_y", [P, 2, D])
    pair = sb("x_pair", [P, GR, 2, D])
    wg, bg = sb("x_wg", [P, DC, E]), sb("x_bg", [P, E])
    b1r, b1c = sb("x_b1r", [E * FT, P]), sb("x_b1c", [P, E * FT])
    b2b = sb("x_b2b", [P, E, D])
    rank = sb("x_rank", [P, E])
    before, ones = sb("x_before", [P, P]), sb("x_ones", [P, P])
    lo, pr, eq, oh1, oh2, both, sa, sc_ = (sb(f"x_{n}", [P, NTB, E])
                                          for n in ("lo", "pr", "eq", "oh1", "oh2", "both", "sa", "sc"))
    m1, m2, ix, dd = (sb(f"x_{n}", [P, NTB]) for n in ("m1", "m2", "ix", "dd"))
    cnt, cum, cum2 = (sb(f"x_{n}", [P, E]) for n in ("cnt", "cum", "cum2"))
    cnti = sb("x_cnti", [P, E], i32)
    tile_no, past = sb("x_tile_no", [1, TILES, E]), sb("x_past", [1, TILES, E])
    tef, te = sb("x_tef", [1, TILES]), sb("x_te", [1, TILES], i32)
    slotf, slot = sb("x_slotf", [P, 2, NTB]), sb("x_slot", [P, 2, NTB], u32)
    stats, mv = sb("x_stats", [P, NTB, 6]), sb("x_mv", [P, NTB, 2])
    rs = [sb(f"x_rs{i}", [P, GRP]) for i in range(3)]
    ps = [ctx.enter_context(nc.psum_tensor(f"x_ps{i}", [P, 512], fp32)) for i in range(8)]

    with nc.Block() as block:
        @block.sync
        def _(sp):
            for g in range(NG):
                sp.dma_start(acc[:, g * GRP:(g + 1) * GRP, :],
                             x3[2 * g:2 * g + 2].rearrange("b (k p) d -> p (b k) d", p=P)).then_inc(sg(f"x_in{g}"), 16)
            sp.dma_start(wg[:, :, :], io["L1_ffn_Wg"].rearrange("(c p) e -> p c e", p=P)).then_inc(sg("small"), 16)
            sp.dma_start(bg[:, :], io["L1_ffn_bg"].partition_broadcast(P)).then_inc(sg("small"), 16)
            sp.dma_start(b1r[:, :], io["L1_ffn_b1"].rearrange("e (c p) -> (e c) p", p=P)).then_inc(sg("small"), 16)
            for e in range(E):
                sp.dma_start(w1[:, e], io["L1_ffn_W1"][e].rearrange("(c p) n -> p c n", p=P)).then_inc(sg("w_in"), 16)
                sp.dma_start(w2[:, e], io["L1_ffn_W2"][e].rearrange("(c p) n -> p c n", p=P)).then_inc(sg("w_in"), 16)
            sp.dma_start(b2b[:, :, :], io["L1_ffn_b2"].partition_broadcast(P)).then_inc(sg("w_in"), 16)
            sp.wait_ge(sg("scattered"), 16 * 2 * NTB)

            def load_tile(i):
                if i >= XR:
                    sp.wait_ge(sg("xt_full"), i - XR + 1)
                sp.dma_start(xt[:, i % XR, :], xs[i * P:(i + 1) * P, :]).then_inc(sg(f"xt_in{i % XR}"), 16)

            for i in range(XR - 1):
                load_tile(i)
            for i in range(TILES):
                if i + XR - 1 < TILES:
                    load_tile(i + XR - 1)
                sp.wait_ge(sg("y"), i + 1)
                sp.dma_start(ys[i * P:(i + 1) * P, :], y[:, i % 2, :]).then_inc(sg(f"y_out{i % 2}"), 16)
            for g in range(NG):
                sp.wait_ge(sg("normed"), GRP * (g + 1))
                sp.dma_start(out[2 * g:2 * g + 2].rearrange("b (k p) d -> p (b k) d", p=P),
                             acc[:, g * GRP:(g + 1) * GRP, :]).then_inc(sg("stored"), 16)
            sp.wait_ge(sg("stored"), 16 * NG)

        @block.gpsimd
        def _(pool):
            g = nc.gpsimd
            g.iota(rank[:, :], pattern=[[1, E]], base=-E, channel_multiplier=0,
                   allow_small_or_imprecise_dtypes=True).then_inc(sg("constants"), 1)
            g.iota(tile_no[:, :, :], pattern=[[1, TILES], [0, E]], base=0, channel_multiplier=0,
                   allow_small_or_imprecise_dtypes=True).then_inc(sg("constants"), 1)
            g.memset(ones[:, :], 1.0).then_inc(sg("constants"), 1)
            pool.wait_ge(sg("constants"), 3)
            g.affine_select(out=before[:, :], in_=ones[:, :], compare_op=ALU.is_ge, fill=0.0, base=-1,
                            pattern=[[1, P]], channel_multiplier=-1).then_inc(sg("constants"), 1)
            pool.wait_ge(sg("slots"), 1)
            for g_ in range(NG):
                pool.wait_ge(sg(f"x_in{g_}"), 16)
            for tb in range(NTB):
                for k in range(2):
                    g.indirect_dma_start(out=xs[:, :], out_offset=bass.IndirectOffsetOnAxis(slot[:, k, tb:tb + 1], 0),
                                         in_=acc[:, tb, :], in_offset=None).then_inc(sg("scattered"), 16)
            pool.wait_ge(sg("y_out0"), 16 * ((TILES + 1) // 2))
            pool.wait_ge(sg("y_out1"), 16 * (TILES // 2))
            for tb in range(NTB):
                if tb >= GR:
                    pool.wait_ge(sg("combined"), tb - GR + 1)
                for k in range(2):
                    g.indirect_dma_start(out=pair[:, tb % GR, k, :], out_offset=None, in_=ys[:, :],
                                         in_offset=bass.IndirectOffsetOnAxis(slot[:, k, tb:tb + 1], 0))\
                        .then_inc(sg(f"pair_in{tb % GR}"), 16)

        @block.tensor
        def _(pe):
            mm, tr = nc.tensor.matmul, nc.tensor.transpose

            def group_t(g):
                pe.wait_ge(sg(f"x_in{g}"), 16)
                if g >= 2:
                    for c in range(DC):
                        pe.wait_ge(sg(f"xT{c}"), g - 1)
                for c in range(DC):
                    for k in range(GRP):
                        last = tr(ps[g % 2 * 2 + c][:, k * P:(k + 1) * P], acc[:, g * GRP + k, c * P:(c + 1) * P],
                                  ident[:, :])
                    last.then_inc(sg("xT_full"), 1)

            def scores(g):
                for c in range(DC):
                    pe.wait_ge(sg(f"xT{c}"), g + 1)
                for k in range(GRP):
                    tb = g * GRP + k
                    for c in range(DC):
                        last = mm(ps[4][:, tb * E:(tb + 1) * E], xTr[:, g % 2, c, k * P:(k + 1) * P], wg[:, c, :],
                                  start=c == 0, stop=c == DC - 1)
                last.then_inc(sg("scores_full"), 1)

            group_t(0)
            pe.wait_ge(sg("small"), 48)
            tr(ps[6][:, 0:E * FT], b1r[:, :], ident[0:E * FT, 0:E * FT]).then_inc(sg("b1_full"), 1)
            for g in range(NG):
                if g + 1 < NG:
                    group_t(g + 1)
                scores(g)
            pe.wait_ge(sg("constants"), 4)
            pe.wait_ge(sg("both"), 1)
            flat = both[:, :, :].rearrange("p t e -> p (t e)")
            mm(ps[5][:, 0:NTB * E], before[:, :], flat, start=True, stop=True)
            mm(ps[5][:, NTB * E:2 * NTB * E], ones[:, :], flat, start=True, stop=True).then_inc(sg("counts_full"), 1)

            def rows_t(i):
                pe.wait_ge(sg(f"xt_in{i % XR}"), 16 * (i // XR + 1))
                if i >= 2:
                    pe.wait_ge(sg("xtT"), i - 1)
                for c in range(DC):
                    last = tr(ps[6 + i % 2][:, c * P:(c + 1) * P], xt[:, i % XR, c * P:(c + 1) * P], ident[:, :])
                last.then_inc(sg("xt_full"), 1)

            pe.wait_ge(sg("b1"), 1)
            rows_t(0)
            pe.wait_ge(sg("te"), 1)
            pe.wait_ge(sg("w_in"), 16 * (2 * E + 1))
            expert = None
            for i in range(TILES + 1):
                last_expert = expert
                if i < TILES:
                    expert = pe.value_load(te[0:1, i:i + 1], min_val=0, max_val=E - 1)
                    pe.wait_ge(sg("xtT"), i + 1)
                    if i:
                        pe.wait_ge(sg("raw"), 2 * i)
                    for h in range(2):
                        for c in range(DC):
                            last = mm(ps[h][:, :], xtT[:, i % 2, c, :],
                                      w1[:, bass.ds(expert, 1), c, h * HALF:(h + 1) * HALF],
                                      start=c == 0, stop=c == DC - 1)
                        last.then_inc(sg("up_full"), 1)
                if i + 1 < TILES:
                    rows_t(i + 1)
                if i:
                    pe.wait_ge(sg("hT"), FT * i)
                    if i >= 3:
                        pe.wait_ge(sg("y"), i - 2)
                    for f in range(FT):
                        last = mm(ps[4 + (i - 1) % 2][:, 0:D], hT[:, (i - 1) % 2, f, :],
                                  w2[:, bass.ds(last_expert, 1), f, :], start=f == 0, stop=f == FT - 1)
                    last.then_inc(sg("down_full"), 1)
                if i < TILES:
                    for h in range(2):
                        pe.wait_ge(sg("raw"), 2 * i + h + 1)
                        for k in range(KH):
                            last = tr(ps[2 + h][:, k * P:(k + 1) * P], raw[:, h, k * P:(k + 1) * P], ident[:, :])
                        last.then_inc(sg("hT_full"), 1)

        @block.scalar
        def _(act):
            sc = nc.scalar
            for g in range(NG):
                if g >= 2:
                    act.wait_ge(sg("scores_full"), g - 1)
                act.wait_ge(sg("xT_full"), DC * g + 1)
                sc.copy(xTr[:, g % 2, 0, :], ps[g % 2 * 2][:, :]).then_inc(sg("xT0"), 1)
            act.wait_ge(sg("b1_full"), 1)
            sc.copy(b1c[:, :], ps[6][:, 0:E * FT]).then_inc(sg("b1"), 1)
            act.wait_ge(sg("shifted"), 1)
            sc.activation(pr[:, :, :], lo[:, :, :], ACT.Exp).then_inc(sg("exps"), 1)
            act.wait_ge(sg("two"), 1)
            sc.activation(dd[:, :], m2[:, :], ACT.Exp).then_inc(sg("exps"), 1)

            def rows_in(i):
                act.wait_ge(sg("xt_full"), i + 1)
                if i >= 2:
                    act.wait_ge(sg("up_full"), 2 * (i - 1))
                sc.copy(xtT[:, i % 2, :, :], ps[6 + i % 2][:, 0:D].rearrange("p (c t) -> p c t", c=DC))\
                    .then_inc(sg("xtT"), 1)

            rows_in(0)
            act.wait_ge(sg("te"), 1)
            act.wait_ge(sg("b1"), 1)
            for i in range(TILES):
                if i + 1 < TILES:
                    rows_in(i + 1)
                expert = act.value_load(te[0:1, i:i + 1], min_val=0, max_val=E - 1)
                if i >= 2:
                    act.wait_ge(sg("down_full"), i - 1)
                for f in range(FT):
                    if f % KH == 0:
                        act.wait_ge(sg("hT_full"), 2 * i + f // KH + 1)
                    sc.activation(hT[:, i % 2, f, :], ps[2 + f // KH][:, f % KH * P:(f % KH + 1) * P], ACT.Relu,
                                  bias=b1c[:, bass.ds(expert * FT + f, 1)]).then_inc(sg("hT"), 1)

        @block.vector
        def _(dve):
            v = nc.vector
            s = Counted(dve, sg("dve_steps"))
            shape = [P, NTB, E]

            def over(ap):
                return ap.unsqueeze(2).to_broadcast(shape)

            for g in range(NG):
                if g >= 2:
                    dve.wait_ge(sg("scores_full"), g - 1)
                dve.wait_ge(sg("xT_full"), DC * g + 2)
                v.tensor_copy(xTr[:, g % 2, 1, :], ps[g % 2 * 2 + 1][:, :]).then_inc(sg("xT1"), 1)
            dve.wait_ge(sg("small"), 48)
            dve.wait_ge(sg("constants"), 4)
            dve.wait_ge(sg("scores_full"), NG)
            s.step(v.tensor_tensor(lo[:, :, :], ps[4][:, 0:NTB * E].rearrange("p (t e) -> p t e", e=E),
                                   bg[:, :].unsqueeze(1).to_broadcast(shape), ALU.add))
            s.step(v.tensor_reduce(m1[:, :], lo[:, :, :], AX.X, ALU.max))
            v.tensor_tensor(lo[:, :, :], lo[:, :, :], over(m1[:, :]), ALU.subtract).then_inc(sg("shifted"), 1)
            dve.wait_ge(sg("exps"), 1)
            s.step(v.tensor_reduce(m1[:, :], pr[:, :, :], AX.X, ALU.add))
            s.step(v.reciprocal(m1[:, :], m1[:, :]))
            s.step(v.tensor_tensor(pr[:, :, :], pr[:, :, :], over(m1[:, :]), ALU.mult))
            for m, oh in ((m1, oh1), (m2, oh2)):
                s.step(v.tensor_reduce(m[:, :], pr[:, :, :], AX.X, ALU.max))
                s.step(v.tensor_tensor(eq[:, :, :], pr[:, :, :], over(m[:, :]), ALU.is_equal))
                s.step(v.tensor_tensor(eq[:, :, :], eq[:, :, :], rank[:, :].unsqueeze(1).to_broadcast(shape),
                                       ALU.mult))
                s.step(v.tensor_reduce(ix[:, :], eq[:, :, :], AX.X, ALU.min))
                s.step(v.tensor_tensor(oh[:, :, :], rank[:, :].unsqueeze(1).to_broadcast(shape), over(ix[:, :]),
                                       ALU.is_equal))
                s.step(v.scalar_tensor_tensor(pr[:, :, :].rearrange("p t e -> p (t e)"),
                                              oh[:, :, :].rearrange("p t e -> p (t e)"), -4.0,
                                              pr[:, :, :].rearrange("p t e -> p (t e)"), ALU.mult, ALU.add))
            v.tensor_tensor(both[:, :, :], oh1[:, :, :], oh2[:, :, :], ALU.add).then_inc(sg("both"), 1)
            v.tensor_tensor(m2[:, :], m2[:, :], m1[:, :], ALU.subtract).then_inc(sg("two"), 1)
            dve.wait_ge(sg("exps"), 2)
            s.step(v.tensor_scalar(m1[:, :], dd[:, :], 1.0, None, ALU.add))
            s.step(v.reciprocal(m1[:, :], m1[:, :]))
            s.mark(v.tensor_tensor(dd[:, :], dd[:, :], m1[:, :], ALU.mult))
            dve.wait_ge(sg("counts_full"), 1)
            inside = ps[5][:, 0:NTB * E].rearrange("p (t e) -> p t e", e=E)
            total = ps[5][:, NTB * E:2 * NTB * E].rearrange("p (t e) -> p t e", e=E)
            s.step(v.tensor_copy(sa[:, :, :], total))
            src, dst = sa, sc_
            for d in (1, 2, 4, 8):
                s.mark(v.tensor_copy(dst[:, 0:d, :], src[:, 0:d, :]))
                s.step(v.tensor_tensor(dst[:, d:, :], src[:, d:, :], src[:, 0:NTB - d, :], ALU.add))
                src, dst = dst, src
            s.step(v.tensor_scalar(cnti[:, :], src[:, NTB - 1, :], float(P - 1), None, ALU.add))
            s.step(v.tensor_scalar(cnti[:, :], cnti[:, :], P.bit_length() - 1, None, ALU.logical_shift_right))
            s.step(v.tensor_copy(cnt[:, :], cnti[:, :]))
            s.step(v.tensor_copy(cum[:, :], cnt[:, :]))
            a, b = cum, cum2
            for d in (1, 2, 4):
                s.mark(v.tensor_copy(b[:, 0:d], a[:, 0:d]))
                s.step(v.tensor_tensor(b[:, d:], a[:, d:], a[:, 0:E - d], ALU.add))
                a, b = b, a
            s.step(v.tensor_tensor(cnt[:, :], a[:, :], cnt[:, :], ALU.subtract))
            s.step(v.tensor_scalar(cnt[:, :], cnt[:, :], float(P), None, ALU.mult))
            s.step(v.tensor_tensor(src[:, :, :], src[:, :, :], total, ALU.subtract))
            s.step(v.tensor_tensor(src[:, :, :], src[:, :, :], inside, ALU.add))
            s.step(v.tensor_tensor(src[:, :, :], src[:, :, :], cnt[:, :].unsqueeze(1).to_broadcast(shape), ALU.add))
            for k, oh in enumerate((oh1, oh2)):
                s.step(v.tensor_tensor(oh[:, :, :], oh[:, :, :], src[:, :, :], ALU.mult))
                s.step(v.tensor_reduce(slotf[:, k, :], oh[:, :, :], AX.X, ALU.add))
            v.tensor_copy(slot[:, :, :], slotf[:, :, :]).then_inc(sg("slots"), 1)
            s.step(v.tensor_tensor(past[:, :, :], a[0:1, :].unsqueeze(1).to_broadcast([1, TILES, E]),
                                   tile_no[:, :, :], ALU.is_le))
            s.step(v.tensor_reduce(tef[:, :], past[:, :, :], AX.X, ALU.add))
            s.step(v.tensor_scalar(tef[:, :], tef[:, :], float(E - 1), None, ALU.min))
            v.tensor_copy(te[:, :], tef[:, :]).then_inc(sg("te"), 1)
            dve.wait_ge(sg("te"), 1)
            dve.wait_ge(sg("w_in"), 16 * (2 * E + 1))
            for i in range(TILES + 1):
                if i < TILES:
                    for h in range(2):
                        dve.wait_ge(sg("up_full"), 2 * i + h + 1)
                        if i:
                            dve.wait_ge(sg("hT_full"), 2 * (i - 1) + h + 1)
                        v.tensor_copy(raw[:, h, :], ps[h][:, :]).then_inc(sg("raw"), 1)
                if i:
                    j = i - 1
                    expert = dve.value_load(te[0:1, j:j + 1], min_val=0, max_val=E - 1)
                    dve.wait_ge(sg("down_full"), i)
                    if j >= 2:
                        dve.wait_ge(sg(f"y_out{j % 2}"), 16 * (j // 2))
                    v.tensor_tensor(y[:, j % 2, :], ps[4 + j % 2][:, 0:D], b2b[:, bass.ds(expert, 1), :]
                                    .rearrange("p o d -> p (o d)"), ALU.add).then_inc(sg("y"), 1)
            for tb in range(1, NTB, 2):
                two = (tb - 1, tb)
                for k, share in ((0, m1), (1, dd)):
                    for t in two:
                        if k == 0:
                            dve.wait_ge(sg(f"pair_in{t % GR}"), 32 * (t // GR + 1))
                        s.mark(v.scalar_tensor_tensor(acc[:, t, :], pair[:, t % GR, k, :], share[:, t:t + 1],
                                                      acc[:, t, :], ALU.mult, ALU.add))
                    s.sync()
                dve.sem_inc(sg("combined"), 2)
                for t in two:
                    s.mark(v.bn_stats(stats[:, t, :], acc[:, t, :]))
                if tb % GRP == GRP - 1:
                    g = slice(tb - GRP + 1, tb + 1)
                    s.sync()
                    for k in range(g.start, g.stop):
                        s.mark(v.bn_aggr(mv[:, k, :], stats[:, k, :]))
                    s.sync()
                    x_, y_, a_ = (r[:, :] for r in rs)
                    s.step(v.tensor_scalar(x_, mv[:, g, 1], LN_EPS, None, ALU.add))
                    rsqrt_steps(s, v, x_, y_, a_)
                    for k in range(g.start, g.stop):
                        v.tensor_scalar(acc[:, k, :], acc[:, k, :], mv[:, k, 0:1], rs[1][:, k % GRP:k % GRP + 1],
                                        ALU.subtract, ALU.mult).then_inc(sg("normed"), 1)
                    dve.wait_ge(sg("normed"), g.stop)


def two_layers(nc, io, out):
    h0 = nc.dram_tensor("h0", (T, B, D), fp32).ap()
    x3 = nc.dram_tensor("x3", (B, T, D), fp32).ap()
    TOP, E = 2, 8
    slots = ((TOP * B * T + E * (P - 1)) // P) * P
    xs = nc.dram_tensor("x_slots", (slots, D), fp32).ap()
    ys = nc.dram_tensor("y_slots", (slots, D), fp32).ap()
    with ExitStack() as whole:
        ident = whole.enter_context(nc.sbuf_tensor("ident", [P, P], fp32))
        with ExitStack() as layers:
            weights = Weights(nc, layers, whole, io)
            with ExitStack() as ctx:
                s4_tokens(nc, ctx, whole, io["x"], io["L0_tok_log_dt"], io["L0_tok_inv_A_real"],
                          io["L0_tok_A_imag"], io["L0_tok_B_ri"], h0, ident, xs, weights)
            with ExitStack() as ctx:
                main_loop(nc, ctx, whole, io, h0, x3, ident, weights)
        with ExitStack() as ctx:
            expert_mixture(nc, ctx, io, x3, xs, ys, out, ident)


_UNUSED = ("L0_ffn_gate_w",)


def kernel(**inputs):
    import concourse.bacc as bacc
    from concourse.bass_utils import run_bass_kernel_spmd

    nc = bacc.Bacc("TRN2", target_bir_lowering=False, num_devices=1)
    arrays, io = {}, {}
    for name, value in inputs.items():
        if name in _UNUSED:
            continue
        a = np.ascontiguousarray(value)
        if name == "L0_tok_log_dt":
            a = np.ascontiguousarray(a.reshape(T // P, P).T)
        arrays[f"in_{name}"] = a
        io[name] = nc.dram_tensor(f"in_{name}", a.shape, mybir.dt.from_np(a.dtype), kind="ExternalInput").ap()
    out = nc.dram_tensor("out_h", (B, T, D), fp32, kind="ExternalOutput").ap()
    two_layers(nc, io, out)
    return run_bass_kernel_spmd(nc, [arrays], core_ids=[0]).results[0]["out_h"]
```
